# Optimizing a Trainium2 kernel written in Bass

```python
import numpy as np
import jax
import jax.numpy as jnp

def _softmax(x, axis=-1):
    return jax.nn.softmax(x, axis=axis)

def _gelu(x):
    return jax.nn.gelu(x, approximate=True)

def _silu(x):
    return jax.nn.silu(x)

def _sigmoid(x):
    return jax.nn.sigmoid(x)

def _layernorm(x, axis=-1, eps=1e-05):
    m = jnp.mean(x, axis=axis, keepdims=True)
    v = jnp.var(x, axis=axis, keepdims=True)
    return (x - m) / jnp.sqrt(v + eps)

def _scatter_add(tgt, idx, src, axis=0):
    return tgt.at[idx].add(src)

def _segment_sum(src, seg, n):
    return jax.ops.segment_sum(src, seg, n)
kernel_name = 'mk_xattn_ffn_d2_seqx_r8_496b78'

def setup_inputs(seed: int=0):
    np.random.seed(seed)
    _w = jnp.asarray

    def _rec_inputs():
        import jax
        import jax.numpy as jnp
        _rk = jax.random.key(seed)
        x = -0.0002928 + 1 * jax.random.normal(jax.random.fold_in(_rk, 1), (64, 64, 256), jnp.float32)
        _lenS = 64 - jax.random.randint(jax.random.fold_in(_rk, 7), (64,), 0, max(1, 64 // 4) + 1, jnp.int32)
        _lenS2 = 64 - jax.random.randint(jax.random.fold_in(_rk, 8), (64,), 0, max(1, 64 // 4) + 1, jnp.int32)
        _ctx_2048P = jax.random.normal(jax.random.fold_in(_rk, 11), (64, 16, 256), jnp.float32)
        _ctx_2048c = jax.random.dirichlet(jax.random.fold_in(_rk, 511), 0.3 * jnp.ones((16,), jnp.float32), (64, 64))
        _ctx_2048t = jnp.einsum('bsk,bkd->bsd', _ctx_2048c, _ctx_2048P)
        _ctx_2048t = _ctx_2048t * jax.lax.rsqrt(jnp.mean(jnp.square(_ctx_2048t)) + 1e-12) * 0.953939
        ctx_2048 = -1.39393e-06 + 0.999914 * (_ctx_2048t + 0.3 * jax.random.normal(jax.random.fold_in(_rk, 611), (64, 64, 256), jnp.float32))
        _validS = jnp.arange(64)[None, :] < _lenS[:, None]
        _validS2 = jnp.arange(64)[None, :] < _lenS2[:, None]
        _causal = jnp.tril(jnp.ones((64, 64), dtype=bool))
        mask_BxS2_ik0 = jnp.where(jnp.broadcast_to(_validS2[:, :], (64, 64)), 0, 1).astype(jnp.int32)
        return (x, ctx_2048, mask_BxS2_ik0)
    x, ctx_2048, mask_BxS2_ik0 = _rec_inputs()

    def _L0_xattn_setup():
        import jax, jax.numpy as jnp
        import numpy as np
        DIM = 64
        CTX_DIM = 64
        NUM_HEADS = 8
        DIM_HEAD = 64
        INNER = NUM_HEADS * DIM_HEAD
        B, N, CTX_LEN = (4, 256, 256)
        key = jax.random.key(seed)
        ks = jax.random.split(key, 6)
        x = jax.random.normal(ks[0], (B, DIM, N), dtype=jnp.float32)
        context = jax.random.normal(ks[1], (B, CTX_DIM, CTX_LEN), dtype=jnp.float32)
        W_q = jax.random.normal(ks[2], (DIM, INNER), dtype=jnp.float32) / np.sqrt(DIM)
        W_kv = jax.random.normal(ks[3], (CTX_DIM, 2 * INNER), dtype=jnp.float32) / np.sqrt(CTX_DIM)
        W_out = jax.random.normal(ks[4], (INNER, DIM), dtype=jnp.float32) / np.sqrt(INNER)
        b_out = jax.random.normal(ks[5], (DIM,), dtype=jnp.float32) * 0.01
        return {'x': x, 'context': context, 'W_q': W_q, 'W_kv': W_kv, 'W_out': W_out, 'b_out': b_out}
    _L0_xattn_all = _L0_xattn_setup()
    _L0_xattn_in = {k: v for k, v in _L0_xattn_all.items() if k in ('W_q', 'W_kv', 'W_out', 'b_out')}
    del _L0_xattn_all

    def _L0_ffn_setup():
        import jax, jax.numpy as jnp
        import numpy as np
        H = 256
        E = 16
        I = 64
        IS = 256
        TOP_K = 2
        B, S = (1, 256)
        key = jax.random.key(seed)
        ks = jax.random.split(key, 9)
        std = 0.02
        return {'hidden_states': jax.random.normal(ks[0], (B, S, H), dtype=jnp.float32), 'gate_w': jax.random.normal(ks[1], (E, H), dtype=jnp.float32) * std, 'w1': jax.random.normal(ks[2], (E, I, H), dtype=jnp.float32) * std, 'w2': jax.random.normal(ks[3], (E, H, I), dtype=jnp.float32) * std, 'w3': jax.random.normal(ks[4], (E, I, H), dtype=jnp.float32) * std, 'ws_gate': jax.random.normal(ks[5], (IS, H), dtype=jnp.float32) * std, 'ws_up': jax.random.normal(ks[6], (IS, H), dtype=jnp.float32) * std, 'ws_down': jax.random.normal(ks[7], (H, IS), dtype=jnp.float32) * std, 'shared_gate_w': jax.random.normal(ks[8], (1, H), dtype=jnp.float32) * std}
    _L0_ffn_all = _L0_ffn_setup()
    _L0_ffn_in = {k: v for k, v in _L0_ffn_all.items() if k in ('gate_w', 'w1', 'w2', 'w3', 'ws_gate', 'ws_up', 'ws_down', 'shared_gate_w')}
    del _L0_ffn_all

    def _L1_xattn_setup():
        import jax, jax.numpy as jnp
        import numpy as np
        import math
        H = 256
        NH = 16
        HD = H // NH
        EPS_LN = 1e-05
        RES_SCALE_MAX = 0.3

        def _nan_clean(x, lim=10000.0):
            return jnp.nan_to_num(x, nan=0.0, posinf=lim, neginf=-lim)
        key = jax.random.key(seed)
        ks = jax.random.split(key, 12)
        B, S, T = (4, 256, 32)
        std = 1.0 / math.sqrt(H)
        return {'hidden_states': jax.random.normal(ks[0], (B, S, H), jnp.float32), 'audio_tokens': jax.random.normal(ks[1], (B, T, H), jnp.float32), 'attention_mask': jax.random.randint(ks[2], (B, T), 0, 2, jnp.int32), 'Wq': jax.random.normal(ks[3], (H, H), jnp.float32) * std, 'bq': jnp.zeros((H,), jnp.float32), 'Wk': jax.random.normal(ks[4], (H, H), jnp.float32) * std, 'bk': jnp.zeros((H,), jnp.float32), 'Wv': jax.random.normal(ks[5], (H, H), jnp.float32) * std, 'bv': jnp.zeros((H,), jnp.float32), 'Wo': jax.random.normal(ks[6], (H, H), jnp.float32) * std, 'bo': jnp.zeros((H,), jnp.float32), 'ln_gamma': jnp.ones((H,), jnp.float32), 'ln_beta': jnp.zeros((H,), jnp.float32), 'residual_scale': jnp.float32(0.05)}
    _L1_xattn_all = _L1_xattn_setup()
    _L1_xattn_in = {k: v for k, v in _L1_xattn_all.items() if k in ('Wq', 'bq', 'Wk', 'bk', 'Wv', 'bv', 'Wo', 'bo', 'ln_gamma', 'ln_beta', 'residual_scale')}
    del _L1_xattn_all

    def _L1_ffn_setup():
        import jax, jax.numpy as jnp
        import numpy as np
        SWIGLU_ALPHA = 1.702
        SWIGLU_LIMIT = 7.0
        B, S, H, E, K, I = (2, 256, 256, 32, 4, 128)
        key = jax.random.key(seed)
        ks = jax.random.split(key, 8)
        return {'hidden_states': jax.random.normal(ks[0], (B, S, H), jnp.float32), 'gate_w': jax.random.normal(ks[1], (E, H), jnp.float32) * 0.02, 'gate_b': jnp.zeros((E,), jnp.float32), 'w_gate': jax.random.normal(ks[2], (E, H, I), jnp.float32) * 0.02, 'b_gate': jnp.zeros((E, I), jnp.float32), 'w_up': jax.random.normal(ks[3], (E, H, I), jnp.float32) * 0.02, 'b_up': jnp.zeros((E, I), jnp.float32), 'w_down': jax.random.normal(ks[4], (E, I, H), jnp.float32) * 0.02, 'b_down': jnp.zeros((E, H), jnp.float32)}
    _L1_ffn_all = _L1_ffn_setup()
    _L1_ffn_in = {k: v for k, v in _L1_ffn_all.items() if k in ('gate_w', 'gate_b', 'w_gate', 'b_gate', 'w_up', 'b_up', 'w_down', 'b_down')}
    del _L1_ffn_all
    return {'x': x, 'ctx_2048': ctx_2048, 'mask_BxS2_ik0': mask_BxS2_ik0, 'L0_xattn_W_q': _L0_xattn_in['W_q'], 'L0_xattn_W_kv': _L0_xattn_in['W_kv'], 'L0_xattn_W_out': _L0_xattn_in['W_out'], 'L0_xattn_b_out': _L0_xattn_in['b_out'], 'L0_ffn_gate_w': _L0_ffn_in['gate_w'], 'L0_ffn_w1': _L0_ffn_in['w1'], 'L0_ffn_w2': _L0_ffn_in['w2'], 'L0_ffn_w3': _L0_ffn_in['w3'], 'L0_ffn_ws_gate': _L0_ffn_in['ws_gate'], 'L0_ffn_ws_up': _L0_ffn_in['ws_up'], 'L0_ffn_ws_down': _L0_ffn_in['ws_down'], 'L0_ffn_shared_gate_w': _L0_ffn_in['shared_gate_w'], 'L1_xattn_Wq': _L1_xattn_in['Wq'], 'L1_xattn_bq': _L1_xattn_in['bq'], 'L1_xattn_Wk': _L1_xattn_in['Wk'], 'L1_xattn_bk': _L1_xattn_in['bk'], 'L1_xattn_Wv': _L1_xattn_in['Wv'], 'L1_xattn_bv': _L1_xattn_in['bv'], 'L1_xattn_Wo': _L1_xattn_in['Wo'], 'L1_xattn_bo': _L1_xattn_in['bo'], 'L1_xattn_ln_gamma': _L1_xattn_in['ln_gamma'], 'L1_xattn_ln_beta': _L1_xattn_in['ln_beta'], 'L1_xattn_residual_scale': _L1_xattn_in['residual_scale'], 'L1_ffn_gate_w': _L1_ffn_in['gate_w'], 'L1_ffn_gate_b': _L1_ffn_in['gate_b'], 'L1_ffn_w_gate': _L1_ffn_in['w_gate'], 'L1_ffn_b_gate': _L1_ffn_in['b_gate'], 'L1_ffn_w_up': _L1_ffn_in['w_up'], 'L1_ffn_b_up': _L1_ffn_in['b_up'], 'L1_ffn_w_down': _L1_ffn_in['w_down'], 'L1_ffn_b_down': _L1_ffn_in['b_down']}

def reference(x, ctx_2048, mask_BxS2_ik0, L0_xattn_W_q, L0_xattn_W_kv, L0_xattn_W_out, L0_xattn_b_out, L0_ffn_gate_w, L0_ffn_w1, L0_ffn_w2, L0_ffn_w3, L0_ffn_ws_gate, L0_ffn_ws_up, L0_ffn_ws_down, L0_ffn_shared_gate_w, L1_xattn_Wq, L1_xattn_bq, L1_xattn_Wk, L1_xattn_bk, L1_xattn_Wv, L1_xattn_bv, L1_xattn_Wo, L1_xattn_bo, L1_xattn_ln_gamma, L1_xattn_ln_beta, L1_xattn_residual_scale, L1_ffn_gate_w, L1_ffn_gate_b, L1_ffn_w_gate, L1_ffn_b_gate, L1_ffn_w_up, L1_ffn_b_up, L1_ffn_w_down, L1_ffn_b_down):
    import jax
    import jax.numpy as jnp

    def _L0_xattn_ref(x, context, W_q, W_kv, W_out, b_out):
        import jax, jax.numpy as jnp
        import numpy as np
        DIM = 64
        CTX_DIM = 64
        NUM_HEADS = 8
        DIM_HEAD = 64
        INNER = NUM_HEADS * DIM_HEAD
        B, N, CTX_LEN = (4, 256, 256)
        scale = DIM_HEAD ** (-0.5)
        xs = jnp.swapaxes(x, 1, 2)
        cs = jnp.swapaxes(context, 1, 2)
        b, n, _ = xs.shape
        m = cs.shape[1]
        q = xs @ W_q
        kv = cs @ W_kv
        k, v = jnp.split(kv, 2, axis=-1)
        q = q.reshape(b, n, NUM_HEADS, DIM_HEAD).transpose(0, 2, 1, 3)
        k = k.reshape(b, m, NUM_HEADS, DIM_HEAD).transpose(0, 2, 1, 3)
        v = v.reshape(b, m, NUM_HEADS, DIM_HEAD).transpose(0, 2, 1, 3)
        attn = jnp.einsum('bhqd,bhkd->bhqk', q * scale, k)
        attn = jax.nn.softmax(attn, axis=-1)
        out = jnp.einsum('bhqk,bhkd->bhqd', attn, v)
        out = out.transpose(0, 2, 1, 3).reshape(b, n, INNER)
        out = out @ W_out + b_out
        return jnp.swapaxes(out, 1, 2)

    def _L0_ffn_ref(hidden_states, gate_w, w1, w2, w3, ws_gate, ws_up, ws_down, shared_gate_w):
        import jax, jax.numpy as jnp
        import numpy as np
        H = 256
        E = 16
        I = 64
        IS = 256
        TOP_K = 2
        B, S = (1, 256)
        b, s, h = hidden_states.shape
        x = hidden_states.reshape(-1, h)
        T = x.shape[0]
        router_logits = x @ gate_w.T
        routing = jax.nn.softmax(router_logits.astype(jnp.float32), axis=-1)
        topw, sel = jax.lax.top_k(routing, TOP_K)
        topw = topw / jnp.sum(topw, axis=-1, keepdims=True)
        topw = topw.astype(x.dtype)
        combine = jnp.zeros((T, E), dtype=x.dtype).at[jnp.arange(T)[:, None], sel].set(topw)
        hmid = jax.nn.silu(jnp.einsum('th,eih->tei', x, w1)) * jnp.einsum('th,eih->tei', x, w3)
        hmid = hmid * combine[:, :, None]
        moe_out = jnp.einsum('tei,ehi->th', hmid, w2)
        shared = jax.nn.silu(x @ ws_gate.T) * (x @ ws_up.T) @ ws_down.T
        shared = jax.nn.sigmoid(x @ shared_gate_w.T) * shared
        return (moe_out + shared).reshape(b, s, h)

    def _L1_xattn_ref(hidden_states, audio_tokens, attention_mask, Wq, bq, Wk, bk, Wv, bv, Wo, bo, ln_gamma, ln_beta, residual_scale):
        import jax, jax.numpy as jnp
        import numpy as np
        import math
        H = 256
        NH = 16
        HD = H // NH
        EPS_LN = 1e-05
        RES_SCALE_MAX = 0.3

        def _nan_clean(x, lim=10000.0):
            return jnp.nan_to_num(x, nan=0.0, posinf=lim, neginf=-lim)
        B, S, _ = hidden_states.shape
        T = audio_tokens.shape[1]
        hs = _nan_clean(hidden_states).astype(jnp.float32)
        at = _nan_clean(audio_tokens).astype(jnp.float32)

        def proj(x, W, b, L):
            y = x @ W.T + b
            return y.reshape(B, L, NH, HD).transpose(0, 2, 1, 3)
        q = _nan_clean(proj(hs, Wq, bq, S))
        k = _nan_clean(proj(at, Wk, bk, T))
        v = _nan_clean(proj(at, Wv, bv, T))
        scale = max(math.sqrt(HD), 1e-08)
        scores = jnp.einsum('bhsd,bhtd->bhst', q, k) / scale
        scores = jnp.clip(scores, -50.0, 50.0)
        scores = jnp.nan_to_num(scores, nan=0.0, posinf=50.0, neginf=-50.0)
        attend = (attention_mask.astype(jnp.float32) > 0.5)[:, None, None, :]
        scores = jnp.where(attend, scores, -10000.0)
        scores = jnp.clip(scores, -50.0, 50.0)
        probs = jax.nn.softmax(scores, axis=-1)
        probs = jnp.nan_to_num(probs, nan=0.0, posinf=1.0, neginf=0.0)
        probs = probs / (probs.sum(axis=-1, keepdims=True) + 1e-08)
        ctx = jnp.einsum('bhst,bhtd->bhsd', probs, v)
        ctx = ctx.transpose(0, 2, 1, 3).reshape(B, S, H)
        delta = _nan_clean(ctx @ Wo.T + bo)
        rs = jnp.clip(residual_scale, 0.0, RES_SCALE_MAX)
        delta = rs * delta
        mu = delta.mean(axis=-1, keepdims=True)
        var = jnp.mean((delta - mu) ** 2, axis=-1, keepdims=True)
        delta = (delta - mu) / jnp.sqrt(var + EPS_LN) * ln_gamma + ln_beta
        return delta

    def _L1_ffn_ref(hidden_states, gate_w, gate_b, w_gate, b_gate, w_up, b_up, w_down, b_down):
        import jax, jax.numpy as jnp
        import numpy as np
        SWIGLU_ALPHA = 1.702
        SWIGLU_LIMIT = 7.0
        B, S, H, E, K, I = (2, 256, 256, 32, 4, 128)
        Bb, Ss, Hh = hidden_states.shape
        x = hidden_states.reshape(-1, Hh)
        logits = x @ gate_w.T + gate_b
        topk_logits, topk_idx = jax.lax.top_k(logits, K)
        topk_weight = jax.nn.softmax(topk_logits.astype(jnp.float32), axis=-1)
        flat_idx = topk_idx.reshape(-1)
        xs = jnp.repeat(x, K, axis=0)
        order = jnp.argsort(flat_idx)
        xt = xs[order]
        gid = flat_idx[order]
        group_sizes = jnp.bincount(flat_idx, length=E).astype(jnp.int32)
        gate = jax.lax.ragged_dot(xt, w_gate, group_sizes) + b_gate[gid]
        up = jax.lax.ragged_dot(xt, w_up, group_sizes) + b_up[gid]
        gate = jnp.minimum(gate, SWIGLU_LIMIT)
        up = jnp.clip(up, -SWIGLU_LIMIT, SWIGLU_LIMIT)
        glu = gate * jax.nn.sigmoid(SWIGLU_ALPHA * gate)
        activated = (up + 1.0) * glu
        outs = jax.lax.ragged_dot(activated, w_down, group_sizes) + b_down[gid]
        inv = jnp.argsort(order)
        outs = outs[inv].reshape(-1, K, Hh)
        y = jnp.sum(outs * topk_weight[..., None], axis=1).astype(x.dtype)
        return y.reshape(Bb, Ss, Hh)
    x = x + _L0_xattn_ref(_layernorm(x, axis=-1), ctx_2048, L0_xattn_W_q, L0_xattn_W_kv, L0_xattn_W_out, L0_xattn_b_out)
    x = x + _L0_ffn_ref(_layernorm(x, axis=-1), L0_ffn_gate_w, L0_ffn_w1, L0_ffn_w2, L0_ffn_w3, L0_ffn_ws_gate, L0_ffn_ws_up, L0_ffn_ws_down, L0_ffn_shared_gate_w)
    x = x + _L1_xattn_ref(_layernorm(x, axis=-1), ctx_2048, mask_BxS2_ik0, L1_xattn_Wq, L1_xattn_bq, L1_xattn_Wk, L1_xattn_bk, L1_xattn_Wv, L1_xattn_bv, L1_xattn_Wo, L1_xattn_bo, L1_xattn_ln_gamma, L1_xattn_ln_beta, L1_xattn_residual_scale)
    x = x + _L1_ffn_ref(_layernorm(x, axis=-1), L1_ffn_gate_w, L1_ffn_gate_b, L1_ffn_w_gate, L1_ffn_b_gate, L1_ffn_w_up, L1_ffn_b_up, L1_ffn_w_down, L1_ffn_b_down)
    return x

_drawn_inputs = setup_inputs


def setup_inputs(seed=0):
    import zlib

    import numpy as np

    out = dict(_drawn_inputs(seed))
    spreads = {'L1_xattn_bq': (0.0, 0.972),
     'L1_xattn_bk': (0.0, 2.0),
     'L1_xattn_bv': (0.0, 0.28),
     'L1_xattn_bo': (0.0, 0.293),
     'L1_xattn_ln_gamma': (1.0, 0.2),
     'L1_xattn_ln_beta': (0.0, 0.39),
     'L1_ffn_gate_b': (0.0, 0.39),
     'L1_ffn_b_gate': (0.0, 0.8),
     'L1_ffn_b_up': (0.0, 0.8),
     'L1_ffn_b_down': (0.0, 0.8)}
    factors = {'L0_xattn_b_out': 42.758,
     'L0_ffn_gate_w': 8.0,
     'L0_ffn_w1': 8.0,
     'L0_ffn_w2': 8.0,
     'L0_ffn_w3': 8.0,
     'L0_ffn_ws_gate': 8.0,
     'L0_ffn_ws_up': 8.0,
     'L0_ffn_ws_down': 8.0,
     'L0_ffn_shared_gate_w': 8.0,
     'L1_ffn_w_gate': 4.036,
     'L1_ffn_w_up': 8.0,
     'L1_ffn_w_down': 3.766}
    for name, (base, spread) in spreads.items():
        noise = np.random.default_rng([zlib.crc32(name.encode()), seed]).standard_normal(out[name].shape)
        drawn = base * np.exp(spread * noise) if base else spread * noise
        out[name] = jnp.asarray(drawn.astype(out[name].dtype))
    for name, factor in factors.items():
        out[name] = (out[name] * factor).astype(out[name].dtype)
    return out
```

```python
import concourse.bass as bass
from concourse import mybir
from contextlib import ExitStack

F32 = mybir.dt.float32
BF16 = mybir.dt.bfloat16
I32 = mybir.dt.int32
ALU = mybir.AluOpType
ACT = mybir.ActivationFunctionType
AX = mybir.AxisListType

P = 128
B, S, H = 64, 64, 256
T = B * S
NT = T // P
KT = H // P
EPS = 1e-5

A_HEADS = 8
A_DH = 64
A_N = H

LEAD = 2


class Phase:

    def __init__(self, ctx, nc, name):
        self.ctx, self.nc, self.name = ctx, nc, name
        self.semaphores = []
        ctx.callback(self.clear)

    def clear(self):
        if self.semaphores:
            self.nc.clear_and_free_semaphores(self.semaphores)
            self.nc.all_engine_barrier()

    def sbuf(self, name, shape, dt=F32):
        return self.ctx.enter_context(self.nc.sbuf_tensor(f"{self.name}_{name}", shape, dt))

    def psum(self, name, shape, dt=F32):
        return self.ctx.enter_context(self.nc.psum_tensor(f"{self.name}_{name}", shape, dt))

    def sem(self, name):
        semaphore = self.nc.alloc_semaphore(f"{self.name}_{name}")
        self.semaphores.append(semaphore)
        return semaphore


def setup_attention_weights(nc, ins, sb, later=(), later_loaded=None):
    with ExitStack() as ctx:
        ph = Phase(ctx, nc, "fold")
        wq = ph.sbuf("wq_dup", [A_DH, A_HEADS, 2, S])
        wk = ph.sbuf("wk_h", [A_DH, A_HEADS, S])
        wv = ph.sbuf("wv_dup", [A_DH, A_HEADS, 2, S])
        wo = ph.sbuf("wo_h", [A_DH, A_HEADS, S])
        ps = ph.psum("ps_fold", [P, 2, A_HEADS * S])
        weights_in = ph.sem("weights_in")
        zeroed = ph.sem("zeroed")
        folded = ph.sem("products")
        copied = ph.sem("copied")
        block = ctx.enter_context(nc.Block())

        @block.sync
        def _(sp):
            for c in range(2):
                sp.dma_start(wq[:, :, c, :], ins["wq"]).then_inc(weights_in, 16)
                sp.dma_start(wv[:, :, c, :], ins["wv"]).then_inc(weights_in, 16)
                sp.dma_start(sb["b_out"][c * S:(c + 1) * S, :], ins["b_out"]).then_inc(weights_in, 16)
            sp.dma_start(wk[:, :, :], ins["wk"]).then_inc(weights_in, 16)
            sp.dma_start(wo[:, :, :], ins["wo"]).then_inc(weights_in, 16)
            for into, source in later:
                sp.dma_start(into, source).then_inc(later_loaded, 16)

        @block.gpsimd
        def _(pool):
            pool.memset(sb["minus_half"][:, :], -0.5)
            pool.memset(sb["onesf"][:, :], 1.0)
            pool.memset(sb["ident"][:, :], 0.0).then_inc(zeroed, 1)
            pool.wait_ge(zeroed, 1)
            pool.affine_select(out=sb["ident"][:, :], in_=sb["ident"][:, :], compare_op=ALU.not_equal, fill=1.0,
                               base=0, pattern=[[-1, P]], channel_multiplier=1).then_inc(zeroed, 1)

        @block.tensor
        def _(pe):
            pe.wait_ge(weights_in, 16 * 8)
            for h in range(A_HEADS):
                nc.tensor.matmul(ps[:, 0, h * S:(h + 1) * S], wq[:, h, :, :].rearrange("d c s -> d (c s)"),
                                 wk[:, h, :], start=True, stop=True)
            for h in range(A_HEADS):
                last = nc.tensor.matmul(ps[:, 1, h * S:(h + 1) * S], wv[:, h, :, :].rearrange("d c s -> d (c s)"),
                                        wo[:, h, :], start=True, stop=True)
            last.then_inc(folded, 1)

        @block.vector
        def _(dve):
            nc.vector.memset(sb["a_bd"][:, :, :], 0.0).then_inc(copied, 1)
            nc.vector.memset(sb["ctx_bd"][:, :, :], 0.0).then_inc(copied, 1)
            dve.wait_ge(folded, 1)
            dve.wait_ge(copied, 2)
            for c in range(2):
                half = slice(c * S, (c + 1) * S)
                nc.vector.tensor_scalar(sb["a_bd"][half, :, half], ps[half, 0, :].rearrange("p (h s) -> p h s", h=A_HEADS),
                                        float(A_DH) ** -0.5, None, ALU.mult).then_inc(copied, 1)
            nc.vector.tensor_copy(sb["bv"][:, :], ps[:, 1, :]).then_inc(copied, 1)
            dve.wait_ge(copied, 5)
            dve.wait_ge(weights_in, 16 * 8)


def attention0(nc, ins, sb):
    HD = A_HEADS
    STEPS = NT * HD
    BODY = 2 * HD
    with ExitStack() as ctx:
        ph = Phase(ctx, nc, "attn0")
        x_sb, a_bd, bv, ctx_bd, ident = sb["x"], sb["a_bd"], sb["bv"], sb["ctx_bd"], sb["ident"]
        xn = ph.sbuf("xn", [P, 2, A_N])
        stats = ph.sbuf("stats", [P, 6])
        mv = ph.sbuf("mean_var", [P, 2])
        vare = ph.sbuf("var_eps", [P, 1])
        rstd = ph.sbuf("rstd", [P, 1])
        q_sb = ph.sbuf("q_sb", [P, 2, A_N])
        prob = ph.sbuf("prob", [P, 2, 4, A_N])
        negmax = ph.sbuf("negmax", [P, 2, 4])
        sums = ph.sbuf("sums", [P, 2, 4])
        rsum = ph.sbuf("rsum", [P, 2, 4])
        prob_t = ph.sbuf("prob_t", [P, 2, 2, 2, A_N])
        v_sb = ph.sbuf("v_sb", [P, 2, 2, 2, A_HEADS * S])
        ps_s = ph.psum("ps_s", [P, 2, 4, A_N])
        ps_t = ph.psum("ps_t", [P, 2, 2, A_N])
        ps_qv = ph.psum("ps_qv", [P, 2, A_N])
        ps_o = ph.psum("ps_o", [P, 512])

        loaded = [ph.sem("pair_loaded0"), ph.sem("pair_loaded1")]
        ln_steps = ph.sem("ln_steps")
        rstd_ready = ph.sem("rstd_ready")
        xn_ready = ph.sem("xn_ready")
        q_made, q_ready = ph.sem("q_made"), ph.sem("q_ready")
        s_made, max_ready, exp_ready = ph.sem("s_made"), ph.sem("max_ready"), ph.sem("exp_ready")
        rsum_ready, prob_ready = ph.sem("rsum_ready"), ph.sem("prob_ready")
        t_made, t_ready = ph.sem("t_made"), ph.sem("t_ready")
        o_made = ph.sem("o_made")
        v_made, v_ready = ph.sem("v_made"), ph.sem("v_ready")
        x_ready = ph.sem("x_ready")
        opened = ph.sem("opened")
        passed = ph.sem("passed")
        block = ctx.enter_context(nc.Block())

        def step_done(eng, s, it, r):
            eng.wait_ge(s, it * BODY + (r + 1 + LEAD))

        def pair_done(eng, s, it, q):
            eng.wait_ge(s, it * 2 + (q + 1 + LEAD))

        def pair_loaded(eng, it, q):
            eng.wait_ge(loaded[q % 2], it * 48 + 48 * (q // 2 + 1))

        def exists(it, r):
            return not isinstance(it, int) or it * BODY + r < STEPS

        @block.sync
        def _(sp):
            sp.wait_ge(opened, 1)

            def load(it, q):
                tile = it * 2 + q
                for c in range(2):
                    sp.dma_start(ctx_bd[c * S:(c + 1) * S, q % 2, c * A_N:(c + 1) * A_N],
                                 ins["ctx"][bass.ds(tile * 2 + c, 1), :, :].rearrange("b s n -> (b s) n"))\
                      .then_inc(loaded[q % 2], 16)
                sp.dma_start(x_sb[:, bass.ds(tile, 1), :].rearrange("p a n -> p (a n)"),
                             ins["x"][bass.ds(tile * P, P), :]).then_inc(loaded[q % 2], 16)
            load(0, 0)
            load(0, 1)
            with sp.Fori(0, NT // 2 - 1) as it:
                for q in range(2):
                    step_done(sp, s_made, it, q * HD + HD - 1)
                    sp.sem_inc(passed, 1)
                    step_done(sp, v_made, it, q * HD + HD - 1)
                    sp.sem_inc(passed, 1)
                    pair_done(sp, xn_ready, it, q)
                    sp.sem_inc(passed, 1)
                    load(it, q + 2)

        @block.tensor
        def _(pe):
            pe.wait_ge(opened, 1)

            def queries(it, r):
                pair_done(pe, xn_ready, it, r // HD)
                step_done(pe, q_ready, it, r - 1)
                if exists(it, r + 3):
                    step_done(pe, v_ready, it, max(r + 3, HD - 2) if isinstance(it, int) and it == 0 else r + 3)
                nc.tensor.matmul(ps_qv[:, 0, :], a_bd[:, r % HD, :], xn[:, (r // HD) % 2, :],
                                 start=True, stop=True).then_inc(q_made, 1)

            def scores(it, r):
                pair_loaded(pe, it, r // HD)
                step_done(pe, q_ready, it, r)
                step_done(pe, exp_ready, it, r - 2)
                for qt in range(2):
                    last = nc.tensor.matmul(ps_s[:, r % 2, 2 * qt:2 * qt + 2, :].rearrange("p b k -> p (b k)"),
                                            q_sb[:, r % 2, qt * P:(qt + 1) * P], ctx_bd[:, (r // HD) % 2, :],
                                            start=True, stop=True)
                last.then_inc(s_made, 1)

            def transposes(it, r):
                step_done(pe, prob_ready, it, r)
                step_done(pe, t_ready, it, r - 1)
                for b in range(2):
                    for kt in range(2):
                        for qt in range(2):
                            last = nc.tensor.transpose(ps_t[:, b, kt, qt * P:(qt + 1) * P],
                                                       prob[:, r % 2, 2 * qt + b, kt * P:(kt + 1) * P], ident[:, :])
                last.then_inc(t_made, 1)

            def outputs(it, r):
                h, pair = r % HD, r // HD
                step_done(pe, t_ready, it, r)
                if h == 0:
                    step_done(pe, v_ready, it, pair * HD + HD - 1)
                    pair_done(pe, x_ready, it, pair - 1)
                for kt in range(2):
                    for b in range(2):
                        last = nc.tensor.matmul(ps_o[b * S:(b + 1) * S, 0:A_N],
                                                v_sb[:, pair % 2, b, kt, h * S:(h + 1) * S], prob_t[:, r % 2, b, kt, :],
                                                start=(h == 0 and kt == 0), stop=(h == HD - 1 and kt == 1))
                last.then_inc(o_made, 1)

            def values(it, r):
                pair_loaded(pe, it, r // HD)
                step_done(pe, v_ready, it, r - 1)
                if not (isinstance(it, int) and it * BODY + r < HD - 1):
                    step_done(pe, q_ready, it, r - 5)
                b, kt, ch = (r % HD) // 4, (r % HD) // 2 % 2, r % 2
                nc.tensor.matmul(ps_qv[:, 1, :], ctx_bd[:, (r // HD) % 2, b * A_N + kt * P:b * A_N + (kt + 1) * P],
                                 bv[:, ch * A_N:(ch + 1) * A_N], start=True, stop=True).then_inc(v_made, 1)

            def step(it, r):
                if exists(it, r + 7):
                    values(it, r + 7)
                if exists(it, r + 3):
                    queries(it, r + 3)
                if exists(it, r + 2):
                    scores(it, r + 2)
                transposes(it, r)
                if r > 0 or not isinstance(it, int) or it > 0:
                    outputs(it, r - 1)

            for r in range(HD - 1):
                values(0, r)
            queries(0, 0)
            queries(0, 1)
            scores(0, 0)
            queries(0, 2)
            scores(0, 1)
            step(0, 0)
            with pe.Fori(0, NT // 2 - 1) as it:
                for r in range(1, BODY + 1):
                    step(it, r)
            for r in range(1, BODY):
                step(NT // 2 - 1, r)
            outputs(NT // 2 - 1, BODY - 1)

        @block.scalar
        def _(act):
            act.wait_ge(opened, 1)

            def copy_values(it, r):
                b, kt, ch = (r % HD) // 4, (r % HD) // 2 % 2, r % 2
                step_done(act, v_made, it, r)
                if r % HD == 0:
                    step_done(act, o_made, it, (r // HD - 2) * HD + HD - 1) if not (isinstance(it, int) and it * BODY + r < BODY) else None
                nc.scalar.activation(v_sb[:, (r // HD) % 2, b, kt, ch * A_N:(ch + 1) * A_N], ps_qv[:, 1, :],
                                     ACT.Copy).then_inc(v_ready, 1)

            def copy_queries(it, r):
                step_done(act, q_made, it, r)
                step_done(act, s_made, it, r - 2)
                nc.scalar.activation(q_sb[:, r % 2, :], ps_qv[:, 0, :], ACT.Copy).then_inc(q_ready, 1)

            def exps(it, r):
                step_done(act, max_ready, it, r)
                step_done(act, t_made, it, r - 2)
                step_done(act, rsum_ready, it, r - 2)
                for c in range(4):
                    last = nc.scalar.activation(prob[:, r % 2, c, :], ps_s[:, r % 2, c, :], ACT.Exp,
                                                bias=negmax[:, r % 2, c:c + 1], accum_out=sums[:, r % 2, c:c + 1])
                last.then_inc(exp_ready, 1)

            def step(it, r):
                if exists(it, r + 3):
                    copy_queries(it, r + 3)
                if exists(it, r + 7):
                    copy_values(it, r + 7)
                if exists(it, r + 2):
                    exps(it, r + 2)

            for r in range(HD - 1):
                copy_values(0, r)
            copy_queries(0, 0)
            copy_queries(0, 1)
            exps(0, 0)
            copy_queries(0, 2)
            exps(0, 1)
            step(0, 0)
            with act.Fori(0, NT // 2 - 1) as it:
                for r in range(1, BODY + 1):
                    step(it, r)
            for r in range(1, BODY):
                step(NT // 2 - 1, r)

        @block.vector
        def _(dve):
            dve.wait_ge(opened, 1)

            def norm_statistics(it, q):
                tile = x_sb[:, bass.ds(it * 2 + q, 1), :].rearrange("p a n -> p (a n)")
                base = it * 6 + 3 * q
                pair_loaded(dve, it, q)
                nc.vector.bn_stats(stats[:, :], tile).then_inc(ln_steps, 1)
                dve.wait_ge(ln_steps, base + 1)
                dve.sem_inc(passed, 1)
                nc.vector.bn_aggr(mv[:, :], stats[:, :]).then_inc(ln_steps, 1)
                dve.wait_ge(ln_steps, base + 2)
                nc.vector.tensor_scalar(vare[:, :], mv[:, 1:2], EPS, None, ALU.add).then_inc(ln_steps, 1)

            def norm_apply(it, q):
                tile = x_sb[:, bass.ds(it * 2 + q, 1), :].rearrange("p a n -> p (a n)")
                pair_done(dve, rstd_ready, it, q)
                if not (isinstance(it, int) and it * 2 + q < 2):
                    step_done(dve, q_made, it, (q - 2) * HD + HD - 1)
                nc.vector.tensor_scalar(xn[:, q % 2, :], tile, mv[:, 0:1], rstd[:, 0:1],
                                        ALU.subtract, ALU.mult).then_inc(xn_ready, 1)

            def maxima(it, r):
                step_done(dve, s_made, it, r)
                step_done(dve, exp_ready, it, r - 2)
                nc.vector.tensor_reduce(negmax[:, r % 2, :], ps_s[:, r % 2, :, :], AX.X, ALU.max,
                                        negate=True).then_inc(max_ready, 1)

            def reciprocals(it, r):
                step_done(dve, exp_ready, it, r)
                step_done(dve, prob_ready, it, r - 2)
                nc.vector.reciprocal(rsum[:, r % 2, :], sums[:, r % 2, :]).then_inc(rsum_ready, 1)

            def copy_transposed(it, r):
                step_done(dve, t_made, it, r)
                step_done(dve, o_made, it, r - 2)
                nc.vector.tensor_copy(prob_t[:, r % 2, :, :, :], ps_t[:, :, :, :]).then_inc(t_ready, 1)

            def residual(it, q):
                tile = x_sb[:, bass.ds(it * 2 + q, 1), :].rearrange("p a n -> p (a n)")
                step_done(dve, o_made, it, q * HD + HD - 1)
                nc.vector.scalar_tensor_tensor(out=tile, in0=ps_o[:, 0:A_N], scalar=sb["b_out"][:, 0:1], in1=tile,
                                               op0=ALU.add, op1=ALU.add).then_inc(x_ready, 1)

            def step(it, r):
                if r % HD == 1 and not (isinstance(it, int) and it == 0 and r == 1):
                    residual(it, r // HD - 1)
                if exists(it, r + 2):
                    maxima(it, r + 2)
                if exists(it, r + 1):
                    reciprocals(it, r + 1)
                copy_transposed(it, r)
                if r % HD == 1 and exists(it, r + HD):
                    norm_statistics(it, r // HD + 1)
                if r % HD == 4 and exists(it, r + HD):
                    norm_apply(it, r // HD + 1)

            norm_statistics(0, 0)
            norm_apply(0, 0)
            maxima(0, 0)
            maxima(0, 1)
            reciprocals(0, 0)
            step(0, 0)
            step(0, 1)
            with dve.Fori(0, NT // 2 - 1) as it:
                for r in range(2, BODY + 2):
                    step(it, r)
            for r in range(2, BODY):
                step(NT // 2 - 1, r)
            residual(NT // 2 - 1, 1)
            pair_done(dve, x_ready, NT // 2 - 1, 1)

        @block.gpsimd
        def _(pool):
            for s in (rstd_ready, xn_ready, q_made, q_ready, s_made, max_ready, exp_ready, rsum_ready, prob_ready,
                      t_made, t_ready, o_made, v_made, v_ready, x_ready):
                pool.sem_inc(s, LEAD)
            pool.sem_inc(opened, 1)

            def normalise(it, r):
                step_done(pool, rsum_ready, it, r)
                nc.gpsimd.tensor_tensor(prob[:, r % 2, :, :], prob[:, r % 2, :, :],
                                        rsum[:, r % 2, :].unsqueeze(2).to_broadcast([P, 4, A_N]),
                                        ALU.mult).then_inc(prob_ready, 1)

            def inverse_deviation(it, q):
                pool.wait_ge(ln_steps, it * 6 + 3 * (q + 1))
                pair_done(pool, xn_ready, it, q - 1)
                nc.gpsimd.tensor_tensor(rstd[:, :], vare[:, :], sb["minus_half"][:, :], ALU.pow)\
                    .then_inc(rstd_ready, 1)

            def step(it, r):
                normalise(it, r)
                if r % HD == 3 and exists(it, r + HD):
                    inverse_deviation(it, r // HD + 1)
            inverse_deviation(0, 0)
            with pool.Fori(0, NT // 2 - 1) as it:
                for r in range(BODY):
                    step(it, r)
            for r in range(BODY):
                step(NT // 2 - 1, r)


GT = 4
NG = NT // GT
GN = GT * P


class Moe:

    def __init__(self, nc, name, experts, top, inner):
        self.name, self.E, self.K, self.I = name, experts, top, inner
        self.CAP = T + P
        self.NB = (T * top + experts * (P - 1)) // P + 1
        self.NB += -self.NB % 8
        self.spare = self.NB - T * top // P
        assert self.spare * P <= self.CAP
        rows = experts * self.CAP + self.spare * P
        self.rows_in = nc.dram_tensor(name + "_rows_in", (rows, H), F32, kind="Internal").ap()
        self.rows_out = nc.dram_tensor(name + "_rows_out", (self.NB * P, H), F32, kind="Internal").ap()

    def tables(self, ctx, nc):
        def sbt(name, shape, dt):
            return ctx.enter_context(nc.sbuf_tensor(self.name + name, shape, dt))
        E, K = self.E, self.K
        self.slots = sbt("_slots", [P, NT, K], F32)
        self.offset = sbt("_offset", [P, E], F32)
        self.weights = sbt("_weights", [P, NT, K], F32)
        self.chosen = sbt("_chosen", [P, NT, K], F32)
        self.iota = sbt("_iota", [P, GT * K, E], F32)
        self.region = sbt("_region", [P, GT, E], F32)
        self.total = sbt("_total", [P, E], BF16)
        self.block_expert = sbt("_block_expert", [1, self.NB], I32)
        self.block_row = sbt("_block_row", [1, self.NB], I32)
        self.pad_row = sbt("_pad_row", [1, E], I32)


def setup_constants(nc, ins, sb, moes):
    m0, m1 = moes
    TERMS = 3
    with ExitStack() as ctx:
        ph = Phase(ctx, nc, "const")
        made = ph.sem("constants_made")
        zero = ph.sem("zero_rows_written")
        bias_in = ph.sem("bias_loaded")
        zeroed = ph.sem("operands_zeroed")
        split, spread = ph.sem("split_steps"), ph.sem("terms_written")
        rest = ph.sbuf("bias_rest", [m1.E, 2, 2 * m1.I])
        term = ph.sbuf("bias_term", [m1.E, 3, 2 * m1.I], BF16)
        block = ctx.enter_context(nc.Block())

        @block.gpsimd
        def _(pool):
            nc.gpsimd.memset(sb["ones"][:, :], 1.0).then_inc(made, 1)
            nc.gpsimd.memset(sb["before"][:, :], 1.0).then_inc(made, 1)
            nc.gpsimd.memset(sb["upto"][:, :], 1.0).then_inc(made, 1)
            nc.gpsimd.memset(sb["zeros"][:, :], 0.0).then_inc(made, 1)
            nc.gpsimd.iota(sb["block_iota"][:, :], pattern=[[1, 256]], base=0, channel_multiplier=0,
                           allow_small_or_imprecise_dtypes=True).then_inc(made, 1)
            pool.wait_ge(made, 5)
            nc.gpsimd.affine_select(out=sb["before"][:, :], in_=sb["before"][:, :], compare_op=ALU.is_gt, fill=0.0,
                                    base=0, pattern=[[1, P]], channel_multiplier=-1).then_inc(made, 1)
            nc.gpsimd.affine_select(out=sb["upto"][:, :], in_=sb["upto"][:, :], compare_op=ALU.is_ge, fill=0.0,
                                    base=0, pattern=[[1, P]], channel_multiplier=-1).then_inc(made, 1)
            for m in moes:
                nc.gpsimd.iota(m.iota[:, :, :], pattern=[[0, GT * m.K], [1, m.E]], base=0, channel_multiplier=0,
                               allow_small_or_imprecise_dtypes=True).then_inc(made, 1)
                nc.gpsimd.iota(m.region[:, :, :], pattern=[[0, GT], [m.CAP, m.E]], base=0, channel_multiplier=0,
                               allow_small_or_imprecise_dtypes=True).then_inc(made, 1)
                nc.gpsimd.memset(m.total[:, :], 0.0).then_inc(made, 1)
            pool.wait_ge(made, 7 + 3 * len(moes))

        @block.vector
        def _(dve):
            nc.vector.memset(sb["bias1"][:, :, :], 0.0).then_inc(zeroed, 1)
            nc.vector.memset(sb["b_down"][:, :], 0.0).then_inc(zeroed, 1)
            nc.vector.memset(sb["term_ones"][:, :], 0.0).then_inc(zeroed, 1)
            nc.vector.memset(sb["w_down0"][m0.I:P, :, :], 0.0).then_inc(zeroed, 1)
            dve.wait_ge(zeroed, 4)
            nc.vector.memset(sb["term_ones"][0:TERMS, :], 1.0).then_inc(zeroed, 1)
            dve.wait_ge(zeroed, 5)
            dve.wait_ge(bias_in, 16)
            for n in range(TERMS):
                nc.vector.tensor_copy(term[:, n, :], rest[:, n % 2, :]).then_inc(split, 1)
                if n < TERMS - 1:
                    dve.wait_ge(split, 2 * n + 1)
                    nc.vector.tensor_tensor(rest[:, (n + 1) % 2, :], rest[:, n % 2, :], term[:, n, :],
                                            ALU.subtract).then_inc(split, 1)
                    dve.wait_ge(split, 2 * n + 2)

        @block.sync
        def _(sp):
            sp.dma_start(rest[:, 0, :], ins["bias_gu1"]).then_inc(bias_in, 16)
            sp.wait_ge(made, 5)
            for m in moes:
                for c in range(m.spare):
                    sp.dma_start(m.rows_in[m.E * m.CAP + c * P:m.E * m.CAP + (c + 1) * P, :], sb["zeros"][:, :])\
                      .then_inc(zero, 16)
            sp.wait_ge(split, 2 * TERMS - 1)
            sp.wait_ge(zeroed, 2)
            sp.dma_start(sb["b_down"][0:m1.E, :], ins["b_down1"]).then_inc(spread, 16)
            for n in range(TERMS):
                sp.dma_start(sb["bias1"][n:n + 1, :, :], term[:, n, :]).then_inc(spread, 16)
            sp.wait_ge(spread, 16 * (TERMS + 1))
            sp.wait_ge(zero, 16 * sum(m.spare for m in moes))


def block_tables(nc, sb, m):
    E, NB = m.E, m.NB
    with ExitStack() as ctx:
        ph = Phase(ctx, nc, f"{m.name}_tables")
        count = ph.sbuf("count", [E, 4])
        count_i = ph.sbuf("count_i", [E, 1], I32)
        blocks = ph.sbuf("blocks", [E, 1])
        blocks_wide = ph.sbuf("blocks_wide", [E, P], BF16)
        below = ph.sbuf("below", [E, NB])
        row = ph.sbuf("row", [1, 3, NB])
        esum = ph.sbuf("esum", [P, NT])
        wexp = ph.sbuf("wexp", [P, NT, m.K])
        ps = ph.psum("ps_tables", [P, 4, 512])
        pe_done = ph.sem("tables_products")
        dve_done = ph.sem("tables_steps")
        act_done = ph.sem("weights_exponentials")
        tables_ready = ph.sem("tables_ready")
        padded = ph.sem("padding_written")
        block = ctx.enter_context(nc.Block())

        @block.tensor
        def _(pe):
            nc.tensor.matmul(ps[0:E, 0, 0:1], m.total[:, :], sb["ones"][:, 0:1], start=True, stop=True)
            nc.tensor.matmul(ps[0:1, 1, 0:E], sb["ones"][:, 0:1], m.total[:, :], start=True, stop=True).then_inc(pe_done, 1)
            pe.wait_ge(dve_done, 5)
            nc.tensor.matmul(ps[0:E, 2, 0:1], sb["upto"][0:E, 0:E], blocks[:, :], start=True, stop=True)
            nc.tensor.matmul(ps[:, 2, 128:128 + E], blocks_wide[:, :], sb["before"][0:E, 0:E], start=True, stop=True)\
              .then_inc(pe_done, 1)
            pe.wait_ge(dve_done, 6)
            nc.tensor.matmul(ps[0:1, 3, 0:NB], sb["onesf"][0:E, 0:1], below[:, :], start=True, stop=True)
            nc.tensor.matmul(ps[0:1, 3, 256:256 + NB], blocks[:, :], below[:, :], start=True, stop=True).then_inc(pe_done, 1)

        @block.scalar
        def _(act):
            act.activation(wexp[:, :, :], m.weights[:, :, :], ACT.Exp).then_inc(act_done, 1)

        @block.vector
        def _(dve):
            dve.wait_ge(pe_done, 1)
            nc.vector.tensor_scalar(count[:, 0:1], ps[0:E, 0, 0:1], float(P - 1), None, ALU.add).then_inc(dve_done, 1)
            nc.vector.tensor_tensor(m.pad_row[:, :], ps[0:1, 1, 0:E], m.region[0:1, 0, :], ALU.add).then_inc(tables_ready, 1)
            dve.wait_ge(dve_done, 1)
            nc.vector.tensor_copy(count_i[:, :], count[:, 0:1]).then_inc(dve_done, 1)
            dve.wait_ge(dve_done, 2)
            nc.vector.tensor_single_scalar(count_i[:, :], count_i[:, :], 7, ALU.arith_shift_right).then_inc(dve_done, 1)
            dve.wait_ge(dve_done, 3)
            nc.vector.tensor_copy(blocks[:, :], count_i[:, :]).then_inc(dve_done, 1)
            nc.vector.tensor_copy(blocks_wide[:, :], count_i[:, 0:1].to_broadcast([E, P])).then_inc(dve_done, 1)
            dve.wait_ge(pe_done, 2)
            nc.vector.tensor_copy(count[:, 1:2], ps[0:E, 2, 0:1]).then_inc(tables_ready, 1)
            dve.wait_ge(tables_ready, 2)
            nc.vector.tensor_scalar(below[:, :], sb["block_iota"][0:E, 0:NB], count[:, 1:2], None, ALU.is_ge).then_inc(dve_done, 1)
            nc.vector.scalar_tensor_tensor(out=m.offset[:, :], in0=ps[:, 2, 128:128 + E], scalar=float(P),
                                           in1=m.region[:, 0, :], op0=ALU.mult, op1=ALU.subtract)
            dve.wait_ge(act_done, 1)
            nc.vector.tensor_reduce(esum[:, :], wexp[:, :, :], AX.X, ALU.add).then_inc(dve_done, 1)
            dve.wait_ge(dve_done, 7)
            nc.vector.reciprocal(esum[:, :], esum[:, :]).then_inc(dve_done, 1)
            dve.wait_ge(dve_done, 8)
            nc.vector.tensor_tensor(m.weights[:, :, :], wexp[:, :, :], esum[:, :].unsqueeze(2).to_broadcast([P, NT, m.K]),
                                    ALU.mult).then_inc(dve_done, 1)
            dve.wait_ge(pe_done, 3)
            nc.vector.tensor_scalar(m.block_expert[:, :], ps[0:1, 3, 0:NB], float(E - 1), None, ALU.min).then_inc(dve_done, 1)
            nc.vector.tensor_scalar(row[:, 0, :], ps[0:1, 3, 0:NB], float(m.CAP), None, ALU.mult).then_inc(dve_done, 1)
            nc.vector.tensor_tensor(row[:, 1, :], sb["block_iota"][0:1, 0:NB], ps[0:1, 3, 256:256 + NB], ALU.subtract).then_inc(dve_done, 1)
            dve.wait_ge(dve_done, 12)
            nc.vector.scalar_tensor_tensor(out=m.block_row[:, :], in0=row[:, 1, :], scalar=float(P), in1=row[:, 0, :],
                                           op0=ALU.mult, op1=ALU.add).then_inc(dve_done, 1)
            dve.wait_ge(dve_done, 13)

        @block.sync
        def _(sp):
            sp.wait_ge(tables_ready, 1)
            with sp.Fori(0, E) as e:
                at = sp.value_load(m.pad_row[0:1, bass.ds(e, 1)], min_val=0, max_val=(E - 1) * m.CAP + T)
                sp.dma_start(m.rows_in[bass.ds(at, P), :], sb["zeros"][:, :]).then_inc(padded, 16)
            sp.wait_ge(padded, 16 * E)


def experts(nc, sb, m, w_gu, w_down, bias, up_ones, activate):
    NB, I = m.NB, m.I
    BODY = 8
    OUTS = 4
    NI = NB // BODY
    with ExitStack() as ctx:
        ph = Phase(ctx, nc, f"{m.name}_experts")
        rows = ph.sbuf("rows", [P, BODY, H])
        rows_t = ph.sbuf("rows_t", [P, 2, KT, P])
        act_t = ph.sbuf("act_t", [P, 2, P])
        work = ph.sbuf("act_work", [P, 2, 4, I])
        outs = ph.sbuf("outs", [P, OUTS, H])
        ps_x = ph.psum("ps_x", [P, 2, 512])
        ps_gu = ph.psum("ps_gu", [P, 2, 512])
        ps_a = ph.psum("ps_a", [P, 512])
        ps_y = ph.psum("ps_y", [P, 2, 512])
        opened, passed = ph.sem("opened"), ph.sem("passed")
        rows_loaded = [ph.sem(f"rows_loaded{n}") for n in range(BODY)]
        rows_stored = [ph.sem(f"rows_stored{n}") for n in range(OUTS)]
        x_made, x_ready = ph.sem("x_made"), ph.sem("x_ready")
        gu_made, clipped, function_ready = ph.sem("gu_made"), ph.sem("clipped"), ph.sem("function_ready")
        steps = ph.sem("activation_steps")
        a_ready, at_made, at_ready = ph.sem("a_ready"), ph.sem("at_made"), ph.sem("at_ready")
        y_made, y_ready = ph.sem("y_made"), ph.sem("y_ready")
        act_sems = dict(gu_made=gu_made, clipped=clipped, function_ready=function_ready, steps=steps, a_ready=a_ready,
                        at_made=at_made)
        block = ctx.enter_context(nc.Block())

        LD = 4

        def done(eng, s, it, r):
            eng.wait_ge(s, it * BODY + (r + 1 + LD))

        def exists(it, r):
            return not isinstance(it, int) or it * BODY + r < NB

        def started(it, r):
            return not isinstance(it, int) or it * BODY + r >= 0

        @block.sync
        def _(sp):
            sp.wait_ge(opened, 1)
            top = m.E * m.CAP + (m.spare - 1) * P

            def load(it, r):
                at = sp.value_load(m.block_row[0:1, bass.ds(it * BODY + r, 1)], min_val=0, max_val=top)
                if not (isinstance(it, int) and it * BODY + r < BODY):
                    done(sp, x_made, it, r - BODY)
                    sp.sem_inc(passed, 1)
                sp.dma_start(rows[:, r % BODY, :], m.rows_in[bass.ds(at, P), :]).then_inc(rows_loaded[r % BODY], 16)

            for r in range(BODY):
                load(0, r)
            with sp.Fori(0, NI - 1) as it:
                for r in range(BODY):
                    load(it, r + BODY)

        @block.tensor
        def _(pe):
            pe.wait_ge(opened, 1)

            def step(it, r):
                if exists(it, r + 3):
                    q = r + 3
                    pe.wait_ge(rows_loaded[q % BODY], it * 16 + 16 * (q // BODY + 1))
                    done(pe, x_ready, it, q - 2)
                    for kt in range(KT):
                        last = nc.tensor.transpose(ps_x[:, q % 2, kt * P:(kt + 1) * P], rows[:, q % BODY, kt * P:(kt + 1) * P],
                                                   sb["ident"][:, :])
                    last.then_inc(x_made, 1)
                if exists(it, r + 2) and started(it, r + 2):
                    q = r + 2
                    e = pe.value_load(m.block_expert[0:1, bass.ds(it * BODY + q, 1)], min_val=0, max_val=m.E - 1)
                    done(pe, x_ready, it, q)
                    done(pe, a_ready, it, q - 2)
                    out = ps_gu[:, q % 2, 0:2 * I]
                    for kt in range(KT):
                        last = nc.tensor.matmul(out, rows_t[:, q % 2, kt, :],
                                                w_gu[:, bass.ds(e, 1), kt, :].rearrange("p a n -> p (a n)"),
                                                start=(kt == 0), stop=(kt == KT - 1 and bias is None))
                    if bias is not None:
                        last = nc.tensor.matmul(out, up_ones[:, :], bias[:, bass.ds(e, 1), :].rearrange("p a n -> p (a n)"),
                                                start=False, stop=True)
                    last.then_inc(gu_made, 1)
                if started(it, r) and exists(it, r):
                    done(pe, a_ready, it, r)
                    done(pe, at_ready, it, r - 1)
                    pe.sem_inc(passed, 1)
                    nc.tensor.transpose(ps_a[0:I, 0:P], work[:, r % 2, 3, :], sb["ident"][:, :]).then_inc(at_made, 1)
                if started(it, r - 1):
                    q = r - 1
                    e = pe.value_load(m.block_expert[0:1, bass.ds(it * BODY + q, 1)], min_val=0, max_val=m.E - 1)
                    done(pe, at_ready, it, q)
                    done(pe, y_ready, it, q - 2)
                    nc.tensor.matmul(ps_y[:, q % 2, 0:H], act_t[:, q % 2, :],
                                     w_down[:, bass.ds(e, 1), :].rearrange("p a n -> p (a n)"),
                                     start=True, stop=True).then_inc(y_made, 1)
            for r in range(-3, 1):
                step(0, r)
            with pe.Fori(0, NI - 1) as it:
                for r in range(1, BODY + 1):
                    step(it, r)
            for r in range(1, BODY + 1):
                step(NI - 1, r)

        @block.scalar
        def _(act):
            act.wait_ge(opened, 1)

            def step(it, r):
                if exists(it, r + 3):
                    q = r + 3
                    done(act, x_made, it, q)
                    done(act, gu_made, it, q - 2)
                    nc.scalar.activation(rows_t[:, q % 2, :, :], ps_x[:, q % 2, 0:H].rearrange("p (k t) -> p k t", k=KT),
                                         ACT.Copy).then_inc(x_ready, 1)
                if exists(it, r + 2) and started(it, r + 2):
                    q = r + 2
                    activate.function(nc, act, done, it, q, ps_gu, work, act_sems)
                if started(it, r) and exists(it, r):
                    done(act, at_made, it, r)
                    done(act, y_made, it, r - 2)
                    nc.scalar.activation(act_t[0:I, r % 2, :], ps_a[0:I, 0:P], ACT.Copy).then_inc(at_ready, 1)
            for r in range(-3, 1):
                step(0, r)
            with act.Fori(0, NI - 1) as it:
                for r in range(1, BODY + 1):
                    step(it, r)
            for r in range(1, BODY):
                step(NI - 1, r)

        @block.vector
        def _(dve):
            dve.wait_ge(opened, 1)

            def step(it, r):
                def copy_out():
                    if started(it, r - 1):
                        q = r - 1
                        done(dve, y_made, it, q)
                        if not (isinstance(it, int) and it * BODY + q < OUTS):
                            dve.wait_ge(rows_stored[q % OUTS], it * (16 * BODY // OUTS) + 16 * (q // OUTS))
                        nc.vector.tensor_copy(outs[:, q % OUTS, :], ps_y[:, q % 2, 0:H]).then_inc(y_ready, 1)
                if exists(it, r + 2) and started(it, r + 2):
                    activate.product(nc, dve, done, it, r + 2, ps_gu, work, act_sems, BODY, copy_out)
                else:
                    copy_out()
            if I < P:
                nc.vector.memset(act_t[I:P, :, :], 0.0).then_inc(steps, 1)
                dve.wait_ge(steps, 1)
                dve.sem_inc(at_ready, LD)
            else:
                dve.sem_inc(at_ready, LD)
            for r in range(-3, BODY + 1):
                step(0, r)
            with dve.Fori(1, NI - 1) as it:
                for r in range(1, BODY + 1):
                    step(it, r)
            for r in range(1, BODY + 1):
                step(NI - 1, r)

        @block.gpsimd
        def _(pool):
            for s in (x_made, x_ready, gu_made, clipped, function_ready, a_ready, at_made, y_made, y_ready):
                pool.sem_inc(s, LD)
            pool.sem_inc(opened, 1)

            def store(it, r):
                done(pool, y_ready, it, r)
                pool.sem_inc(passed, 1)
                pool.dma_start(m.rows_out[bass.ds((it * BODY + r) * P, P), :], outs[:, r % OUTS, :])\
                    .then_inc(rows_stored[r % OUTS], 16)
            with pool.Fori(0, NI) as it:
                for r in range(BODY):
                    store(it, r)
            for n in range(OUTS):
                pool.wait_ge(rows_stored[n], 16 * (NB // OUTS))


class Swish:
    STEPS = 0

    @staticmethod
    def function(nc, act, done, it, q, ps_gu, work, s):
        I = work.shape[3]
        done(act, s["gu_made"], it, q)
        done(act, s["a_ready"], it, q - 2)
        nc.scalar.activation(work[:, q % 2, 0, :], ps_gu[:, q % 2, 0:I], ACT.Silu).then_inc(s["function_ready"], 1)

    @staticmethod
    def product(nc, dve, done, it, q, ps_gu, work, s, body, between):
        I = work.shape[3]
        done(dve, s["function_ready"], it, q)
        done(dve, s["at_made"], it, q - 2)
        between()
        nc.vector.tensor_tensor(work[:, q % 2, 3, :], work[:, q % 2, 0, :], ps_gu[:, q % 2, I:2 * I], ALU.mult)\
            .then_inc(s["a_ready"], 1)


class ClippedSwish:
    ALPHA, LIMIT = 1.702, 7.0

    @staticmethod
    def function(nc, act, done, it, q, ps_gu, work, s):
        done(act, s["clipped"], it, q)
        nc.scalar.activation(work[:, q % 2, 0, :], work[:, q % 2, 1, :], ACT.Sigmoid, scale=ClippedSwish.ALPHA)\
            .then_inc(s["function_ready"], 1)

    @staticmethod
    def product(nc, dve, done, it, q, ps_gu, work, s, body, between):
        I = work.shape[3]
        L = ClippedSwish.LIMIT
        steps = s["steps"]
        done(dve, s["gu_made"], it, q)
        nc.vector.tensor_scalar(work[:, q % 2, 1, :], ps_gu[:, q % 2, 0:I], L, None, ALU.min).then_inc(s["clipped"], 1)
        nc.vector.tensor_scalar(work[:, q % 2, 2, :], ps_gu[:, q % 2, I:2 * I], L, -L, ALU.min, ALU.max).then_inc(steps, 1)
        between()
        dve.wait_ge(steps, it * 2 * body + (2 * q + 1))
        done(dve, s["clipped"], it, q)
        nc.vector.scalar_tensor_tensor(out=work[:, q % 2, 2, :], in0=work[:, q % 2, 2, :], scalar=1.0,
                                       in1=work[:, q % 2, 1, :], op0=ALU.add, op1=ALU.mult).then_inc(steps, 1)
        dve.wait_ge(steps, it * 2 * body + (2 * q + 2))
        done(dve, s["function_ready"], it, q)
        done(dve, s["at_made"], it, q - 2)
        nc.vector.tensor_tensor(work[:, q % 2, 3, :], work[:, q % 2, 0, :], work[:, q % 2, 2, :], ALU.mult)\
            .then_inc(s["a_ready"], 1)


class Routing:

    def __init__(self, ctx, nc, sb, m, wg, bias):
        ph = Phase(ctx, nc, f"{m.name}_routing")
        E, K = m.E, m.K
        self.nc, self.sb, self.m, self.wg, self.bias = nc, sb, m, wg, bias
        self.W = wg.shape[2]
        self.logits = ph.sbuf("logits", [P, GT, self.W])
        self.top = ph.sbuf("top", [P, GT, 8])
        self.index = ph.sbuf("index", [P, GT, 8], mybir.dt.uint32)
        self.chosen = ph.sbuf("group_chosen", [P, GT * K])
        self.onehot = ph.sbuf("onehot", [P, GT * K, E])
        self.mask = ph.sbuf("mask", [P, GT, E], BF16)
        self.added = ph.sbuf("added", [P, E])
        self.place = ph.sbuf("place", [P, GT, E])
        self.picked = ph.sbuf("picked", [P, GT * K, E])
        self.slots = ph.sbuf("group_slots", [P, 2, GT * K], I32)
        self.ps = ph.psum("ps_logits", [P, 512])
        self.slots_f = ph.sbuf("group_slots_f", [P, GT * K])
        self.logits_made = ph.sem("logits_made")
        self.logits_ready = ph.sem("logits_ready")
        self.mask_ready = ph.sem("mask_ready")
        self.ranks_made = ph.sem("ranks_made")
        self.place_ready = ph.sem("place_ready")
        self.slots_ready = ph.sem("slots_ready")
        self.steps = ph.sem("routing_steps")
        self.scattered = [ph.sem("scattered0"), ph.sem("scattered1")]
        self.rows_sent = ph.sem("rows_sent")

    STEPS = 9

    def step_done(self, dve, it, q, n):
        dve.wait_ge(self.steps, it * (2 * self.STEPS) + (self.STEPS * q + n))

    def make_logits(self, pe, it, q, xt, done):
        done(pe, self.place_ready, it, q - 1)
        for j in range(GT):
            for kt in range(KT):
                last = self.nc.tensor.matmul(self.ps[:, j * self.W:(j + 1) * self.W], xt[:, kt, j * P:(j + 1) * P],
                                             self.wg[:, kt, :], start=(kt == 0), stop=(kt == KT - 1))
        last.then_inc(self.logits_made, 1)

    def choose(self, dve, it, q, done):
        nc, m, K, E = self.nc, self.m, self.m.K, self.m.E
        done(dve, self.logits_made, it, q)
        ps = self.ps[:, 0:GT * self.W].rearrange("p (j e) -> p j e", j=GT)
        if self.bias is None:
            nc.vector.tensor_copy(self.logits[:, :, :], ps).then_inc(self.logits_ready, 1)
        else:
            nc.vector.tensor_tensor(self.logits[:, :, :], ps, self.bias[:, :].unsqueeze(1).to_broadcast([P, GT, E]),
                                    ALU.add).then_inc(self.logits_ready, 1)
        done(dve, self.logits_ready, it, q)
        dve.sem_inc(self.passed, 1)
        for j in range(GT):
            last = nc.vector.max(self.top[:, j, :], self.logits[:, j, 0:E])
        last.then_inc(self.steps, 1)
        self.step_done(dve, it, q, 1)
        dve.sem_inc(self.passed, 1)
        for j in range(GT):
            last = nc.vector.max_index(self.index[:, j, :], self.top[:, j, :], self.logits[:, j, 0:E])
        last.then_inc(self.steps, 1)
        nc.vector.tensor_tensor(m.weights[:, bass.ds((it * 2 + q) * GT, GT), :], self.top[:, :, 0:K],
                                self.top[:, :, 0:1].to_broadcast([P, GT, K]), ALU.subtract).then_inc(self.steps, 1)
        self.step_done(dve, it, q, 2)
        nc.vector.tensor_copy(self.chosen[:, :].rearrange("p (j k) -> p j k", j=GT), self.index[:, :, 0:K])\
            .then_inc(self.steps, 1)
        self.step_done(dve, it, q, 4)
        nc.vector.tensor_copy(m.chosen[:, bass.ds((it * 2 + q) * GT, GT), :],
                              self.chosen[:, :].rearrange("p (j k) -> p j k", j=GT)).then_inc(self.steps, 1)
        nc.vector.tensor_tensor(self.onehot[:, :, :], m.iota[:, :, :],
                                self.chosen[:, :].unsqueeze(2).to_broadcast([P, GT * K, E]), ALU.is_equal)\
            .then_inc(self.steps, 1)
        self.step_done(dve, it, q, 6)
        done(dve, self.ranks_made, it, q - 1)
        with nc.allow_low_precision("a mask of zeros and ones"):
            nc.vector.tensor_reduce(self.mask[:, :, :],
                                    self.onehot[:, :, :].rearrange("p (j k) e -> p j e k", j=GT), AX.X, ALU.add)\
                .then_inc(self.mask_ready, 1)

    def make_ranks(self, pe, it, q, done):
        nc, sb, m, E = self.nc, self.sb, self.m, self.m.E
        done(pe, self.mask_ready, it, q)
        for j in range(GT):
            out = self.ps[:, j * E:(j + 1) * E]
            nc.tensor.matmul(out, sb["before"][:, :], self.mask[:, j, :], start=True, stop=False)
            for i in range(j):
                nc.tensor.matmul(out, sb["ones"][:, :], self.mask[:, i, :], start=False, stop=False)
            last = nc.tensor.matmul(out, sb["ones"][:, :], m.total[:, :], start=False, stop=True)
        last.then_inc(self.ranks_made, 1)

    def place_rows(self, dve, it, q, done):
        nc, m, K, E = self.nc, self.m, self.m.K, self.m.E
        done(dve, self.ranks_made, it, q)
        nc.vector.tensor_tensor(self.place[:, :, :], self.ps[:, 0:GT * E].rearrange("p (j e) -> p j e", j=GT),
                                m.region[:, :, :], ALU.add).then_inc(self.place_ready, 1)
        nc.vector.tensor_reduce(self.added[:, :], self.mask[:, :, :].rearrange("p j e -> p e j"), AX.X, ALU.add)\
            .then_inc(self.steps, 1)
        self.step_done(dve, it, q, 7)
        with nc.allow_low_precision("counts up to 32"):
            nc.vector.tensor_tensor(m.total[:, :], m.total[:, :], self.added[:, :], ALU.add)
        done(dve, self.place_ready, it, q)
        nc.vector.tensor_tensor(self.picked[:, :, :].rearrange("p (j k) e -> p j k e", j=GT),
                                self.onehot[:, :, :].rearrange("p (j k) e -> p j k e", j=GT),
                                self.place[:, :, :].unsqueeze(2).to_broadcast([P, GT, K, E]), ALU.mult)\
            .then_inc(self.steps, 1)
        self.step_done(dve, it, q, 8)
        done(dve, self.rows_sent, it, q - 2)
        nc.vector.tensor_reduce(self.slots_f[:, :], self.picked[:, :, :], AX.X, ALU.add).then_inc(self.steps, 1)
        self.step_done(dve, it, q, 9)
        nc.vector.tensor_copy(self.slots[:, q % 2, :], self.slots_f[:, :]).then_inc(self.slots_ready, 1)
        nc.vector.tensor_copy(m.slots[:, bass.ds((it * 2 + q) * GT, GT), :],
                              self.slots_f[:, :].rearrange("p (j k) -> p j k", j=GT))

    def scatter(self, pool, it, q, xn, tiles, done):
        K = self.m.K
        done(pool, self.slots_ready, it, q)
        pool.sem_inc(self.passed, 1)
        for j in tiles:
            for k in range(K):
                n = j * K + k
                pool.indirect_dma_start(self.m.rows_in, bass.IndirectOffsetOnAxis(ap=self.slots[:, q % 2, n:n + 1], axis=0),
                                        xn[:, j, :], None).then_inc(self.scattered[q % 2], 16)

    def mark_sent(self, pool, it, q):
        n = 16 * GT * self.m.K
        pool.wait_ge(self.scattered[q % 2], it * n + n * (q // 2 + 1))
        pool.sem_inc(self.rows_sent, 1)

    def start(self, pool, lead):
        for s in (self.logits_made, self.logits_ready, self.mask_ready, self.ranks_made, self.place_ready,
                  self.slots_ready):
            pool.sem_inc(s, lead)
        pool.sem_inc(self.rows_sent, lead)


def shared_expert(nc, sb, m, w):
    with ExitStack() as ctx:
        ph = Phase(ctx, nc, "shared")
        x_sb = sb["x"]
        stats = ph.sbuf("stats", [P, GT, 6])
        mv = ph.sbuf("mean_var", [P, GT, 2])
        vare = ph.sbuf("var_eps", [P, GT])
        rstd = ph.sbuf("rstd", [P, GT])
        xn = ph.sbuf("xn", [P, 2, GT, H])
        xt = ph.sbuf("xt", [P, 2, KT, GN])
        silu = ph.sbuf("silu", [P, 2, GN])
        hidden = ph.sbuf("hidden", [P, 2, 2, GN])
        sg = ph.sbuf("sg", [P, GT])
        ps_x = ph.psum("ps_x", [P, KT, GN])
        ps_gu = ph.psum("ps_gu", [P, 2, 2, GN])
        ps_o = ph.psum("ps_o", [P, 2, H])
        rt = Routing(ctx, nc, sb, m, w["gate"], None)
        opened, passed = ph.sem("opened"), ph.sem("passed")
        rt.passed = passed
        norm_steps = ph.sem("norm_steps")
        rstd_ready, xn_ready = ph.sem("rstd_ready"), ph.sem("xn_ready")
        xt_made, xt_ready = ph.sem("xt_made"), ph.sem("xt_ready")
        gu_made = [ph.sem("gu_made0"), ph.sem("gu_made1")]
        silu_ready = [ph.sem("silu_ready0"), ph.sem("silu_ready1")]
        h_ready = [ph.sem("h_ready0"), ph.sem("h_ready1")]
        sg_ready = ph.sem("sg_ready")
        o_made = [ph.sem("o_made0"), ph.sem("o_made1")]
        x_ready = [ph.sem("x_ready0"), ph.sem("x_ready1")]
        block = ctx.enter_context(nc.Block())

        def done(eng, s, it, q):
            eng.wait_ge(s, it * 2 + (q + 1 + LEAD))

        def exists(it, q):
            return not isinstance(it, int) or it * 2 + q < NG

        @block.tensor
        def _(pe):
            pe.wait_ge(opened, 1)

            def transposes(it, q):
                done(pe, xn_ready, it, q)
                done(pe, xt_ready, it, q - 1)
                for j in range(GT):
                    for kt in range(KT):
                        last = nc.tensor.transpose(ps_x[:, kt, j * P:(j + 1) * P], xn[:, q % 2, j, kt * P:(kt + 1) * P],
                                                   sb["ident"][:, :])
                last.then_inc(xt_made, 1)

            def gate_up_half(it, q, f):
                done(pe, h_ready[f], it, q - 1)
                if f == 0:
                    done(pe, x_ready[1], it, q - 1)
                for u in range(2):
                    for kt in range(KT):
                        last = nc.tensor.matmul(ps_gu[:, f, u, :], w["shared_in"][:, u, kt, f * P:(f + 1) * P],
                                                xt[:, q % 2, kt, :], start=(kt == 0), stop=(kt == KT - 1))
                last.then_inc(gu_made[f], 1)

            def down(it, q, pair):
                if pair == 0:
                    for f in range(2):
                        done(pe, h_ready[f], it, q)
                    done(pe, x_ready[0], it, q - 1)
                out = ps_o if pair == 0 else ps_gu[:, 0, 0, :].rearrange("p (j n) -> p j n", j=2)
                for j in range(2):
                    for f in range(2):
                        t = 2 * pair + j
                        last = nc.tensor.matmul(out[:, j, :], hidden[:, q % 2, f, t * P:(t + 1) * P], w["shared_out"][:, f, :],
                                                start=(f == 0), stop=(f == 1))
                last.then_inc(o_made[pair], 1)

            def step(it, q):
                done(pe, xt_ready, it, q)
                rt.make_logits(pe, it, q, xt[:, q % 2, :, :], done)
                gate_up_half(it, q, 0)
                gate_up_half(it, q, 1)
                rt.make_ranks(pe, it, q, done)
                if exists(it, q + 1):
                    transposes(it, q + 1)
                down(it, q, 0)
                down(it, q, 1)
            transposes(0, 0)
            with pe.Fori(0, NG // 2 - 1) as it:
                for q in range(2):
                    step(it, q)
            for q in range(2):
                step(NG // 2 - 1, q)

        @block.scalar
        def _(act):
            act.wait_ge(opened, 1)

            def copy_xt(it, q):
                done(act, xt_made, it, q)
                done(act, gu_made[1], it, q - 2)
                for kt in range(KT):
                    last = nc.scalar.activation(xt[:, q % 2, kt, :], ps_x[:, kt, :], ACT.Copy)
                last.then_inc(xt_ready, 1)

            def step(it, q):
                done(act, rt.logits_ready, it, q)
                done(act, x_ready[1], it, q - 1)
                nc.scalar.activation(sg[:, :], rt.logits[:, :, m.E], ACT.Sigmoid).then_inc(sg_ready, 1)
                for f in range(2):
                    done(act, gu_made[f], it, q)
                    done(act, h_ready[f], it, q - 1)
                    nc.scalar.activation(silu[:, f, :], ps_gu[:, f, 0, :], ACT.Silu).then_inc(silu_ready[f], 1)
                if exists(it, q + 1):
                    copy_xt(it, q + 1)
            copy_xt(0, 0)
            with act.Fori(0, NG // 2 - 1) as it:
                for q in range(2):
                    step(it, q)
            for q in range(2):
                step(NG // 2 - 1, q)

        @block.vector
        def _(dve):
            dve.wait_ge(opened, 1)

            def apply(it, q):
                def free():
                    done(dve, xt_made, it, q - 2)
                    done(dve, rt.rows_sent, it, q - 2)
                norm_apply(nc, dve, x_sb, it, q, mv, rstd, xn[:, q % 2, :, :], rstd_ready, xn_ready, done, free)

            def step(it, q):
                if exists(it, q + 1):
                    norm_statistics(nc, dve, x_sb, it, q + 1, stats, mv, vare, norm_steps, passed)
                rt.choose(dve, it, q, done)
                if exists(it, q + 1):
                    apply(it, q + 1)
                for f in range(2):
                    done(dve, silu_ready[f], it, q)
                    if f == 0:
                        done(dve, o_made[1], it, q - 2)
                    nc.vector.tensor_tensor(hidden[:, q % 2, f, :], silu[:, f, :], ps_gu[:, f, 1, :], ALU.mult)\
                        .then_inc(h_ready[f], 1)
                rt.place_rows(dve, it, q, done)
                done(dve, sg_ready, it, q)
                for pair in range(2):
                    done(dve, o_made[pair], it, q)
                    out = ps_o if pair == 0 else ps_gu[:, 0, 0, :].rearrange("p (j n) -> p j n", j=2)
                    for j in range(2):
                        t = 2 * pair + j
                        tile = x_sb[:, bass.ds((it * 2 + q) * GT + t, 1), :].rearrange("p a n -> p (a n)")
                        last = nc.vector.scalar_tensor_tensor(out=tile, in0=out[:, j, :], scalar=sg[:, t:t + 1], in1=tile,
                                                              op0=ALU.mult, op1=ALU.add)
                    last.then_inc(x_ready[pair], 1)
            norm_statistics(nc, dve, x_sb, 0, 0, stats, mv, vare, norm_steps, passed)
            apply(0, 0)
            with dve.Fori(0, NG // 2 - 1) as it:
                for q in range(2):
                    step(it, q)
            for q in range(2):
                step(NG // 2 - 1, q)
            done(dve, x_ready[1], NG // 2 - 1, 1)

        @block.gpsimd
        def _(pool):
            for s in (rstd_ready, xn_ready, xt_made, xt_ready, *gu_made, *silu_ready, *h_ready, 
                      sg_ready, *o_made, *x_ready):
                pool.sem_inc(s, LEAD)
            rt.start(pool, LEAD)
            pool.sem_inc(opened, 1)

            def step(it, q):
                if exists(it, q + 1):
                    norm_deviation(nc, pool, sb, it, q + 1, vare, rstd, norm_steps, xn_ready, rstd_ready, done)
                if exists(it, q) and not (isinstance(it, int) and it * 2 + q == 0):
                    rt.mark_sent(pool, it, q - 1)
                rt.scatter(pool, it, q, xn[:, q % 2, :, :], range(GT), done)
            norm_deviation(nc, pool, sb, 0, 0, vare, rstd, norm_steps, xn_ready, rstd_ready, done)
            for q in range(2):
                step(0, q)
            with pool.Fori(1, NG // 2 - 1) as it:
                for q in range(2):
                    step(it, q)
            for q in range(2):
                step(NG // 2 - 1, q)
            rt.mark_sent(pool, NG // 2 - 1, 1)


def norm_statistics(nc, dve, x_sb, it, q, stats, mv, vare, norm_steps, passed):
    base = it * 6 + 3 * q
    for j in range(GT):
        last = nc.vector.bn_stats(stats[:, j, :], x_sb[:, bass.ds((it * 2 + q) * GT + j, 1), :].rearrange("p a n -> p (a n)"))
    last.then_inc(norm_steps, 1)
    dve.wait_ge(norm_steps, base + 1)
    dve.sem_inc(passed, 1)
    for j in range(GT):
        last = nc.vector.bn_aggr(mv[:, j, :], stats[:, j, :])
    last.then_inc(norm_steps, 1)
    dve.wait_ge(norm_steps, base + 2)
    nc.vector.tensor_scalar(vare[:, :], mv[:, :, 1], EPS, None, ALU.add).then_inc(norm_steps, 1)


def norm_deviation(nc, pool, sb, it, q, vare, rstd, norm_steps, xn_ready, rstd_ready, done):
    pool.wait_ge(norm_steps, it * 6 + 3 * (q + 1))
    done(pool, xn_ready, it, q - 1)
    nc.gpsimd.tensor_tensor(rstd[:, :], vare[:, :], sb["minus_half"][:, 0:1].to_broadcast([P, GT]), ALU.pow)\
        .then_inc(rstd_ready, 1)


def norm_apply(nc, dve, x_sb, it, q, mv, rstd, xn, rstd_ready, xn_ready, done, free):
    done(dve, rstd_ready, it, q)
    free()
    for j in range(GT):
        last = nc.vector.tensor_scalar(xn[:, j, :],
                                       x_sb[:, bass.ds((it * 2 + q) * GT + j, 1), :].rearrange("p a n -> p (a n)"),
                                       mv[:, j, 0:1], rstd[:, j:j + 1], ALU.subtract, ALU.mult)
    last.then_inc(xn_ready, 1)


class SlotFinder:

    def __init__(self, ph, nc, m):
        self.nc, self.m = nc, m
        self.onehot = ph.sbuf("onehot", [P, GT * m.K, m.E])
        self.picked = ph.sbuf("picked", [P, GT * m.K, m.E])
        self.shift = ph.sbuf("shift", [P, GT, m.K])
        self.steps = ph.sem("finder_steps")

    def rows(self, dve, it, q, slots, staged):
        nc, m = self.nc, self.m
        group = bass.ds((it * 2 + q) * GT, GT)
        base = it * 6 + 3 * q
        nc.vector.tensor_tensor(self.onehot[:, :, :].rearrange("p (j k) e -> p j k e", j=GT),
                                m.iota[:, :, :].rearrange("p (j k) e -> p j k e", j=GT),
                                m.chosen[:, group, :].unsqueeze(3).to_broadcast([P, GT, m.K, m.E]), ALU.is_equal)\
            .then_inc(self.steps, 1)
        dve.wait_ge(self.steps, base + 1)
        nc.vector.tensor_tensor(self.picked[:, :, :], self.onehot[:, :, :],
                                m.offset[:, :].unsqueeze(1).to_broadcast([P, GT * m.K, m.E]), ALU.mult)\
            .then_inc(self.steps, 1)
        dve.wait_ge(self.steps, base + 2)
        nc.vector.tensor_reduce(self.shift[:, :, :].rearrange("p j k -> p (j k)"), self.picked[:, :, :], AX.X, ALU.add)\
            .then_inc(self.steps, 1)
        dve.wait_ge(self.steps, base + 3)
        nc.vector.tensor_tensor(slots[:, q % 2, :].rearrange("p (j k) -> p j k", j=GT), self.shift[:, :, :],
                                m.slots[:, group, :], ALU.add).then_inc(staged, 1)


def combine0(nc, sb, m):
    K = m.K
    with ExitStack() as ctx:
        ph = Phase(ctx, nc, "combine0")
        slots = ph.sbuf("slots_now", [P, 2, GT * K], I32)
        weights = ph.sbuf("weights_now", [P, 2, GT * K])
        got = ph.sbuf("rows_got", [P, GT, K, H])
        acc = ph.sbuf("acc", [P, GT, 2, H])
        find = SlotFinder(ph, nc, m)
        opened, passed = ph.sem("opened"), ph.sem("passed")
        staged, steps, used = ph.sem("slots_staged"), ph.sem("sum_steps"), ph.sem("rows_used")
        gathered = [ph.sem(f"gathered{j}") for j in range(GT)]
        block = ctx.enter_context(nc.Block())

        @block.gpsimd
        def _(pool):
            with pool.Fori(0, NG // 2) as it:
                for q in range(2):
                    pool.wait_ge(staged, it * 2 + (q + 1))
                    for j in range(GT):
                        pool.wait_ge(used, it * (2 * GT) + (q * GT + j + 1))
                        pool.sem_inc(passed, 1)
                        for k in range(K):
                            n = j * K + k
                            pool.indirect_dma_start(got[:, j, k, :], None, m.rows_out,
                                                    bass.IndirectOffsetOnAxis(ap=slots[:, q, n:n + 1], axis=0))\
                                .then_inc(gathered[j], 16)

        @block.vector
        def _(dve):
            dve.sem_inc(used, GT)

            def stage(it, q):
                if not (isinstance(it, int) and it * 2 + q == 0):
                    dve.wait_ge(used, it * (2 * GT) + q * GT)
                nc.vector.tensor_copy(weights[:, q % 2, :].rearrange("p (j k) -> p j k", j=GT),
                                      m.weights[:, bass.ds((it * 2 + q) * GT, GT), :])
                find.rows(dve, it, q, slots, staged)

            def tile(it, q, j):
                x = sb["x"][:, bass.ds((it * 2 + q) * GT + j, 1), :].rearrange("p a n -> p (a n)")
                if j == 0:
                    dve.wait_ge(staged, it * 2 + (q + 1))
                dve.wait_ge(gathered[j], it * (32 * K) + 16 * K * (q + 1))
                dve.wait_ge(used, it * (2 * GT) + (q * GT + j + 1))
                base = it * (2 * GT * (K - 1)) + (q * GT + j) * (K - 1)
                for k in range(K):
                    into = x if k == K - 1 else acc[:, j, k % 2, :]
                    add = x if k == 0 else acc[:, j, (k - 1) % 2, :]
                    if k > 0:
                        dve.wait_ge(steps, base + k)
                    nc.vector.scalar_tensor_tensor(out=into, in0=got[:, j, k, :],
                                                   scalar=weights[:, q % 2, j * K + k:j * K + k + 1], in1=add,
                                                   op0=ALU.mult, op1=ALU.add).then_inc(used if k == K - 1 else steps, 1)
            stage(0, 0)
            with dve.Fori(0, NG // 2 - 1) as it:
                for q in range(2):
                    stage(it, q + 1)
                    for j in range(GT):
                        tile(it, q, j)
            for q in range(2):
                if q == 0:
                    stage(NG // 2 - 1, 1)
                for j in range(GT):
                    tile(NG // 2 - 1, q, j)
            dve.wait_ge(used, NT + GT)


C_HEADS = 16
C_DH = H // C_HEADS
C_HALF = C_HEADS // KT
VW = C_DH + 1


def attention1(nc, ins, sb, m, w):
    with ExitStack() as ctx:
        ph = Phase(ctx, nc, "attn1")
        x_sb, ident = sb["x"], sb["ident"]
        stats_a, mv_a = ph.sbuf("stats_a", [P, GT, 6]), ph.sbuf("mv_a", [P, GT, 2])
        vare_a, rstd_a = ph.sbuf("vare_a", [P, GT]), ph.sbuf("rstd_a", [P, GT])
        stats_f, mv_f = ph.sbuf("stats_f", [P, GT, 6]), ph.sbuf("mv_f", [P, GT, 2])
        vare_f, rstd_f = ph.sbuf("vare_f", [P, GT]), ph.sbuf("rstd_f", [P, GT])
        stats_d, mv_d = ph.sbuf("stats_d", [P, 2, 6]), ph.sbuf("mv_d", [P, 2, 2])
        vare_d, rstd_d = ph.sbuf("vare_d", [P, 2]), ph.sbuf("rstd_d", [P, 2])
        xa = ph.sbuf("xa", [P, GT, H])
        xf = ph.sbuf("xf", [P, 2, GT, H])
        xt = ph.sbuf("xt", [P, KT, GN])
        xft = ph.sbuf("xft", [P, KT, GN])
        ct = ph.sbuf("ct", [P, 2, KT, GN])
        q_t = ph.sbuf("q_t", [P, 2, KT, GN])
        k_t = ph.sbuf("k_t", [P, 2, KT, GN])
        q_bd = ph.sbuf("q_bd", [P, 2, KT, 2, C_HALF, S])
        v_bd = ph.sbuf("v_bd", [P, 4, C_HEADS, 2, VW])
        clipped = ph.sbuf("clipped", [P, KT, 512])
        probs = ph.sbuf("probs", [P, 2, KT, 512])
        rsum = ph.sbuf("rsum", [P, C_HALF, 2])
        heads = ph.sbuf("heads", [P, 2, C_HALF, C_DH])
        ctx_t = ph.sbuf("ctx_t", [P, KT, 2, S])
        delta = ph.sbuf("delta", [P, 2, H])
        scaled = ph.sbuf("scaled", [P, H])
        xb = ph.sbuf("xb", [P, 2, H])
        ps_x = ph.psum("ps_x", [P, KT, GN])
        ps_q = ph.psum("ps_q", [P, GN])
        ps_s = ph.psum("ps_s", [P, KT, 512])
        ps_pv = ph.psum("ps_pv", [P, 512])
        ps_c = ph.psum("ps_c", [P, 512])
        rt = Routing(ctx, nc, sb, m, w["gate"], w["gate_b"])
        opened, passed = ph.sem("opened"), ph.sem("passed")
        rt.passed = passed
        loaded = [ph.sem("ct_loaded0"), ph.sem("ct_loaded1")]
        steps_a, steps_f, steps_d = ph.sem("norm_steps_a"), ph.sem("norm_steps_f"), ph.sem("norm_steps_d")
        rstd_a_ready, xa_ready, xa_t_made, xt_ready = (ph.sem(n) for n in ("rstd_a", "xa_ready", "xa_t_made", "xt_ready"))
        rstd_f_ready, xf_ready, xf_t_made, xft_ready = (ph.sem(n) for n in ("rstd_f", "xf_ready", "xf_t_made", "xft_ready"))
        by_group = [rstd_a_ready, xa_ready, xa_t_made, xt_ready, rstd_f_ready, xf_ready, xf_t_made, xft_ready]
        names = ("qbd0_ready", "qbd1_ready", "s_made", "clip_ready", "exp_ready", "pv_made", "rsum_ready",
                 "heads_ready", "ct_made", "ct_copied", "y_made", "delta_ready", "rstd_d", "xb_ready", "scaled_ready",
                 "x_ready")
        by_tile = {n: ph.sem(n) for n in names}
        (qbd0_ready, qbd1_ready, s_made, clip_ready, exp_ready, pv_made, rsum_ready, heads_ready, ct_made,
         ct_copied, y_made, delta_ready, rstd_d_ready, xb_ready, scaled_ready, x_ready) = by_tile.values()
        bank_made, bank_free = ph.sem("bank_made"), ph.sem("bank_free")
        USES = 8
        prepared = ph.sem("prepared")
        masks_now = ph.sbuf("masks_now", [P, 4, 2])
        LG, LT = 4, 4
        BODY = 2 * GT
        block = ctx.enter_context(nc.Block())

        def gdone(eng, s, it, q):
            eng.wait_ge(s, it * 2 + (q + 1 + LG))

        def tdone(eng, s, it, r):
            eng.wait_ge(s, it * BODY + (r + 1 + LT))

        def use_done(eng, s, it, u):
            eng.wait_ge(s, it * (2 * USES) + (u + 1 + USES))

        def gexists(it, q):
            return not isinstance(it, int) or 0 <= it * 2 + q < NG

        def texists(it, r):
            return not isinstance(it, int) or 0 <= it * BODY + r < NT

        def value_use(r):
            return USES * (r // GT) + (0, 1, 4, 7)[r % GT]

        def queries_ready(eng, it, q):
            use_done(eng, bank_free, it, USES * (q - 1) + 3)

        def keys_ready(eng, it, q):
            use_done(eng, bank_free, it, USES * (q - 1) + 6)

        def run(eng, step):
            for r in range(BODY):
                step(0, r)
            with eng.Fori(1, NG // 2 - 1) as it:
                for r in range(BODY):
                    step(it, r)
            for r in range(BODY + 2 * GT + 2):
                step(NG // 2 - 1, r)

        @block.sync
        def _(sp):
            def load(it, q):
                sp.dma_start(ct[:, q % 2, :, :], ins["ctx_t"][:, :, bass.ds((it * 2 + q) * GN, GN)]).then_inc(loaded[q % 2], 16)
            load(0, 0)
            load(0, 1)
            with sp.Fori(0, NG // 2 - 1) as it:
                for q in range(2):
                    use_done(sp, bank_made, it, value_use(q * GT + 1))
                    sp.sem_inc(passed, 1)
                    load(it, q + 2)

        def block_diagonal(engine, it, r, f, ready):
            t0 = (r % GT) * P
            for b in range(2):
                source = q_t[:, (r // GT) % 2, f, t0 + b * S:t0 + (b + 1) * S]
                last = engine.tensor_tensor(q_bd[:, r % 2, f, b, :, :], source.unsqueeze(1).to_broadcast([P, C_HALF, S]),
                                            w["head_mask"][:, :].unsqueeze(2).to_broadcast([P, C_HALF, S]), ALU.mult)
            last.then_inc(ready, 1)

        @block.tensor
        def _(pe):
            pe.wait_ge(opened, 1)

            def ct_loaded(it, q):
                pe.wait_ge(loaded[q % 2], it * 16 + 16 * (q // 2 + 1))

            def values(it, r, u):
                ct_loaded(it, r // GT)
                use_done(pe, bank_free, it, u - 1)
                for kt in range(KT):
                    last = nc.tensor.matmul(ps_q[:, 0:H], ct[:, (r // GT) % 2, kt, (r % GT) * P:(r % GT + 1) * P],
                                            w["v"][:, kt, :], start=(kt == 0), stop=(kt == KT - 1))
                last.then_inc(bank_made, 1)

            def project(it, q, f, u, weights, source):
                use_done(pe, bank_free, it, u - 1)
                for kt in range(KT):
                    last = nc.tensor.matmul(ps_q[:, :], weights[:, kt, f * P:(f + 1) * P], source[:, kt, :],
                                            start=(kt == 0), stop=(kt == KT - 1))
                last.then_inc(bank_made, 1)

            def queries(it, q, f, u):
                gdone(pe, xt_ready, it, q)
                project(it, q, f, u, w["q"], xt)

            def keys(it, q, f, u):
                ct_loaded(it, q)
                project(it, q, f, u, w["k"], ct[:, q % 2, :, :])

            def scores(it, r):
                keys_ready(pe, it, r // GT)
                tdone(pe, qbd0_ready, it, r)
                tdone(pe, qbd1_ready, it, r)
                tdone(pe, clip_ready, it, r - 1)
                for f in range(KT):
                    for b in range(2):
                        t0 = (r % GT) * P + b * S
                        last = nc.tensor.matmul(ps_s[b * S:(b + 1) * S, f, :], k_t[:, (r // GT) % 2, f, t0:t0 + S],
                                                q_bd[:, r % 2, f, b, :, :].rearrange("p h s -> p (h s)"),
                                                start=True, stop=True)
                last.then_inc(s_made, 1)

            def transposes(it, q, source, ready, free, made):
                gdone(pe, ready, it, q)
                for s, d in free:
                    gdone(pe, s, it, q + d)
                for j in range(GT):
                    for kt in range(KT):
                        last = nc.tensor.transpose(ps_x[:, kt, j * P:(j + 1) * P], source[:, j, kt * P:(kt + 1) * P], ident[:, :])
                last.then_inc(made, 1)

            def context_transposes(it, r):
                tdone(pe, heads_ready, it, r)
                tdone(pe, delta_ready, it, r - 1)
                for b in range(2):
                    last = nc.tensor.transpose(ps_c[:, b * P:(b + 1) * P], heads[:, b, :, :].rearrange("p h d -> p (h d)"),
                                               ident[:, :])
                last.then_inc(ct_made, 1)

            def outputs(it, r):
                tdone(pe, exp_ready, it, r)
                use_done(pe, bank_free, it, value_use(r - 2))
                tdone(pe, heads_ready, it, r - 1)
                for h in range(C_HALF):
                    for f in range(KT):
                        hh = f * C_HALF + h
                        last = nc.tensor.matmul(ps_pv[f * S:(f + 1) * S, h * 2 * VW:(h + 1) * 2 * VW],
                                                probs[:, r % 2, f, h * S:(h + 1) * S],
                                                v_bd[:, r % 4, hh, :, :].rearrange("p b d -> p (b d)"), start=True, stop=True)
                last.then_inc(pv_made, 1)

            def projection(it, r):
                tdone(pe, ct_copied, it, r)
                for f in range(KT):
                    last = nc.tensor.matmul(ps_c[:, 256:512], ctx_t[:, f, :, :].rearrange("p b s -> p (b s)"), w["o"][:, f, :],
                                            start=(f == 0), stop=(f == KT - 1))
                last.then_inc(y_made, 1)

            def step(it, r):
                g, j = r // GT, r % GT
                u = value_use(r)
                if texists(it, r + 2):
                    values(it, r + 2, u)
                if texists(it, r + 1):
                    scores(it, r + 1)
                if j == 0 and gexists(it, g + 1):
                    transposes(it, g + 1, xa, xa_ready, ((xt_ready, -1), (xft_ready, -3)), xa_t_made)
                if j == 2 and gexists(it, g - 1):
                    transposes(it, g - 1, xf[:, (g - 1) % 2, :, :], xf_ready,
                               ((xft_ready, -1),) + (((xt_ready, 2),) if gexists(it, g + 1) else ()), xf_t_made)
                if texists(it, r - 1):
                    context_transposes(it, r - 1)
                for f in range(KT):
                    if j == 1 and gexists(it, g + 1):
                        queries(it, g + 1, f, u + 1 + f)
                    if j == 2 and gexists(it, g + 1):
                        keys(it, g + 1, f, u + 1 + f)
                    if f == 0 and texists(it, r):
                        outputs(it, r)
                if texists(it, r - 1):
                    projection(it, r - 1)
                if j == 3 and gexists(it, g - 1):
                    gdone(pe, xft_ready, it, g - 1)
                    rt.make_logits(pe, it, g - 1, xft, gdone)
                if j == 0 and gexists(it, g - 2):
                    rt.make_ranks(pe, it, g - 2, gdone)

            transposes(0, 0, xa, xa_ready, (), xa_t_made)
            for f in range(KT):
                queries(0, 0, f, f - 6)
            values(0, 0, -4)
            for f in range(KT):
                keys(0, 0, f, f - 3)
            values(0, 1, -1)
            scores(0, 0)
            run(pe, step)

        @block.scalar
        def _(act):
            act.wait_ge(opened, 1)

            def copy_projected(it, q, f, u, out, bias, scale):
                use_done(act, bank_made, it, u)
                if not (isinstance(it, int) and it * 2 + q < 2):
                    tdone(act, s_made, it, (q - 1) * GT - 1)
                    tdone(act, qbd0_ready, it, (q - 1) * GT - 1)
                    tdone(act, qbd1_ready, it, (q - 1) * GT - 1)
                nc.scalar.activation(out[:, q % 2, f, :], ps_q[:, :], ACT.Identity, bias=bias[:, f:f + 1],
                                     scale=scale).then_inc(bank_free, 1)

            def exponentials(it, r):
                tdone(act, clip_ready, it, r)
                tdone(act, pv_made, it, r - 2)
                nc.scalar.activation(probs[:, r % 2, :, :], clipped[:, :, :], ACT.Exp, bias=masks_now[:, r % 4, 1:2],
                                     scale=masks_now[:, r % 4, 0:1]).then_inc(exp_ready, 1)

            def copy_transposed(it, q, out, made, ready, reader):
                gdone(act, made, it, q)
                reader(it, q)
                last = nc.scalar.activation(out[:, :, :], ps_x[:, :, :], ACT.Copy)
                last.then_inc(ready, 1)

            def xt_reader(it, q):
                if not (isinstance(it, int) and it * 2 + q < 1):
                    use_done(act, bank_made, it, USES * (q - 2) + 3)

            def xft_reader(it, q):
                gdone(act, rt.logits_made, it, q - 1)

            def copy_context(it, r):
                tdone(act, ct_made, it, r)
                tdone(act, y_made, it, r - 1)
                nc.scalar.activation(ctx_t[:, :, :, :], ps_c[:, 0:256].rearrange("p (b f s) -> p f b s", b=2, f=KT), ACT.Copy)\
                    .then_inc(ct_copied, 1)

            def step(it, r):
                g, j = r // GT, r % GT
                u = value_use(r)
                if j == 0 and gexists(it, g + 1):
                    copy_transposed(it, g + 1, xt, xa_t_made, xt_ready, xt_reader)
                if j == 2 and gexists(it, g - 1):
                    copy_transposed(it, g - 1, xft, xf_t_made, xft_ready, xft_reader)
                if texists(it, r - 1):
                    copy_context(it, r - 1)
                for f in range(KT):
                    if j == 1 and gexists(it, g + 1):
                        copy_projected(it, g + 1, f, u + 1 + f, q_t, w["bq"], C_DH ** -0.5)
                    if j == 2 and gexists(it, g + 1):
                        copy_projected(it, g + 1, f, u + 1 + f, k_t, w["bk"], 1.0)
                    if f == 0 and texists(it, r + 1):
                        exponentials(it, r + 1)

            copy_transposed(0, 0, xt, xa_t_made, xt_ready, xt_reader)
            for f in range(KT):
                copy_projected(0, 0, f, f - 6, q_t, w["bq"], C_DH ** -0.5)
            for f in range(KT):
                copy_projected(0, 0, f, f - 3, k_t, w["bk"], 1.0)
            exponentials(0, 0)
            run(act, step)

        @block.vector
        def _(dve):
            dve.wait_ge(opened, 1)

            def statistics(it, q, stats, mv, vare, steps):
                norm_statistics(nc, dve, x_sb, it, q, stats, mv, vare, steps, passed)

            def apply_a(it, q):
                norm_apply(nc, dve, x_sb, it, q, mv_a, rstd_a, xa, rstd_a_ready, xa_ready, gdone,
                           lambda: gdone(dve, xa_t_made, it, q - 1))

            def apply_f(it, q):
                def free():
                    gdone(dve, xf_t_made, it, q - 2)
                    gdone(dve, rt.rows_sent, it, q - 2)
                norm_apply(nc, dve, x_sb, it, q, mv_f, rstd_f, xf[:, q % 2, :, :], rstd_f_ready, xf_ready, gdone, free)

            def copy_values(it, r, u):
                use_done(dve, bank_made, it, u)
                tdone(dve, pv_made, it, r - 4)
                for b in range(2):
                    half = slice(b * S, (b + 1) * S)
                    last = nc.vector.tensor_tensor(v_bd[half, r % 4, :, b, 0:C_DH],
                                                   ps_q[half, 0:H].rearrange("p (h d) -> p h d", h=C_HEADS),
                                                   w["bv"][half, :].rearrange("p (h d) -> p h d", h=C_HEADS), ALU.add)
                last.then_inc(bank_free, 1)

            def spread_queries(it, r):
                queries_ready(dve, it, r // GT)
                tdone(dve, s_made, it, r - 2)
                block_diagonal(nc.vector, it, r, 0, qbd0_ready)

            def clip(it, r):
                tdone(dve, s_made, it, r)
                tdone(dve, exp_ready, it, r - 1)
                nc.vector.tensor_copy(masks_now[:, r % 4, :], sb["masks"][:, bass.ds(it * BODY + r, 1), :]
                                      .rearrange("p a c -> p (a c)"))
                nc.vector.tensor_scalar(clipped[:, :, :], ps_s[:, :, :], 50.0, -50.0, ALU.min, ALU.max).then_inc(clip_ready, 1)

            def normalise(it, r):
                tdone(dve, pv_made, it, r)
                ps = ps_pv[:, 0:C_HALF * 2 * VW].rearrange("p (h b v) -> p h b v", h=C_HALF, b=2)
                tdone(dve, heads_ready, it, r - 1)
                nc.vector.reciprocal(rsum[:, :, :], ps[:, :, :, C_DH]).then_inc(rsum_ready, 1)
                tdone(dve, rsum_ready, it, r)
                tdone(dve, ct_made, it, r - 1)
                nc.vector.tensor_tensor(heads[:, :, :, :].rearrange("p b h d -> p h b d"), ps[:, :, :, 0:C_DH],
                                        rsum[:, :, :].unsqueeze(3).to_broadcast([P, C_HALF, 2, C_DH]), ALU.mult)\
                    .then_inc(heads_ready, 1)

            def delta_statistics(it, r):
                base = it * (3 * BODY) + 3 * r
                tdone(dve, y_made, it, r)
                tdone(dve, scaled_ready, it, r - 2)
                nc.vector.tensor_tensor(delta[:, r % 2, :], ps_c[:, 256:512], w["bo"][:, :], ALU.add).then_inc(delta_ready, 1)
                tdone(dve, delta_ready, it, r)
                dve.sem_inc(passed, 1)
                nc.vector.bn_stats(stats_d[:, r % 2, :], delta[:, r % 2, :]).then_inc(steps_d, 1)
                dve.wait_ge(steps_d, base + 1)
                dve.sem_inc(passed, 1)
                nc.vector.bn_aggr(mv_d[:, r % 2, :], stats_d[:, r % 2, :]).then_inc(steps_d, 1)
                dve.wait_ge(steps_d, base + 2)
                nc.vector.tensor_scalar(vare_d[:, r % 2:r % 2 + 1], mv_d[:, r % 2, 1:2], w["rs"][:, 1:2], EPS,
                                        ALU.mult, ALU.add).then_inc(steps_d, 1)

            def residual(it, r):
                tile = x_sb[:, bass.ds(it * BODY + r, 1), :].rearrange("p a n -> p (a n)")
                tdone(dve, rstd_d_ready, it, r)
                tdone(dve, xb_ready, it, r)
                tdone(dve, x_ready, it, r - 1)
                nc.vector.scalar_tensor_tensor(out=scaled[:, :], in0=delta[:, r % 2, :], scalar=mv_d[:, r % 2, 0:1],
                                               in1=w["gamma"][:, :], op0=ALU.subtract, op1=ALU.mult).then_inc(scaled_ready, 1)
                tdone(dve, scaled_ready, it, r)
                nc.vector.scalar_tensor_tensor(out=tile, in0=scaled[:, :], scalar=rstd_d[:, r % 2:r % 2 + 1],
                                               in1=xb[:, r % 2, :], op0=ALU.mult, op1=ALU.add).then_inc(x_ready, 1)

            def step(it, r):
                g, j = r // GT, r % GT
                if texists(it, r - 2):
                    residual(it, r - 2)
                if j == 2 and gexists(it, g - 1):
                    apply_f(it, g - 1)
                if texists(it, r + 2):
                    copy_values(it, r + 2, value_use(r))
                if j == 0 and gexists(it, g - 2):
                    rt.choose(dve, it, g - 2, gdone)
                if j == 1 and gexists(it, g - 1):
                    tdone(dve, x_ready, it, g * GT - 1)
                    statistics(it, g - 1, stats_f, mv_f, vare_f, steps_f)
                if texists(it, r + 1):
                    clip(it, r + 1)
                if texists(it, r + 2):
                    spread_queries(it, r + 2)
                if texists(it, r):
                    normalise(it, r)
                if j == 1 and gexists(it, g - 2):
                    rt.place_rows(dve, it, g - 2, gdone)
                if texists(it, r - 1):
                    delta_statistics(it, r - 1)
                if j == 2 and gexists(it, g + 2):
                    statistics(it, g + 2, stats_a, mv_a, vare_a, steps_a)
                if j == 3 and gexists(it, g + 2):
                    apply_a(it, g + 2)

            nc.vector.memset(v_bd[:, :, :, :, :], 0.0).then_inc(prepared, 1)
            dve.wait_ge(prepared, 1)
            for b in range(2):
                last = nc.vector.memset(v_bd[b * S:(b + 1) * S, :, :, b, C_DH:VW], 1.0)
            last.then_inc(prepared, 1)
            for q in range(2):
                statistics(0, q, stats_a, mv_a, vare_a, steps_a)
                apply_a(0, q)
            copy_values(0, 0, -4)
            copy_values(0, 1, -1)
            spread_queries(0, 0)
            spread_queries(0, 1)
            clip(0, 0)
            run(dve, step)

        @block.gpsimd
        def _(pool):
            for s in by_group:
                pool.sem_inc(s, LG)
            for s in by_tile.values():
                pool.sem_inc(s, LT)
            for s in (bank_made, bank_free):
                pool.sem_inc(s, 2)
            rt.start(pool, LG)
            pool.sem_inc(opened, 1)

            def deviation(it, q, vare, rstd, steps, xn_ready, rstd_ready):
                norm_deviation(nc, pool, sb, it, q, vare, rstd, steps, xn_ready, rstd_ready, gdone)

            def spread_queries(it, r):
                queries_ready(pool, it, r // GT)
                tdone(pool, s_made, it, r - 2)
                block_diagonal(nc.gpsimd, it, r, 1, qbd1_ready)

            def add_beta(it, r):
                tdone(pool, scaled_ready, it, r - 2)
                tdone(pool, x_ready, it, r - 2)
                nc.gpsimd.tensor_tensor(xb[:, r % 2, :], x_sb[:, bass.ds(it * BODY + r, 1), :].rearrange("p a n -> p (a n)"),
                                        w["beta"][:, :], ALU.add).then_inc(xb_ready, 1)

            def delta_deviation(it, r):
                pool.wait_ge(steps_d, it * (3 * BODY) + 3 * (r + 1))
                tdone(pool, x_ready, it, r - 2)
                nc.gpsimd.tensor_tensor(rstd_d[:, r % 2:r % 2 + 1], vare_d[:, r % 2:r % 2 + 1], sb["minus_half"][:, :],
                                        ALU.pow).then_inc(rstd_d_ready, 1)

            def step(it, r):
                g, j = r // GT, r % GT
                if j == 2 and gexists(it, g - 3):
                    rt.mark_sent(pool, it, g - 3)
                if texists(it, r + 2):
                    spread_queries(it, r + 2)
                if j == 1 and gexists(it, g - 1):
                    deviation(it, g - 1, vare_f, rstd_f, steps_f, xf_ready, rstd_f_ready)
                if texists(it, r - 1):
                    add_beta(it, r - 1)
                q = g - 2 if j >= 2 else g - 3
                if gexists(it, q):
                    rt.scatter(pool, it, q, xf[:, q % 2, :, :], ((j + 2) % GT,), gdone)
                if texists(it, r - 1):
                    delta_deviation(it, r - 1)
                if j == 2 and gexists(it, g + 2):
                    deviation(it, g + 2, vare_a, rstd_a, steps_a, xa_ready, rstd_a_ready)

            for q in range(2):
                deviation(0, q, vare_a, rstd_a, steps_a, xa_ready, rstd_a_ready)
            spread_queries(0, 0)
            spread_queries(0, 1)
            for it in range(NG // 2 - 1):
                for r in range(BODY):
                    step(it, r)
            for r in range(BODY + 2 * GT + 2):
                step(NG // 2 - 1, r)


def setup_attention1(nc, ins, sb, w):
    with ExitStack() as ctx:
        ph = Phase(ctx, nc, "setup1")
        mask_i = ph.sbuf("mask_i", [P, NT], I32)
        rs = ph.sbuf("rs_in", [P, 1])
        loaded, steps, masked = ph.sem("weights_loaded"), ph.sem("scale_steps"), ph.sem("mask_steps")
        block = ctx.enter_context(nc.Block())
        names = ("q", "k", "v", "o", "gate")

        @block.sync
        def _(sp):
            for n in names:
                sp.dma_start(w[n][:, :, :], ins["w_" + n]).then_inc(loaded, 16)
            for n in ("bq", "bk"):
                sp.dma_start(w[n][:, :], ins[n]).then_inc(loaded, 16)
            for n in ("bv", "bo", "beta", "gamma", "gate_b"):
                sp.dma_start(w[n][:, :], ins[n].broadcast_to([P, w[n].shape[1]])).then_inc(loaded, 16)
            sp.dma_start(rs[:, :], ins["rs"].broadcast_to([P, 1])).then_inc(loaded, 16)
            sp.dma_start(mask_i[:, :], ins["mask"]).then_inc(loaded, 16)

        @block.vector
        def _(dve):
            dve.wait_ge(loaded, 16 * 14)
            nc.vector.tensor_scalar(w["bq"][:, :], w["bq"][:, :], C_DH ** -0.5, None, ALU.mult).then_inc(steps, 1)
            nc.vector.tensor_scalar(w["rs"][:, 0:1], rs[:, :], 0.0, 0.3, ALU.max, ALU.min).then_inc(steps, 1)
            nc.vector.tensor_copy(sb["masks"][:, :, 0], mask_i[:, :]).then_inc(masked, 1)
            dve.wait_ge(masked, 1)
            nc.vector.tensor_scalar(sb["masks"][:, :, 0], sb["masks"][:, :, 0], 0.5, None, ALU.is_gt).then_inc(masked, 1)
            dve.wait_ge(steps, 2)
            nc.vector.tensor_tensor(w["rs"][:, 1:2], w["rs"][:, 0:1], w["rs"][:, 0:1], ALU.mult).then_inc(steps, 1)
            nc.vector.tensor_scalar(w["gamma"][:, :], w["gamma"][:, :], w["rs"][:, 0:1], None, ALU.mult).then_inc(steps, 1)
            dve.wait_ge(masked, 2)
            nc.vector.tensor_scalar(sb["masks"][:, :, 1], sb["masks"][:, :, 0], 50.0, -50.0, ALU.mult, ALU.add)\
                .then_inc(masked, 1)
            dve.wait_ge(steps, 4)
            dve.wait_ge(masked, 3)

        @block.gpsimd
        def _(pool):
            head_mask = w["head_mask"]
            made = ph.sem("head_mask_made")
            nc.gpsimd.memset(head_mask[:, :], 1.0).then_inc(made, 1)
            pool.wait_ge(made, 1)
            nc.gpsimd.affine_select(out=head_mask[:, :], in_=head_mask[:, :], compare_op=ALU.is_ge, fill=0.0,
                                    base=0, pattern=[[-C_DH, C_HALF]], channel_multiplier=1).then_inc(made, 1)
            pool.wait_ge(made, 2)
            nc.gpsimd.affine_select(out=head_mask[:, :], in_=head_mask[:, :], compare_op=ALU.is_gt, fill=0.0,
                                    base=C_DH, pattern=[[C_DH, C_HALF]], channel_multiplier=-1).then_inc(made, 1)
            pool.wait_ge(made, 3)


def combine1(nc, sb, m, out):
    K, E = m.K, m.E
    with ExitStack() as ctx:
        ph = Phase(ctx, nc, "combine1")
        slots = ph.sbuf("slots_now", [P, 2, GT * K], I32)
        weights = ph.sbuf("weights_now", [P, 2, GT * K])
        got = ph.sbuf("rows_got", [P, GT, K, H])
        acc = ph.sbuf("acc", [P, GT, 2, H])
        weighted = ph.sbuf("weighted", [P, GT * K, E])
        by_expert = ph.sbuf("by_expert", [P, GT, E])
        by_expert_t = ph.sbuf("by_expert_t", [P, 2, GT, P])
        ps_t = ph.psum("ps_t", [P, GT, P])
        ps_b = ph.psum("ps_b", [P, GT, 512])
        find = SlotFinder(ph, nc, m)
        opened, passed = ph.sem("opened"), ph.sem("passed")
        staged, steps, used = ph.sem("slots_staged"), ph.sem("sum_steps"), ph.sem("rows_used")
        weight_steps = ph.sem("weight_steps")
        we_t_made, we_t_ready, bias_made = ph.sem("we_t_made"), ph.sem("we_t_ready"), ph.sem("bias_made")
        gathered = [ph.sem(f"gathered{j}") for j in range(GT)]
        stored = ph.sem("tiles_stored")
        block = ctx.enter_context(nc.Block())

        @block.gpsimd
        def _(pool):
            with pool.Fori(0, NG // 2) as it:
                for q in range(2):
                    pool.wait_ge(staged, it * 2 + (q + 1))
                    for j in range(GT):
                        pool.wait_ge(used, it * (2 * GT) + (q * GT + j + 1))
                        pool.sem_inc(passed, 1)
                        for k in range(K):
                            n = j * K + k
                            pool.indirect_dma_start(got[:, j, k, :], None, m.rows_out,
                                                    bass.IndirectOffsetOnAxis(ap=slots[:, q, n:n + 1], axis=0))\
                                .then_inc(gathered[j], 16)

        @block.tensor
        def _(pe):
            pe.wait_ge(opened, 1)
            with pe.Fori(0, NG // 2) as it:
                for q in range(2):
                    pe.wait_ge(weight_steps, it * 4 + (2 * q + 2))
                    pe.wait_ge(we_t_ready, it * 2 + (q + 1))
                    for j in range(GT):
                        last = nc.tensor.transpose(ps_t[0:E, j, :], by_expert[:, j, :], sb["ident"][:, :])
                    last.then_inc(we_t_made, 1)
                    pe.wait_ge(we_t_ready, it * 2 + (q + 2))
                    pe.wait_ge(used, it * (2 * GT) + (q * GT + GT))
                    for j in range(GT):
                        last = nc.tensor.matmul(ps_b[:, j, 0:H], by_expert_t[:, q, j, :], sb["b_down"][:, :],
                                                start=True, stop=True)
                    last.then_inc(bias_made, 1)

        @block.scalar
        def _(act):
            act.wait_ge(opened, 1)
            with act.Fori(0, NG // 2) as it:
                for q in range(2):
                    act.wait_ge(we_t_made, it * 2 + (q + 1))
                    nc.scalar.activation(by_expert_t[0:E, q, :, :], ps_t[0:E, :, :], ACT.Copy).then_inc(we_t_ready, 1)

        @block.vector
        def _(dve):
            dve.sem_inc(used, GT)
            nc.vector.memset(by_expert_t[:, :, :, :], 0.0).then_inc(we_t_ready, 1)
            dve.wait_ge(we_t_ready, 1)
            dve.sem_inc(opened, 1)

            def stage(it, q):
                if not (isinstance(it, int) and it * 2 + q == 0):
                    dve.wait_ge(used, it * (2 * GT) + q * GT)
                nc.vector.tensor_copy(weights[:, q % 2, :].rearrange("p (j k) -> p j k", j=GT),
                                      m.weights[:, bass.ds((it * 2 + q) * GT, GT), :])
                find.rows(dve, it, q, slots, staged)
                nc.vector.tensor_tensor(weighted[:, :, :].rearrange("p (j k) e -> p j k e", j=GT),
                                        find.onehot[:, :, :].rearrange("p (j k) e -> p j k e", j=GT),
                                        m.weights[:, bass.ds((it * 2 + q) * GT, GT), :].unsqueeze(3)
                                        .to_broadcast([P, GT, K, E]), ALU.mult).then_inc(weight_steps, 1)
                dve.wait_ge(weight_steps, it * 4 + (2 * q + 1))
                if not (isinstance(it, int) and it * 2 + q == 0):
                    dve.wait_ge(we_t_made, it * 2 + q)
                nc.vector.tensor_reduce(by_expert[:, :, :], weighted[:, :, :].rearrange("p (j k) e -> p j e k", j=GT),
                                        AX.X, ALU.add).then_inc(weight_steps, 1)

            def tile(it, q, j):
                x = sb["x"][:, bass.ds((it * 2 + q) * GT + j, 1), :].rearrange("p a n -> p (a n)")
                if j == 0:
                    dve.wait_ge(staged, it * 2 + (q + 1))
                    dve.wait_ge(bias_made, it * 2 + (q + 1))
                dve.wait_ge(gathered[j], it * (32 * K) + 16 * K * (q + 1))
                dve.wait_ge(used, it * (2 * GT) + (q * GT + j + 1))
                base = it * (2 * GT * K) + (q * GT + j) * K
                nc.vector.tensor_tensor(acc[:, j, 1, :], x, ps_b[:, j, 0:H], ALU.add).then_inc(steps, 1)
                for k in range(K):
                    into = x if k == K - 1 else acc[:, j, k % 2, :]
                    dve.wait_ge(steps, base + (k + 1))
                    nc.vector.scalar_tensor_tensor(out=into, in0=got[:, j, k, :],
                                                   scalar=weights[:, q % 2, j * K + k:j * K + k + 1],
                                                   in1=acc[:, j, (k + 1) % 2, :], op0=ALU.mult, op1=ALU.add)\
                        .then_inc(used if k == K - 1 else steps, 1)
            stage(0, 0)
            with dve.Fori(0, NG // 2 - 1) as it:
                for q in range(2):
                    for j in range(GT):
                        tile(it, q, j)
                        if j == 0:
                            stage(it, q + 1)
            for q in range(2):
                for j in range(GT):
                    tile(NG // 2 - 1, q, j)
                    if j == 0 and q == 0:
                        stage(NG // 2 - 1, 1)
            dve.wait_ge(used, NT + GT)

        @block.sync
        def _(sp):
            with sp.Fori(0, NT) as t:
                sp.wait_ge(used, t + (GT + 1))
                sp.sem_inc(passed, 1)
                sp.dma_start(out[bass.ds(t * P, P), :], sb["x"][:, bass.ds(t, 1), :].rearrange("p a n -> p (a n)"))\
                  .then_inc(stored, 16)
            sp.wait_ge(stored, 16 * NT)


def load_weights(nc, into, source, pieces):
    with ExitStack() as ctx:
        ph = Phase(ctx, nc, "load")
        loaded = ph.sem("experts_loaded")
        block = ctx.enter_context(nc.Block())
        n = into.shape[1] // pieces

        @block.sync
        def _(sp):
            for c in range(0, into.shape[1], n):
                sp.dma_start(into[:, c:c + n, :, :], source[:, c:c + n, :, :]).then_inc(loaded, 16)
            sp.wait_ge(loaded, 16 * pieces)


def build_program(nc, ins, out):
    with ExitStack() as ctx:
        def sbt(name, shape, dt=F32):
            return ctx.enter_context(nc.sbuf_tensor(name, shape, dt))
        m0 = Moe(nc, "l0", experts=16, top=2, inner=64)
        m1 = Moe(nc, "l1", experts=32, top=4, inner=128)
        sb = dict(x=sbt("x_sb", [P, NT, H]), ident=sbt("ident", [P, P]), minus_half=sbt("minus_half", [P, 1]),
                  onesf=sbt("onesf", [P, 1]), ones=sbt("ones", [P, P], BF16), before=sbt("before", [P, P], BF16),
                  upto=sbt("upto", [P, P]), zeros=sbt("zeros", [P, H]), block_iota=sbt("block_iota", [P, 256]),
                  masks=sbt("masks", [P, NT, 2]), term_ones=sbt("term_ones", [P, P], BF16),
                  bias1=sbt("bias1", [P, m1.E, 2 * m1.I], BF16), b_down=sbt("b_down_sb", [P, H]),
                  b_out=sbt("b_out", [P, 1]))
        m1.tables(ctx, nc)
        w1 = dict(gate=sbt("w1_gate", [P, KT, m1.E]), gate_b=sbt("w1_gate_b", [P, m1.E]),
                  q=sbt("w1_q", [P, KT, H]), k=sbt("w1_k", [P, KT, H]), v=sbt("w1_v", [P, KT, H]), o=sbt("w1_o", [P, KT, H]),
                  bq=sbt("w1_bq", [P, KT]), bk=sbt("w1_bk", [P, KT]), bv=sbt("w1_bv", [P, H]), bo=sbt("w1_bo", [P, H]),
                  beta=sbt("w1_beta", [P, H]), gamma=sbt("w1_gamma", [P, H]), rs=sbt("w1_rs", [P, 2]),
                  head_mask=sbt("head_mask", [P, C_HALF]))
        w_down1 = sbt("w_down1", [P, m1.E, H])
        later_loaded = ctx.enter_context(nc.semaphore("later_loaded"))

        with ExitStack() as layer0:
            def sb0(name, shape, dt=F32):
                return layer0.enter_context(nc.sbuf_tensor(name, shape, dt))
            m0.tables(layer0, nc)
            w0 = dict(gate=sb0("w0_gate", [P, KT, m0.E + 1]), shared_in=sb0("w0_shared_in", [P, 2, KT, H]),
                      shared_out=sb0("w0_shared_out", [P, 2, H]))
            w_gu0 = sb0("w_gu0", [P, m0.E, KT, 2 * m0.I])
            w_down0 = sb0("w_down0", [P, m0.E, H])
            sb["w_down0"] = w_down0
            later = [(w0["gate"][:, :, :], ins["w0_gate"]), (w0["shared_in"][:, :, :, :], ins["shared_in"]),
                     (w0["shared_out"][:, :, :], ins["shared_out"]), (w_gu0[:, :, :, :], ins["w_gu0"]),
                     (w_down0[0:m0.I, :, :], ins["w_down0"]), (w_down1[:, :, :], ins["w_down1"])]
            with ExitStack() as attention:
                def sba(name, shape):
                    return attention.enter_context(nc.sbuf_tensor(name, shape, F32))
                sb.update(a_bd=sba("a_bd", [P, A_HEADS, P]), bv=sba("bv", [P, A_HEADS * S]),
                          ctx_bd=sba("ctx_bd", [P, 2, 2 * A_N]))
                setup_attention_weights(nc, ins, sb, later, later_loaded)
                setup_constants(nc, ins, sb, (m0, m1))
                setup_attention1(nc, ins, sb, w1)
                attention0(nc, ins, sb)
            wait_for(nc, later_loaded, 16 * len(later))
            shared_expert(nc, sb, m0, w0)
            block_tables(nc, sb, m0)
            experts(nc, sb, m0, w_gu0, w_down0, None, None, Swish)
            combine0(nc, sb, m0)
        attention1(nc, ins, sb, m1, w1)
        block_tables(nc, sb, m1)
        with nc.sbuf_tensor("w_gu1", [P, m1.E, KT, 2 * m1.I], F32) as w_gu1:
            load_weights(nc, w_gu1, ins["w_gu1"], 8)
            experts(nc, sb, m1, w_gu1, w_down1, sb["bias1"], sb["term_ones"], ClippedSwish)
        combine1(nc, sb, m1, out)


def wait_for(nc, semaphore, count):
    with nc.Block() as block:
        @block.sync
        def _(sp):
            sp.wait_ge(semaphore, count)


def _heads(w):
    return w.reshape(64, 8, 64).transpose(2, 1, 0)


def _rows(w):
    return w.T.reshape(KT, P, -1).transpose(1, 0, 2)


def _layouts(a):
    import numpy as np
    w_k, w_v = np.split(a["L0_xattn_W_kv"], 2, axis=1)
    e0, e1 = a["L0_ffn_w1"].shape[0], a["L1_ffn_w_gate"].shape[0]
    gu0 = np.concatenate([a["L0_ffn_w1"], a["L0_ffn_w3"]], axis=1).transpose(0, 2, 1)
    gu1 = np.concatenate([a["L1_ffn_w_gate"], a["L1_ffn_w_up"]], axis=2)
    return {
        "x": a["x"].reshape(T, H), "ctx": a["ctx_2048"],
        "wq": _heads(a["L0_xattn_W_q"]), "wk": _heads(w_k), "wv": _heads(w_v),
        "wo": a["L0_xattn_W_out"].reshape(8, 64, 64).transpose(1, 0, 2), "b_out": a["L0_xattn_b_out"].reshape(64, 1),
        "w0_gate": _rows(np.concatenate([a["L0_ffn_gate_w"], a["L0_ffn_shared_gate_w"]])),
        "shared_in": np.stack([_rows(a["L0_ffn_ws_gate"]), _rows(a["L0_ffn_ws_up"])], axis=1),
        "shared_out": _rows(a["L0_ffn_ws_down"]),
        "w_gu0": gu0.reshape(e0, KT, P, -1).transpose(2, 0, 1, 3),
        "w_down0": a["L0_ffn_w2"].transpose(2, 0, 1),
        "ctx_t": a["ctx_2048"].reshape(T, H).T.reshape(KT, P, T).transpose(1, 0, 2),
        "mask": a["mask_BxS2_ik0"].reshape(NT, P).T,
        "w_q": _rows(a["L1_xattn_Wq"]), "w_k": _rows(a["L1_xattn_Wk"]), "w_v": _rows(a["L1_xattn_Wv"]),
        "w_o": _rows(a["L1_xattn_Wo"]), "w_gate": _rows(a["L1_ffn_gate_w"]),
        "bq": a["L1_xattn_bq"].reshape(KT, P).T, "bk": a["L1_xattn_bk"].reshape(KT, P).T,
        "bv": a["L1_xattn_bv"].reshape(1, H), "bo": a["L1_xattn_bo"].reshape(1, H),
        "beta": a["L1_xattn_ln_beta"].reshape(1, H), "gamma": a["L1_xattn_ln_gamma"].reshape(1, H),
        "gate_b": a["L1_ffn_gate_b"].reshape(1, -1), "rs": a["L1_xattn_residual_scale"].reshape(1, 1),
        "w_gu1": gu1.reshape(e1, KT, P, -1).transpose(2, 0, 1, 3),
        "w_down1": a["L1_ffn_w_down"].transpose(1, 0, 2),
        "bias_gu1": np.concatenate([a["L1_ffn_b_gate"], a["L1_ffn_b_up"]], axis=1), "b_down1": a["L1_ffn_b_down"],
    }


def kernel(**inputs):
    import numpy as np
    import concourse.bacc as bacc
    from concourse.bass_utils import run_bass_kernel_spmd

    nc = bacc.Bacc("TRN2", target_bir_lowering=False, num_devices=1)
    arrays, ins = {}, {}
    for name, a in _layouts({n: np.asarray(a) for n, a in inputs.items()}).items():
        arrays["in_" + name] = np.ascontiguousarray(a)
        ins[name] = nc.dram_tensor("in_" + name, a.shape, mybir.dt.from_np(a.dtype), kind="ExternalInput").ap()
    out = nc.dram_tensor("out", (T, H), F32, kind="ExternalOutput").ap()
    build_program(nc, ins, out)
    result = run_bass_kernel_spmd(nc, [arrays], core_ids=[0])
    return result.results[0]["out"].reshape(B, S, H)
```

```python
import concourse.bass as bass
from concourse import mybir
from contextlib import ExitStack

F32 = mybir.dt.float32
BF16 = mybir.dt.bfloat16
I32 = mybir.dt.int32
ALU = mybir.AluOpType
ACT = mybir.ActivationFunctionType
AX = mybir.AxisListType

P = 128
B, S, H = 64, 64, 256
T = B * S
NT = T // P
KT = H // P
EPS = 1e-5

A_HEADS = 8
A_DH = 64
A_N = H

LEAD = 2


class Phase:

    def __init__(self, ctx, nc, name):
        self.ctx, self.nc, self.name = ctx, nc, name
        self.semaphores = []
        ctx.callback(self.clear)

    def clear(self):
        if self.semaphores:
            self.nc.clear_and_free_semaphores(self.semaphores)
            self.nc.all_engine_barrier()

    def sbuf(self, name, shape, dt=F32):
        return self.ctx.enter_context(self.nc.sbuf_tensor(f"{self.name}_{name}", shape, dt))

    def psum(self, name, shape, dt=F32):
        return self.ctx.enter_context(self.nc.psum_tensor(f"{self.name}_{name}", shape, dt))

    def sem(self, name):
        semaphore = self.nc.alloc_semaphore(f"{self.name}_{name}")
        self.semaphores.append(semaphore)
        return semaphore


def setup_attention_weights(ph, block, nc, ins, sb):
    wq = ph.sbuf("wq_dup", [A_DH, A_HEADS, 2, S])
    wk = ph.sbuf("wk_h", [A_DH, A_HEADS, S])
    wv = ph.sbuf("wv_dup", [A_DH, A_HEADS, 2, S])
    wo = ph.sbuf("wo_h", [A_DH, A_HEADS, S])
    ps = ph.psum("ps_fold", [P, 2, A_HEADS * S])
    weights_in = ph.sem("weights_in")
    zeroed = ph.sem("zeroed")
    folded = ph.sem("products")
    copied = ph.sem("copied")

    @block.sync
    def _(sp):
        for c in range(2):
            sp.dma_start(wq[:, :, c, :], ins["wq"]).then_inc(weights_in, 16)
            sp.dma_start(wv[:, :, c, :], ins["wv"]).then_inc(weights_in, 16)
            sp.dma_start(sb["b_out"][c * S:(c + 1) * S, :], ins["b_out"]).then_inc(weights_in, 16)
        sp.dma_start(wk[:, :, :], ins["wk"]).then_inc(weights_in, 16)
        sp.dma_start(wo[:, :, :], ins["wo"]).then_inc(weights_in, 16)
    @block.gpsimd
    def _(pool):
        pool.memset(sb["minus_half"][:, :], -0.5)
        pool.memset(sb["onesf"][:, :], 1.0)
        pool.memset(sb["ident"][:, :], 0.0).then_inc(zeroed, 1)
        pool.wait_ge(zeroed, 1)
        pool.affine_select(out=sb["ident"][:, :], in_=sb["ident"][:, :], compare_op=ALU.not_equal, fill=1.0,
                           base=0, pattern=[[-1, P]], channel_multiplier=1).then_inc(zeroed, 1)

    @block.tensor
    def _(pe):
        pe.wait_ge(weights_in, 16 * 8)
        for h in range(A_HEADS):
            nc.tensor.matmul(ps[:, 0, h * S:(h + 1) * S], wq[:, h, :, :].rearrange("d c s -> d (c s)"),
                             wk[:, h, :], start=True, stop=True)
        for h in range(A_HEADS):
            last = nc.tensor.matmul(ps[:, 1, h * S:(h + 1) * S], wv[:, h, :, :].rearrange("d c s -> d (c s)"),
                                    wo[:, h, :], start=True, stop=True)
        last.then_inc(folded, 1)

    @block.vector
    def _(dve):
        nc.vector.memset(sb["a_bd"][:, :, :, :], 0.0).then_inc(copied, 1)
        nc.vector.memset(sb["ctx_bd"][:, :, :, :], 0.0).then_inc(copied, 1)
        dve.wait_ge(folded, 1)
        dve.wait_ge(copied, 2)
        for c in range(2):
            half = slice(c * S, (c + 1) * S)
            nc.vector.tensor_scalar(sb["a_bd"][half, c, :, :].rearrange("p g n -> p (g n)"), ps[half, 0, :],
                                    float(A_DH) ** -0.5, None, ALU.mult).then_inc(copied, 1)
            nc.vector.tensor_copy(sb["bv"][half, :, :],
                                  ps[half, 1, :].rearrange("p (g c s) -> p g c s", c=2, s=S)[:, :, c, :]).then_inc(copied, 1)
        dve.wait_ge(copied, 6)
        dve.wait_ge(weights_in, 16 * 8)


def attention0(nc, ins, sb, later=(), later_written=None):
    STEPS = 8
    TOTAL = NT * STEPS
    BODY = 2 * STEPS
    with ExitStack() as ctx:
        ph = Phase(ctx, nc, "attn0")
        x_sb, a_bd, bv, ctx_bd, ident = sb["x"], sb["a_bd"], sb["bv"], sb["ctx_bd"], sb["ident"]
        xn = ph.sbuf("xn", [P, 2, A_N])
        stats = ph.sbuf("stats", [P, 6])
        mv = ph.sbuf("mean_var", [P, 2])
        vare = ph.sbuf("var_eps", [P, 1])
        rstd = ph.sbuf("rstd", [P, 1])
        q_sb = ph.sbuf("q_sb", [P, 2, A_N])
        prob = ph.sbuf("prob", [P, 2, 4, A_N])
        negmax = ph.sbuf("negmax", [P, 2, 4])
        sums = ph.sbuf("sums", [P, 2, 4])
        rsum = ph.sbuf("rsum", [P, 2, 4])
        prob_t = ph.sbuf("prob_t", [P, 2, 2, 2, A_N])
        ctx_keys = ph.sbuf("ctx_keys", [P, 2, 2, 2, S])
        y_sb = ph.sbuf("y_sb", [P, 4, A_N])
        ps_s = ph.psum("ps_s", [P, 2, 4, A_N])
        ps_t = ph.psum("ps_t", [P, 2, 2, A_N])
        ps_qo = ph.psum("ps_qo", [P, 2, A_N])
        ps_y = ph.psum("ps_y", [P, 512])

        loaded = [ph.sem("tile_loaded0"), ph.sem("tile_loaded1")]
        ln_steps = ph.sem("ln_steps")
        rstd_ready = ph.sem("rstd_ready")
        xn_ready = ph.sem("xn_ready")
        q_made, q_ready = ph.sem("q_made"), ph.sem("q_ready")
        s_made, max_ready, exp_ready = ph.sem("s_made"), ph.sem("max_ready"), ph.sem("exp_ready")
        rsum_ready, prob_ready = ph.sem("rsum_ready"), ph.sem("prob_ready")
        t_made, t_ready = ph.sem("t_made"), ph.sem("t_ready")
        y_made, y_ready = ph.sem("y_made"), ph.sem("y_ready")
        o_made, x_ready = ph.sem("o_made"), ph.sem("x_ready")
        opened = ph.sem("opened")
        passed = ph.sem("passed")
        block = ctx.enter_context(nc.Block())

        def step_done(eng, s, it, r):
            eng.wait_ge(s, it * BODY + (r + 1 + LEAD))

        def two_done(eng, s, it, p):
            eng.wait_ge(s, it * (BODY // 2) + (p + 1 + LEAD))

        def tile_done(eng, s, it, q):
            eng.wait_ge(s, it * 2 + (q + 1 + LEAD))

        def tile_loaded(eng, it, q):
            eng.wait_ge(loaded[q % 2], it * 64 + 64 * (q // 2 + 1))

        def exists(it, r):
            return not isinstance(it, int) or 0 <= it * BODY + r < TOTAL

        def run(eng, step):
            for r in range(2):
                step(0, r)
            with eng.Fori(0, NT // 2 - 1) as it:
                for r in range(2, BODY + 2):
                    step(it, r)
            for r in range(2, BODY + 2):
                step(NT // 2 - 1, r)

        @block.sync
        def _(sp):
            sp.wait_ge(opened, 1)

            def load(it, q):
                tile = it * 2 + q
                for c in range(2):
                    sp.dma_start(ctx_bd[c * S:(c + 1) * S, q % 2, :, c * A_N:(c + 1) * A_N],
                                 ins["ctx"][bass.ds(tile * 2, 2), :, :].rearrange("b s n -> s b n"))\
                      .then_inc(loaded[q % 2], 16)
                sp.dma_start(ctx_keys[:, q % 2, :, :, :],
                             ins["ctx_keys"][bass.ds(tile, 1), :, :, :, :].rearrange("a p b k s -> (a p) b k s"))\
                  .then_inc(loaded[q % 2], 16)
                sp.dma_start(x_sb[:, bass.ds(tile, 1), :].rearrange("p a n -> p (a n)"),
                             ins["x"][bass.ds(tile * P, P), :]).then_inc(loaded[q % 2], 16)
            load(0, 0)
            load(0, 1)
            for into, source in later:
                sp.dma_start(into, source).then_inc(later_written, 16)
            with sp.Fori(0, NT // 2 - 1) as it:
                for q in range(2):
                    step_done(sp, s_made, it, q * STEPS + STEPS - 1)
                    sp.sem_inc(passed, 1)
                    step_done(sp, y_made, it, q * STEPS + STEPS - 1)
                    sp.sem_inc(passed, 1)
                    tile_done(sp, xn_ready, it, q)
                    sp.sem_inc(passed, 1)
                    load(it, q + 2)

        @block.tensor
        def _(pe):
            pe.wait_ge(opened, 1)

            def queries(it, r):
                tile_done(pe, xn_ready, it, r // STEPS)
                step_done(pe, q_ready, it, r - 1)
                if exists(it, r - 7):
                    two_done(pe, x_ready, it, (r - 7) // 2)
                nc.tensor.matmul(ps_qo[:, 0, :], a_bd[:, r % 2, r % STEPS // 2, :], xn[:, (r // STEPS) % 2, :],
                                 start=True, stop=True).then_inc(q_made, 1)

            def scores(it, r):
                tile_loaded(pe, it, r // STEPS)
                step_done(pe, q_ready, it, r)
                step_done(pe, exp_ready, it, r - 2)
                for qt in range(2):
                    last = nc.tensor.matmul(ps_s[:, r % 2, 2 * qt:2 * qt + 2, :].rearrange("p h k -> p (h k)"),
                                            q_sb[:, r % 2, qt * P:(qt + 1) * P], ctx_bd[:, (r // STEPS) % 2, r % 2, :],
                                            start=True, stop=True)
                last.then_inc(s_made, 1)

            def project(it, r):
                step_done(pe, y_ready, it, r)
                if exists(it, r + 5):
                    step_done(pe, q_ready, it, r + 5)
                for b in range(2):
                    last = nc.tensor.matmul(ps_qo[b * S:(b + 1) * S, 1, :], bv[:, r % STEPS // 2, :],
                                            y_sb[:, (r - 1 + b) % 4, :], start=True, stop=True)
                last.then_inc(o_made, 1)

            def transposes(it, r):
                step_done(pe, prob_ready, it, r)
                step_done(pe, t_ready, it, r - 1)
                for h in range(2):
                    for kt in range(2):
                        for qt in range(2):
                            last = nc.tensor.transpose(ps_t[:, h, kt, qt * P:(qt + 1) * P],
                                                       prob[:, r % 2, 2 * qt + h, kt * P:(kt + 1) * P], ident[:, :])
                last.then_inc(t_made, 1)

            def context_sums(it, r):
                step_done(pe, t_ready, it, r)
                step_done(pe, y_ready, it, r - 1)
                for kt in range(2):
                    for h in range(2):
                        last = nc.tensor.matmul(ps_y[h * S:(h + 1) * S, 0:A_N], ctx_keys[:, (r // STEPS) % 2, r % 2, kt, :],
                                                prob_t[:, r % 2, h, kt, :], start=(kt == 0), stop=(kt == 1))
                last.then_inc(y_made, 1)

            def step(it, r):
                if exists(it, r + 3):
                    queries(it, r + 3)
                if exists(it, r + 2):
                    scores(it, r + 2)
                if r % 2 == 1 and exists(it, r - 2):
                    project(it, r - 2)
                if exists(it, r):
                    transposes(it, r)
                if exists(it, r - 1):
                    context_sums(it, r - 1)

            queries(0, 0)
            queries(0, 1)
            scores(0, 0)
            queries(0, 2)
            scores(0, 1)
            run(pe, step)

        @block.scalar
        def _(act):
            act.wait_ge(opened, 1)

            def copy_queries(it, r):
                step_done(act, q_made, it, r)
                step_done(act, s_made, it, r - 2)
                nc.scalar.activation(q_sb[:, r % 2, :], ps_qo[:, 0, :], ACT.Copy).then_inc(q_ready, 1)

            def copy_sums(it, r):
                step_done(act, y_made, it, r)
                if exists(it, r - 4):
                    two_done(act, o_made, it, (r - 4) // 2)
                nc.scalar.activation(y_sb[:, r % 4, :], ps_y[:, 0:A_N], ACT.Copy).then_inc(y_ready, 1)

            def exps(it, r):
                step_done(act, max_ready, it, r)
                step_done(act, t_made, it, r - 2)
                step_done(act, rsum_ready, it, r - 2)
                for c in range(4):
                    last = nc.scalar.activation(prob[:, r % 2, c, :], ps_s[:, r % 2, c, :], ACT.Exp,
                                                bias=negmax[:, r % 2, c:c + 1], accum_out=sums[:, r % 2, c:c + 1])
                last.then_inc(exp_ready, 1)

            def step(it, r):
                if exists(it, r - 2):
                    copy_sums(it, r - 2)
                if exists(it, r + 3):
                    copy_queries(it, r + 3)
                if exists(it, r + 2):
                    exps(it, r + 2)

            copy_queries(0, 0)
            copy_queries(0, 1)
            exps(0, 0)
            copy_queries(0, 2)
            exps(0, 1)
            run(act, step)

        @block.vector
        def _(dve):
            dve.wait_ge(opened, 1)

            def norm_statistics(it, q):
                tile = x_sb[:, bass.ds(it * 2 + q, 1), :].rearrange("p a n -> p (a n)")
                base = it * 6 + 3 * q
                tile_loaded(dve, it, q)
                nc.vector.bn_stats(stats[:, :], tile).then_inc(ln_steps, 1)
                dve.wait_ge(ln_steps, base + 1)
                dve.sem_inc(passed, 1)
                nc.vector.bn_aggr(mv[:, :], stats[:, :]).then_inc(ln_steps, 1)
                dve.wait_ge(ln_steps, base + 2)
                nc.vector.tensor_scalar(vare[:, :], mv[:, 1:2], EPS, None, ALU.add).then_inc(ln_steps, 1)

            def norm_apply(it, q):
                tile = x_sb[:, bass.ds(it * 2 + q, 1), :].rearrange("p a n -> p (a n)")
                tile_done(dve, rstd_ready, it, q)
                if not (isinstance(it, int) and it * 2 + q < 2):
                    step_done(dve, q_made, it, (q - 2) * STEPS + STEPS - 1)
                nc.vector.tensor_scalar(xn[:, q % 2, :], tile, mv[:, 0:1], rstd[:, 0:1],
                                        ALU.subtract, ALU.mult).then_inc(xn_ready, 1)

            def maxima(it, r):
                step_done(dve, s_made, it, r)
                step_done(dve, exp_ready, it, r - 2)
                nc.vector.tensor_reduce(negmax[:, r % 2, :], ps_s[:, r % 2, :, :], AX.X, ALU.max,
                                        negate=True).then_inc(max_ready, 1)

            def reciprocals(it, r):
                step_done(dve, exp_ready, it, r)
                step_done(dve, prob_ready, it, r - 2)
                nc.vector.reciprocal(rsum[:, r % 2, :], sums[:, r % 2, :]).then_inc(rsum_ready, 1)

            def copy_transposed(it, r):
                step_done(dve, t_made, it, r)
                step_done(dve, y_made, it, r - 2)
                nc.vector.tensor_copy(prob_t[:, r % 2, :, :, :], ps_t[:, :, :, :]).then_inc(t_ready, 1)

            def residual(it, p):
                tile = x_sb[:, bass.ds(it * 2 + p // 4, 1), :].rearrange("p a n -> p (a n)")
                two_done(dve, o_made, it, p)
                two_done(dve, x_ready, it, p - 1)
                if p % 4 == 3:
                    nc.vector.scalar_tensor_tensor(out=tile, in0=ps_qo[:, 1, :], scalar=sb["b_out"][:, 0:1], in1=tile,
                                                   op0=ALU.add, op1=ALU.add).then_inc(x_ready, 1)
                else:
                    nc.vector.tensor_tensor(tile, ps_qo[:, 1, :], tile, ALU.add).then_inc(x_ready, 1)

            def step(it, r):
                if exists(it, r + 2):
                    maxima(it, r + 2)
                if exists(it, r + 1):
                    reciprocals(it, r + 1)
                if r % 2 == 1 and exists(it, r - 2):
                    residual(it, (r - 3) // 2)
                if exists(it, r):
                    copy_transposed(it, r)
                if r % STEPS == 1 and exists(it, r + STEPS):
                    norm_statistics(it, r // STEPS + 1)
                if r % STEPS == 3 and exists(it, r + STEPS):
                    norm_apply(it, r // STEPS + 1)

            norm_statistics(0, 0)
            norm_apply(0, 0)
            maxima(0, 0)
            maxima(0, 1)
            reciprocals(0, 0)
            run(dve, step)
            two_done(dve, x_ready, NT // 2 - 1, BODY // 2 - 1)

        @block.gpsimd
        def _(pool):
            for s in (rstd_ready, xn_ready, q_made, q_ready, s_made, max_ready, exp_ready, rsum_ready, prob_ready,
                      t_made, t_ready, o_made, y_made, y_ready, x_ready):
                pool.sem_inc(s, LEAD)
            pool.sem_inc(opened, 1)

            def normalise(it, r):
                step_done(pool, rsum_ready, it, r)
                nc.gpsimd.tensor_tensor(prob[:, r % 2, :, :], prob[:, r % 2, :, :],
                                        rsum[:, r % 2, :].unsqueeze(2).to_broadcast([P, 4, A_N]),
                                        ALU.mult).then_inc(prob_ready, 1)

            def inverse_deviation(it, q):
                pool.wait_ge(ln_steps, it * 6 + 3 * (q + 1))
                tile_done(pool, xn_ready, it, q - 1)
                nc.gpsimd.tensor_tensor(rstd[:, :], vare[:, :], sb["minus_half"][:, :], ALU.pow)\
                    .then_inc(rstd_ready, 1)

            def step(it, r):
                normalise(it, r)
                if r % STEPS == 2 and exists(it, r + STEPS):
                    inverse_deviation(it, r // STEPS + 1)
            inverse_deviation(0, 0)
            with pool.Fori(0, NT // 2 - 1) as it:
                for r in range(BODY):
                    step(it, r)
            for r in range(BODY):
                step(NT // 2 - 1, r)


GT = 4
NG = NT // GT
GN = GT * P


class Moe:

    def __init__(self, nc, name, experts, top, inner):
        self.name, self.E, self.K, self.I = name, experts, top, inner
        self.CAP = T + P
        self.NB = (T * top + experts * (P - 1)) // P + 1
        self.NB += -self.NB % 8
        self.spare = self.NB - T * top // P
        assert self.spare * P <= self.CAP
        rows = experts * self.CAP + self.spare * P
        self.rows_in = nc.dram_tensor(name + "_rows_in", (rows, H), F32, kind="Internal").ap()
        self.rows_out = nc.dram_tensor(name + "_rows_out", (self.NB * P, H), F32, kind="Internal").ap()

    def tables(self, ctx, nc):
        def sbt(name, shape, dt):
            return ctx.enter_context(nc.sbuf_tensor(self.name + name, shape, dt))
        E, K = self.E, self.K
        self.slots = sbt("_slots", [P, NT, K], F32)
        self.offset = sbt("_offset", [P, E], F32)
        self.weights = sbt("_weights", [P, NT, K], F32)
        self.chosen = sbt("_chosen", [P, NT, K], F32)
        self.iota = sbt("_iota", [P, GT * K, E], F32)
        self.region = sbt("_region", [P, GT, E], F32)
        self.total = sbt("_total", [P, E], BF16)
        self.block_expert = sbt("_block_expert", [1, self.NB], I32)
        self.block_row = sbt("_block_row", [1, self.NB], I32)
        self.pad_row = sbt("_pad_row", [1, E], I32)


TERMS = 3


def zero_operands(ph, block, nc, sb, m0):
    zeroed = ph.sem("operands_zeroed")

    @block.vector
    def _(dve):
        nc.vector.memset(sb["bias1"][:, :, :], 0.0).then_inc(zeroed, 1)
        nc.vector.memset(sb["b_down"][:, :], 0.0).then_inc(zeroed, 1)
        nc.vector.memset(sb["term_ones"][:, :], 0.0).then_inc(zeroed, 1)
        nc.vector.memset(sb["w_down0"][m0.I:P, :, :], 0.0).then_inc(zeroed, 1)
        dve.wait_ge(zeroed, 4)
        nc.vector.memset(sb["term_ones"][0:TERMS, :], 1.0).then_inc(zeroed, 1)
        dve.wait_ge(zeroed, 5)
    return zeroed


def setup_constants(ph, block, nc, ins, sb, moes, zeroed):
    m0, m1 = moes
    made = ph.sem("constants_made")
    bias_in = ph.sem("bias_loaded")
    split, spread = ph.sem("split_steps"), ph.sem("terms_written")
    rest = ph.sbuf("bias_rest", [m1.E, 2, 2 * m1.I])
    term = ph.sbuf("bias_term", [m1.E, 3, 2 * m1.I], BF16)

    @block.gpsimd
    def _(pool):
        nc.gpsimd.memset(sb["ones"][:, :], 1.0).then_inc(made, 1)
        nc.gpsimd.memset(sb["before"][:, :], 1.0).then_inc(made, 1)
        nc.gpsimd.memset(sb["upto"][:, :], 1.0).then_inc(made, 1)
        nc.gpsimd.memset(sb["zeros"][:, :], 0.0).then_inc(made, 1)
        nc.gpsimd.iota(sb["block_iota"][:, :], pattern=[[1, 256]], base=0, channel_multiplier=0,
                       allow_small_or_imprecise_dtypes=True).then_inc(made, 1)
        pool.wait_ge(made, 5)
        nc.gpsimd.affine_select(out=sb["before"][:, :], in_=sb["before"][:, :], compare_op=ALU.is_gt, fill=0.0,
                                base=0, pattern=[[1, P]], channel_multiplier=-1).then_inc(made, 1)
        nc.gpsimd.affine_select(out=sb["upto"][:, :], in_=sb["upto"][:, :], compare_op=ALU.is_ge, fill=0.0,
                                base=0, pattern=[[1, P]], channel_multiplier=-1).then_inc(made, 1)
        for m in moes:
            nc.gpsimd.iota(m.iota[:, :, :], pattern=[[0, GT * m.K], [1, m.E]], base=0, channel_multiplier=0,
                           allow_small_or_imprecise_dtypes=True).then_inc(made, 1)
            nc.gpsimd.iota(m.region[:, :, :], pattern=[[0, GT], [m.CAP, m.E]], base=0, channel_multiplier=0,
                           allow_small_or_imprecise_dtypes=True).then_inc(made, 1)
            nc.gpsimd.memset(m.total[:, :], 0.0).then_inc(made, 1)
        pool.wait_ge(made, 7 + 3 * len(moes))

    @block.vector
    def _(dve):
        dve.wait_ge(bias_in, 16)
        for n in range(TERMS):
            nc.vector.tensor_copy(term[:, n, :], rest[:, n % 2, :]).then_inc(split, 1)
            if n < TERMS - 1:
                dve.wait_ge(split, 2 * n + 1)
                nc.vector.tensor_tensor(rest[:, (n + 1) % 2, :], rest[:, n % 2, :], term[:, n, :],
                                        ALU.subtract).then_inc(split, 1)
                dve.wait_ge(split, 2 * n + 2)

    @block.sync
    def _(sp):
        sp.dma_start(rest[:, 0, :], ins["bias_gu1"]).then_inc(bias_in, 16)
        sp.wait_ge(split, 2 * TERMS - 1)
        sp.wait_ge(zeroed, 2)
        sp.dma_start(sb["b_down"][0:m1.E, :], ins["b_down1"]).then_inc(spread, 16)
        for n in range(TERMS):
            sp.dma_start(sb["bias1"][n:n + 1, :, :], term[:, n, :]).then_inc(spread, 16)
        sp.wait_ge(spread, 16 * (TERMS + 1))


def block_tables(nc, sb, m):
    E, NB = m.E, m.NB
    with ExitStack() as ctx:
        ph = Phase(ctx, nc, f"{m.name}_tables")
        count = ph.sbuf("count", [E, 4])
        count_i = ph.sbuf("count_i", [E, 1], I32)
        blocks = ph.sbuf("blocks", [E, 1])
        blocks_wide = ph.sbuf("blocks_wide", [E, P], BF16)
        below = ph.sbuf("below", [E, NB])
        row = ph.sbuf("row", [1, 3, NB])
        esum = ph.sbuf("esum", [P, NT])
        wexp = ph.sbuf("wexp", [P, NT, m.K])
        ps = ph.psum("ps_tables", [P, 4, 512])
        pe_done = ph.sem("tables_products")
        dve_done = ph.sem("tables_steps")
        act_done = ph.sem("weights_exponentials")
        tables_ready = ph.sem("tables_ready")
        padded = [ph.sem("padding_written0"), ph.sem("padding_written1")]
        block = ctx.enter_context(nc.Block())

        @block.tensor
        def _(pe):
            nc.tensor.matmul(ps[0:E, 0, 0:1], m.total[:, :], sb["ones"][:, 0:1], start=True, stop=True)
            nc.tensor.matmul(ps[0:1, 1, 0:E], sb["ones"][:, 0:1], m.total[:, :], start=True, stop=True).then_inc(pe_done, 1)
            pe.wait_ge(dve_done, 5)
            nc.tensor.matmul(ps[0:E, 2, 0:1], sb["upto"][0:E, 0:E], blocks[:, :], start=True, stop=True)
            nc.tensor.matmul(ps[:, 2, 128:128 + E], blocks_wide[:, :], sb["before"][0:E, 0:E], start=True, stop=True)\
              .then_inc(pe_done, 1)
            pe.wait_ge(dve_done, 6)
            nc.tensor.matmul(ps[0:1, 3, 0:NB], sb["onesf"][0:E, 0:1], below[:, :], start=True, stop=True)
            nc.tensor.matmul(ps[0:1, 3, 256:256 + NB], blocks[:, :], below[:, :], start=True, stop=True).then_inc(pe_done, 1)

        def pad(eng, engine_type, half):
            eng.wait_ge(tables_ready, 1)
            with eng.Fori(0, E // 8) as n:
                _, at = nc.values_load_multi_w_load_instructions(
                    m.pad_row[0:1, bass.ds(n * 8 + 4 * half, 4)], (engine_type,), min_val=0, max_val=(E - 1) * m.CAP + T,
                    skip_runtime_bounds_check_because="an expert has at most one row of each token")
                for row in at:
                    eng.dma_start(m.rows_in[bass.ds(row, P), :], sb["zeros"][:, :]).then_inc(padded[half], 16)

        @block.scalar
        def _(act):
            act.activation(wexp[:, :, :], m.weights[:, :, :], ACT.Exp).then_inc(act_done, 1)
            pad(act, mybir.EngineType.Activation, 1)

        @block.vector
        def _(dve):
            dve.wait_ge(pe_done, 1)
            nc.vector.tensor_scalar(count[:, 0:1], ps[0:E, 0, 0:1], float(P - 1), None, ALU.add).then_inc(dve_done, 1)
            nc.vector.tensor_tensor(m.pad_row[:, :], ps[0:1, 1, 0:E], m.region[0:1, 0, :], ALU.add).then_inc(tables_ready, 1)
            dve.wait_ge(dve_done, 1)
            nc.vector.tensor_copy(count_i[:, :], count[:, 0:1]).then_inc(dve_done, 1)
            dve.wait_ge(dve_done, 2)
            nc.vector.tensor_single_scalar(count_i[:, :], count_i[:, :], 7, ALU.arith_shift_right).then_inc(dve_done, 1)
            dve.wait_ge(dve_done, 3)
            nc.vector.tensor_copy(blocks[:, :], count_i[:, :]).then_inc(dve_done, 1)
            nc.vector.tensor_copy(blocks_wide[:, :], count_i[:, 0:1].to_broadcast([E, P])).then_inc(dve_done, 1)
            dve.wait_ge(pe_done, 2)
            nc.vector.tensor_copy(count[:, 1:2], ps[0:E, 2, 0:1]).then_inc(tables_ready, 1)
            dve.wait_ge(tables_ready, 2)
            nc.vector.tensor_scalar(below[:, :], sb["block_iota"][0:E, 0:NB], count[:, 1:2], None, ALU.is_ge).then_inc(dve_done, 1)
            nc.vector.scalar_tensor_tensor(out=m.offset[:, :], in0=ps[:, 2, 128:128 + E], scalar=float(P),
                                           in1=m.region[:, 0, :], op0=ALU.mult, op1=ALU.subtract)
            dve.wait_ge(act_done, 1)
            nc.vector.tensor_reduce(esum[:, :], wexp[:, :, :], AX.X, ALU.add).then_inc(dve_done, 1)
            dve.wait_ge(dve_done, 7)
            nc.vector.reciprocal(esum[:, :], esum[:, :]).then_inc(dve_done, 1)
            dve.wait_ge(dve_done, 8)
            nc.vector.tensor_tensor(m.weights[:, :, :], wexp[:, :, :], esum[:, :].unsqueeze(2).to_broadcast([P, NT, m.K]),
                                    ALU.mult).then_inc(dve_done, 1)
            dve.wait_ge(pe_done, 3)
            nc.vector.tensor_scalar(m.block_expert[:, :], ps[0:1, 3, 0:NB], float(E - 1), None, ALU.min).then_inc(dve_done, 1)
            nc.vector.tensor_scalar(row[:, 0, :], ps[0:1, 3, 0:NB], float(m.CAP), None, ALU.mult).then_inc(dve_done, 1)
            nc.vector.tensor_tensor(row[:, 1, :], sb["block_iota"][0:1, 0:NB], ps[0:1, 3, 256:256 + NB], ALU.subtract).then_inc(dve_done, 1)
            dve.wait_ge(dve_done, 12)
            nc.vector.scalar_tensor_tensor(out=m.block_row[:, :], in0=row[:, 1, :], scalar=float(P), in1=row[:, 0, :],
                                           op0=ALU.mult, op1=ALU.add).then_inc(dve_done, 1)
            dve.wait_ge(dve_done, 13)

        @block.sync
        def _(sp):
            pad(sp, mybir.EngineType.SP, 0)
            for s in padded:
                sp.wait_ge(s, 16 * (E // 2))


def experts(nc, sb, m, w_gu, w_down, bias, up_ones, activate):
    NB, I = m.NB, m.I
    BODY = 4
    NI = NB // (2 * BODY)
    with ExitStack() as ctx:
        ph = Phase(ctx, nc, f"{m.name}_experts")
        rows = ph.sbuf("rows", [P, BODY, 2, H])
        rows_t = ph.sbuf("rows_t", [P, 2, 2, KT, P])
        act_t = ph.sbuf("act_t", [P, 2, 2, P])
        work = ph.sbuf("act_work", [P, 2, 4, 2, I])
        outs = ph.sbuf("outs", [P, 2, 2, H])
        ps_x = ph.psum("ps_x", [P, 2, 2, KT, P])
        ps_gu = ph.psum("ps_gu", [P, 2, 2, H])
        ps_a = ph.psum("ps_a", [P, 512])
        ps_y = ph.psum("ps_y", [P, 2, 2, H])
        opened = ph.sem("opened")
        passed = ph.sem("passed")
        rows_loaded = [ph.sem(f"rows_loaded{n}") for n in range(BODY)]
        rows_stored = [ph.sem(f"rows_stored{n}") for n in range(2)]
        x_made, x_ready = ph.sem("x_made"), ph.sem("x_ready")
        gu_made, clipped, function_ready = ph.sem("gu_made"), ph.sem("clipped"), ph.sem("function_ready")
        steps = ph.sem("activation_steps")
        a_ready, at_made, at_ready = ph.sem("a_ready"), ph.sem("at_made"), ph.sem("at_ready")
        y_made, y_ready = ph.sem("y_made"), ph.sem("y_ready")
        act_sems = dict(gu_made=gu_made, clipped=clipped, function_ready=function_ready, steps=steps, a_ready=a_ready,
                        at_made=at_made)
        block = ctx.enter_context(nc.Block())

        LD = 4

        def done(eng, s, it, r):
            eng.wait_ge(s, it * BODY + (r + 1 + LD))

        def exists(it, r):
            return not isinstance(it, int) or 0 <= it * BODY + r < NB // 2

        def run(eng, step):
            for r in range(-2, BODY + 1):
                step(0, r)
            with eng.Fori(1, NI - 1) as it:
                for r in range(1, BODY + 1):
                    step(it, r)
            for r in range(1, BODY + 1):
                step(NI - 1, r)

        @block.sync
        def _(sp):
            top = m.E * m.CAP + (m.spare - 1) * P

            def load(it, r):
                if not (isinstance(it, int) and it * BODY + r < BODY):
                    done(sp, x_made, it, r - BODY)
                    sp.sem_inc(passed, 1)
                _, at = nc.values_load_multi_w_load_instructions(
                    m.block_row[0:1, bass.ds(it * (2 * BODY) + 2 * r, 2)], (mybir.EngineType.SP,), min_val=0,
                    max_val=top, skip_runtime_bounds_check_because="block_tables makes rows of whole blocks")
                for b in range(2):
                    sp.dma_start(rows[:, r % BODY, b, :], m.rows_in[bass.ds(at[b], P), :]).then_inc(rows_loaded[r % BODY], 16)

            for r in range(BODY):
                load(0, r)
            with sp.Fori(0, NI - 1) as it:
                for r in range(BODY):
                    load(it, r + BODY)

        @block.tensor
        def _(pe):
            pe.wait_ge(opened, 1)
            loaded = {}

            def experts_of(it, r):
                first = r // 2 * 2
                if (str(it), first) not in loaded:
                    _, loaded[str(it), first] = nc.values_load_multi_w_load_instructions(
                        m.block_expert[0:1, bass.ds(it * (2 * BODY) + 2 * first, 4)], (mybir.EngineType.PE,), min_val=0,
                        max_val=m.E - 1, skip_runtime_bounds_check_because="block_tables bounds it by the last expert")
                return loaded[str(it), first][2 * (r - first):2 * (r - first) + 2]

            def step(it, r):
                if exists(it, r + 2):
                    q = r + 2
                    pe.wait_ge(rows_loaded[q % BODY], it * 32 + 32 * (q // BODY + 1))
                    done(pe, x_ready, it, q - 2)
                    for b in range(2):
                        for kt in range(KT):
                            last = nc.tensor.transpose(ps_x[:, q % 2, b, kt, :], rows[:, q % BODY, b, kt * P:(kt + 1) * P],
                                                       sb["ident"][:, :])
                    last.then_inc(x_made, 1)
                if exists(it, r + 1):
                    q = r + 1
                    e = experts_of(it, q)
                    done(pe, x_ready, it, q)
                    done(pe, a_ready, it, q - 2)
                    for b in range(2):
                        out = ps_gu[:, q % 2, b, 0:2 * I]
                        for kt in range(KT):
                            last = nc.tensor.matmul(out, rows_t[:, q % 2, b, kt, :],
                                                    w_gu[:, bass.ds(e[b], 1), kt, :].rearrange("p a n -> p (a n)"),
                                                    start=(kt == 0), stop=(kt == KT - 1 and bias is None))
                        if bias is not None:
                            last = nc.tensor.matmul(out, up_ones[:, :],
                                                    bias[:, bass.ds(e[b], 1), :].rearrange("p a n -> p (a n)"),
                                                    start=False, stop=True)
                    last.then_inc(gu_made, 1)
                if exists(it, r):
                    done(pe, a_ready, it, r)
                    done(pe, at_ready, it, r - 1)
                    pe.sem_inc(passed, 1)
                    for b in range(2):
                        last = nc.tensor.transpose(ps_a[0:I, b * P:(b + 1) * P], work[:, r % 2, 3, b, :], sb["ident"][:, :])
                    last.then_inc(at_made, 1)
                if exists(it, r - 1):
                    q = r - 1
                    e = experts_of(it, q)
                    done(pe, at_ready, it, q)
                    done(pe, y_ready, it, q - 2)
                    for b in range(2):
                        last = nc.tensor.matmul(ps_y[:, q % 2, b, :], act_t[:, q % 2, b, :],
                                                w_down[:, bass.ds(e[b], 1), :].rearrange("p a n -> p (a n)"),
                                                start=True, stop=True)
                    last.then_inc(y_made, 1)
            run(pe, step)

        @block.scalar
        def _(act):
            act.wait_ge(opened, 1)

            def step(it, r):
                if exists(it, r + 2):
                    q = r + 2
                    done(act, x_made, it, q)
                    done(act, gu_made, it, q - 2)
                    nc.scalar.activation(rows_t[:, q % 2, :, :, :], ps_x[:, q % 2, :, :, :], ACT.Copy).then_inc(x_ready, 1)
                if exists(it, r + 1):
                    activate.function(nc, act, done, it, r + 1, ps_gu, work, act_sems)
                if exists(it, r):
                    done(act, at_made, it, r)
                    done(act, y_made, it, r - 2)
                    nc.scalar.activation(act_t[0:I, r % 2, :, :], ps_a[0:I, 0:2 * P].rearrange("p (b t) -> p b t", b=2),
                                         ACT.Copy).then_inc(at_ready, 1)
            run(act, step)

        @block.vector
        def _(dve):
            dve.wait_ge(opened, 1)

            def step(it, r):
                def copy_out():
                    if exists(it, r - 1):
                        q = r - 1
                        done(dve, y_made, it, q)
                        if not (isinstance(it, int) and it * BODY + q < 2):
                            dve.wait_ge(rows_stored[q % 2], it * (8 * BODY) + 16 * (q // 2))
                        nc.vector.tensor_copy(outs[:, q % 2, :, :], ps_y[:, q % 2, :, :]).then_inc(y_ready, 1)
                if exists(it, r + 1):
                    activate.product(nc, dve, done, it, r + 1, ps_gu, work, act_sems, BODY, copy_out)
                else:
                    copy_out()
            if I < P:
                nc.vector.memset(act_t[I:P, :, :, :], 0.0).then_inc(steps, 1)
                dve.wait_ge(steps, 1)
            dve.sem_inc(at_ready, LD)
            run(dve, step)

        @block.gpsimd
        def _(pool):
            for s in (x_made, x_ready, gu_made, clipped, function_ready, a_ready, at_made, y_made, y_ready):
                pool.sem_inc(s, LD)
            pool.sem_inc(opened, 1)

            def store(it, r):
                done(pool, y_ready, it, r)
                pool.sem_inc(passed, 1)
                pool.dma_start(m.rows_out[bass.ds((it * BODY + r) * (2 * P), 2 * P), :].rearrange("(b p) n -> p b n", b=2),
                               outs[:, r % 2, :, :]).then_inc(rows_stored[r % 2], 16)
            with pool.Fori(0, NI) as it:
                for r in range(BODY):
                    store(it, r)
            for n in range(2):
                pool.wait_ge(rows_stored[n], 16 * (NB // 4))


class Swish:

    @staticmethod
    def function(nc, act, done, it, q, ps_gu, work, s):
        I = work.shape[4]
        done(act, s["gu_made"], it, q)
        done(act, s["a_ready"], it, q - 2)
        nc.scalar.activation(work[:, q % 2, 0, :, :], ps_gu[:, q % 2, :, 0:I], ACT.Silu).then_inc(s["function_ready"], 1)

    @staticmethod
    def product(nc, dve, done, it, q, ps_gu, work, s, body, between):
        I = work.shape[4]
        between()
        done(dve, s["function_ready"], it, q)
        done(dve, s["at_made"], it, q - 2)
        nc.vector.tensor_tensor(work[:, q % 2, 3, :, :], work[:, q % 2, 0, :, :], ps_gu[:, q % 2, :, I:2 * I], ALU.mult)\
            .then_inc(s["a_ready"], 1)


class ClippedSwish:
    ALPHA, LIMIT = 1.702, 7.0

    @staticmethod
    def function(nc, act, done, it, q, ps_gu, work, s):
        done(act, s["clipped"], it, q)
        nc.scalar.activation(work[:, q % 2, 0, :, :], work[:, q % 2, 1, :, :], ACT.Sigmoid, scale=ClippedSwish.ALPHA)\
            .then_inc(s["function_ready"], 1)

    @staticmethod
    def product(nc, dve, done, it, q, ps_gu, work, s, body, between):
        I = work.shape[4]
        L = ClippedSwish.LIMIT
        steps = s["steps"]
        done(dve, s["gu_made"], it, q)
        nc.vector.tensor_scalar(work[:, q % 2, 1, :, :], ps_gu[:, q % 2, :, 0:I], L, None, ALU.min).then_inc(s["clipped"], 1)
        nc.vector.tensor_scalar(work[:, q % 2, 2, :, :], ps_gu[:, q % 2, :, I:2 * I], L, -L, ALU.min, ALU.max).then_inc(steps, 1)
        between()
        dve.wait_ge(steps, it * 2 * body + (2 * q + 1))
        done(dve, s["clipped"], it, q)
        nc.vector.scalar_tensor_tensor(out=work[:, q % 2, 2, :, :], in0=work[:, q % 2, 2, :, :], scalar=1.0,
                                       in1=work[:, q % 2, 1, :, :], op0=ALU.add, op1=ALU.mult).then_inc(steps, 1)
        dve.wait_ge(steps, it * 2 * body + (2 * q + 2))
        done(dve, s["function_ready"], it, q)
        done(dve, s["at_made"], it, q - 2)
        nc.vector.tensor_tensor(work[:, q % 2, 3, :, :], work[:, q % 2, 0, :, :], work[:, q % 2, 2, :, :], ALU.mult)\
            .then_inc(s["a_ready"], 1)


class Routing:

    def __init__(self, ctx, nc, sb, m, wg, bias):
        ph = Phase(ctx, nc, f"{m.name}_routing")
        E, K = m.E, m.K
        self.nc, self.sb, self.m, self.wg, self.bias = nc, sb, m, wg, bias
        self.W = wg.shape[2]
        self.logits = ph.sbuf("logits", [P, GT, self.W])
        self.top = ph.sbuf("top", [P, GT, 8])
        self.index = ph.sbuf("index", [P, GT, 8], mybir.dt.uint32)
        self.chosen = ph.sbuf("group_chosen", [P, GT * K])
        self.onehot = ph.sbuf("onehot", [P, GT * K, E])
        self.mask = ph.sbuf("mask", [P, GT, E], BF16)
        self.added = ph.sbuf("added", [P, E])
        self.place = ph.sbuf("place", [P, GT, E])
        self.picked = ph.sbuf("picked", [P, GT * K, E])
        self.slots = ph.sbuf("group_slots", [P, 2, GT * K], I32)
        self.ps = ph.psum("ps_logits", [P, 512])
        self.slots_f = ph.sbuf("group_slots_f", [P, GT * K])
        self.logits_made = ph.sem("logits_made")
        self.logits_ready = ph.sem("logits_ready")
        self.mask_ready = ph.sem("mask_ready")
        self.ranks_made = ph.sem("ranks_made")
        self.place_ready = ph.sem("place_ready")
        self.slots_ready = ph.sem("slots_ready")
        self.steps = ph.sem("routing_steps")
        self.scattered = [ph.sem("scattered0"), ph.sem("scattered1")]
        self.rows_sent = ph.sem("rows_sent")

    STEPS = 9

    def step_done(self, dve, it, q, n):
        dve.wait_ge(self.steps, it * (2 * self.STEPS) + (self.STEPS * q + n))

    def make_logits(self, pe, it, q, xt, done):
        done(pe, self.place_ready, it, q - 1)
        for j in range(GT):
            for kt in range(KT):
                last = self.nc.tensor.matmul(self.ps[:, j * self.W:(j + 1) * self.W], xt[:, kt, j * P:(j + 1) * P],
                                             self.wg[:, kt, :], start=(kt == 0), stop=(kt == KT - 1))
        last.then_inc(self.logits_made, 1)

    def choose(self, dve, it, q, done):
        nc, m, K, E = self.nc, self.m, self.m.K, self.m.E
        done(dve, self.logits_made, it, q)
        ps = self.ps[:, 0:GT * self.W].rearrange("p (j e) -> p j e", j=GT)
        if self.bias is None:
            nc.vector.tensor_copy(self.logits[:, :, :], ps).then_inc(self.logits_ready, 1)
        else:
            nc.vector.tensor_tensor(self.logits[:, :, :], ps, self.bias[:, :].unsqueeze(1).to_broadcast([P, GT, E]),
                                    ALU.add).then_inc(self.logits_ready, 1)
        done(dve, self.logits_ready, it, q)
        dve.sem_inc(self.passed, 1)
        for j in range(GT):
            last = nc.vector.max(self.top[:, j, :], self.logits[:, j, 0:E])
        last.then_inc(self.steps, 1)
        self.step_done(dve, it, q, 1)
        dve.sem_inc(self.passed, 1)
        for j in range(GT):
            last = nc.vector.max_index(self.index[:, j, :], self.top[:, j, :], self.logits[:, j, 0:E])
        last.then_inc(self.steps, 1)
        nc.vector.tensor_tensor(m.weights[:, bass.ds((it * 2 + q) * GT, GT), :], self.top[:, :, 0:K],
                                self.top[:, :, 0:1].to_broadcast([P, GT, K]), ALU.subtract).then_inc(self.steps, 1)
        self.step_done(dve, it, q, 2)
        nc.vector.tensor_copy(self.chosen[:, :].rearrange("p (j k) -> p j k", j=GT), self.index[:, :, 0:K])\
            .then_inc(self.steps, 1)
        self.step_done(dve, it, q, 4)
        nc.vector.tensor_copy(m.chosen[:, bass.ds((it * 2 + q) * GT, GT), :],
                              self.chosen[:, :].rearrange("p (j k) -> p j k", j=GT)).then_inc(self.steps, 1)
        nc.vector.tensor_tensor(self.onehot[:, :, :], m.iota[:, :, :],
                                self.chosen[:, :].unsqueeze(2).to_broadcast([P, GT * K, E]), ALU.is_equal)\
            .then_inc(self.steps, 1)
        self.step_done(dve, it, q, 6)
        done(dve, self.ranks_made, it, q - 1)
        with nc.allow_low_precision("a mask of zeros and ones"):
            nc.vector.tensor_reduce(self.mask[:, :, :],
                                    self.onehot[:, :, :].rearrange("p (j k) e -> p j e k", j=GT), AX.X, ALU.add)\
                .then_inc(self.mask_ready, 1)

    def make_ranks(self, pe, it, q, done):
        nc, sb, m, E = self.nc, self.sb, self.m, self.m.E
        done(pe, self.mask_ready, it, q)
        for j in range(GT):
            out = self.ps[:, j * E:(j + 1) * E]
            nc.tensor.matmul(out, sb["before"][:, :], self.mask[:, j, :], start=True, stop=False)
            for i in range(j):
                nc.tensor.matmul(out, sb["ones"][:, :], self.mask[:, i, :], start=False, stop=False)
            last = nc.tensor.matmul(out, sb["ones"][:, :], m.total[:, :], start=False, stop=True)
        last.then_inc(self.ranks_made, 1)

    def place_rows(self, dve, it, q, done):
        nc, m, K, E = self.nc, self.m, self.m.K, self.m.E
        done(dve, self.ranks_made, it, q)
        nc.vector.tensor_tensor(self.place[:, :, :], self.ps[:, 0:GT * E].rearrange("p (j e) -> p j e", j=GT),
                                m.region[:, :, :], ALU.add).then_inc(self.place_ready, 1)
        nc.vector.tensor_reduce(self.added[:, :], self.mask[:, :, :].rearrange("p j e -> p e j"), AX.X, ALU.add)\
            .then_inc(self.steps, 1)
        self.step_done(dve, it, q, 7)
        with nc.allow_low_precision("counts up to 32"):
            nc.vector.tensor_tensor(m.total[:, :], m.total[:, :], self.added[:, :], ALU.add)
        done(dve, self.place_ready, it, q)
        nc.vector.tensor_tensor(self.picked[:, :, :].rearrange("p (j k) e -> p j k e", j=GT),
                                self.onehot[:, :, :].rearrange("p (j k) e -> p j k e", j=GT),
                                self.place[:, :, :].unsqueeze(2).to_broadcast([P, GT, K, E]), ALU.mult)\
            .then_inc(self.steps, 1)
        self.step_done(dve, it, q, 8)
        done(dve, self.rows_sent, it, q - 2)
        nc.vector.tensor_reduce(self.slots_f[:, :], self.picked[:, :, :], AX.X, ALU.add).then_inc(self.steps, 1)
        self.step_done(dve, it, q, 9)
        nc.vector.tensor_copy(self.slots[:, q % 2, :], self.slots_f[:, :]).then_inc(self.slots_ready, 1)
        nc.vector.tensor_copy(m.slots[:, bass.ds((it * 2 + q) * GT, GT), :],
                              self.slots_f[:, :].rearrange("p (j k) -> p j k", j=GT))

    def scatter(self, pool, it, q, xn, tiles, done):
        K = self.m.K
        done(pool, self.slots_ready, it, q)
        pool.sem_inc(self.passed, 1)
        for j in tiles:
            for k in range(K):
                n = j * K + k
                pool.indirect_dma_start(self.m.rows_in, bass.IndirectOffsetOnAxis(ap=self.slots[:, q % 2, n:n + 1], axis=0),
                                        xn[:, j, :], None).then_inc(self.scattered[q % 2], 16)

    def mark_sent(self, pool, it, q):
        n = 16 * GT * self.m.K
        pool.wait_ge(self.scattered[q % 2], it * n + n * (q // 2 + 1))
        pool.sem_inc(self.rows_sent, 1)

    def start(self, pool, lead):
        for s in (self.logits_made, self.logits_ready, self.mask_ready, self.ranks_made, self.place_ready,
                  self.slots_ready):
            pool.sem_inc(s, lead)
        pool.sem_inc(self.rows_sent, lead)


def shared_expert(nc, sb, m, w):
    with ExitStack() as ctx:
        ph = Phase(ctx, nc, "shared")
        x_sb = sb["x"]
        stats = ph.sbuf("stats", [P, GT, 6])
        mv = ph.sbuf("mean_var", [P, GT, 2])
        vare = ph.sbuf("var_eps", [P, GT])
        rstd = ph.sbuf("rstd", [P, GT])
        xn = ph.sbuf("xn", [P, 2, GT, H])
        xt = ph.sbuf("xt", [P, 2, KT, GN])
        silu = ph.sbuf("silu", [P, 2, GN])
        hidden = ph.sbuf("hidden", [P, 2, 2, GN])
        sg = ph.sbuf("sg", [P, GT])
        ps_x = ph.psum("ps_x", [P, KT, GN])
        ps_gu = ph.psum("ps_gu", [P, 2, 2, GN])
        ps_o = ph.psum("ps_o", [P, 2, H])
        rt = Routing(ctx, nc, sb, m, w["gate"], None)
        opened, passed = ph.sem("opened"), ph.sem("passed")
        rt.passed = passed
        norm_steps = ph.sem("norm_steps")
        rstd_ready, xn_ready = ph.sem("rstd_ready"), ph.sem("xn_ready")
        xt_made, xt_ready = ph.sem("xt_made"), ph.sem("xt_ready")
        gu_made = [ph.sem("gu_made0"), ph.sem("gu_made1")]
        silu_ready = [ph.sem("silu_ready0"), ph.sem("silu_ready1")]
        h_ready = [ph.sem("h_ready0"), ph.sem("h_ready1")]
        sg_ready = ph.sem("sg_ready")
        o_made = [ph.sem("o_made0"), ph.sem("o_made1")]
        x_ready = [ph.sem("x_ready0"), ph.sem("x_ready1")]
        block = ctx.enter_context(nc.Block())

        def done(eng, s, it, q):
            eng.wait_ge(s, it * 2 + (q + 1 + LEAD))

        def exists(it, q):
            return not isinstance(it, int) or it * 2 + q < NG

        @block.tensor
        def _(pe):
            pe.wait_ge(opened, 1)

            def transposes(it, q):
                done(pe, xn_ready, it, q)
                done(pe, xt_ready, it, q - 1)
                for j in range(GT):
                    for kt in range(KT):
                        last = nc.tensor.transpose(ps_x[:, kt, j * P:(j + 1) * P], xn[:, q % 2, j, kt * P:(kt + 1) * P],
                                                   sb["ident"][:, :])
                last.then_inc(xt_made, 1)

            def gate_up_half(it, q, f):
                done(pe, h_ready[f], it, q - 1)
                if f == 0:
                    done(pe, x_ready[1], it, q - 1)
                for u in range(2):
                    for kt in range(KT):
                        last = nc.tensor.matmul(ps_gu[:, f, u, :], w["shared_in"][:, u, kt, f * P:(f + 1) * P],
                                                xt[:, q % 2, kt, :], start=(kt == 0), stop=(kt == KT - 1))
                last.then_inc(gu_made[f], 1)

            def down(it, q, pair):
                if pair == 0:
                    for f in range(2):
                        done(pe, h_ready[f], it, q)
                    done(pe, x_ready[0], it, q - 1)
                out = ps_o if pair == 0 else ps_gu[:, 0, 0, :].rearrange("p (j n) -> p j n", j=2)
                for j in range(2):
                    for f in range(2):
                        t = 2 * pair + j
                        last = nc.tensor.matmul(out[:, j, :], hidden[:, q % 2, f, t * P:(t + 1) * P], w["shared_out"][:, f, :],
                                                start=(f == 0), stop=(f == 1))
                last.then_inc(o_made[pair], 1)

            def step(it, q):
                done(pe, xt_ready, it, q)
                rt.make_logits(pe, it, q, xt[:, q % 2, :, :], done)
                gate_up_half(it, q, 0)
                gate_up_half(it, q, 1)
                rt.make_ranks(pe, it, q, done)
                if exists(it, q + 1):
                    transposes(it, q + 1)
                down(it, q, 0)
                down(it, q, 1)
            transposes(0, 0)
            with pe.Fori(0, NG // 2 - 1) as it:
                for q in range(2):
                    step(it, q)
            for q in range(2):
                step(NG // 2 - 1, q)

        @block.scalar
        def _(act):
            act.wait_ge(opened, 1)

            def copy_xt(it, q):
                done(act, xt_made, it, q)
                done(act, gu_made[1], it, q - 2)
                for kt in range(KT):
                    last = nc.scalar.activation(xt[:, q % 2, kt, :], ps_x[:, kt, :], ACT.Copy)
                last.then_inc(xt_ready, 1)

            def step(it, q):
                done(act, rt.logits_ready, it, q)
                done(act, x_ready[1], it, q - 1)
                nc.scalar.activation(sg[:, :], rt.logits[:, :, m.E], ACT.Sigmoid).then_inc(sg_ready, 1)
                for f in range(2):
                    done(act, gu_made[f], it, q)
                    done(act, h_ready[f], it, q - 1)
                    nc.scalar.activation(silu[:, f, :], ps_gu[:, f, 0, :], ACT.Silu).then_inc(silu_ready[f], 1)
                if exists(it, q + 1):
                    copy_xt(it, q + 1)
            copy_xt(0, 0)
            with act.Fori(0, NG // 2 - 1) as it:
                for q in range(2):
                    step(it, q)
            for q in range(2):
                step(NG // 2 - 1, q)

        @block.vector
        def _(dve):
            dve.wait_ge(opened, 1)

            def apply(it, q):
                def free():
                    done(dve, xt_made, it, q - 2)
                    done(dve, rt.rows_sent, it, q - 2)
                norm_apply(nc, dve, x_sb, it, q, mv, rstd, xn[:, q % 2, :, :], rstd_ready, xn_ready, done, free)

            def step(it, q):
                if exists(it, q + 1):
                    norm_statistics(nc, dve, x_sb, it, q + 1, stats, mv, vare, norm_steps, passed)
                rt.choose(dve, it, q, done)
                if exists(it, q + 1):
                    apply(it, q + 1)
                for f in range(2):
                    done(dve, silu_ready[f], it, q)
                    if f == 0:
                        done(dve, o_made[1], it, q - 2)
                    nc.vector.tensor_tensor(hidden[:, q % 2, f, :], silu[:, f, :], ps_gu[:, f, 1, :], ALU.mult)\
                        .then_inc(h_ready[f], 1)
                rt.place_rows(dve, it, q, done)
                done(dve, sg_ready, it, q)
                for pair in range(2):
                    done(dve, o_made[pair], it, q)
                    out = ps_o if pair == 0 else ps_gu[:, 0, 0, :].rearrange("p (j n) -> p j n", j=2)
                    for j in range(2):
                        t = 2 * pair + j
                        tile = x_sb[:, bass.ds((it * 2 + q) * GT + t, 1), :].rearrange("p a n -> p (a n)")
                        last = nc.vector.scalar_tensor_tensor(out=tile, in0=out[:, j, :], scalar=sg[:, t:t + 1], in1=tile,
                                                              op0=ALU.mult, op1=ALU.add)
                    last.then_inc(x_ready[pair], 1)
            norm_statistics(nc, dve, x_sb, 0, 0, stats, mv, vare, norm_steps, passed)
            apply(0, 0)
            with dve.Fori(0, NG // 2 - 1) as it:
                for q in range(2):
                    step(it, q)
            for q in range(2):
                step(NG // 2 - 1, q)
            done(dve, x_ready[1], NG // 2 - 1, 1)

        @block.gpsimd
        def _(pool):
            for s in (rstd_ready, xn_ready, xt_made, xt_ready, *gu_made, *silu_ready, *h_ready, 
                      sg_ready, *o_made, *x_ready):
                pool.sem_inc(s, LEAD)
            rt.start(pool, LEAD)
            pool.sem_inc(opened, 1)

            def step(it, q):
                if exists(it, q + 1):
                    norm_deviation(nc, pool, sb, it, q + 1, vare, rstd, norm_steps, xn_ready, rstd_ready, done)
                if exists(it, q) and not (isinstance(it, int) and it * 2 + q == 0):
                    rt.mark_sent(pool, it, q - 1)
                rt.scatter(pool, it, q, xn[:, q % 2, :, :], range(GT), done)
            norm_deviation(nc, pool, sb, 0, 0, vare, rstd, norm_steps, xn_ready, rstd_ready, done)
            for q in range(2):
                step(0, q)
            with pool.Fori(1, NG // 2 - 1) as it:
                for q in range(2):
                    step(it, q)
            for q in range(2):
                step(NG // 2 - 1, q)
            rt.mark_sent(pool, NG // 2 - 1, 1)


def norm_statistics(nc, dve, x_sb, it, q, stats, mv, vare, norm_steps, passed):
    base = it * 6 + 3 * q
    for j in range(GT):
        last = nc.vector.bn_stats(stats[:, j, :], x_sb[:, bass.ds((it * 2 + q) * GT + j, 1), :].rearrange("p a n -> p (a n)"))
    last.then_inc(norm_steps, 1)
    dve.wait_ge(norm_steps, base + 1)
    dve.sem_inc(passed, 1)
    for j in range(GT):
        last = nc.vector.bn_aggr(mv[:, j, :], stats[:, j, :])
    last.then_inc(norm_steps, 1)
    dve.wait_ge(norm_steps, base + 2)
    nc.vector.tensor_scalar(vare[:, :], mv[:, :, 1], EPS, None, ALU.add).then_inc(norm_steps, 1)


def norm_deviation(nc, pool, sb, it, q, vare, rstd, norm_steps, xn_ready, rstd_ready, done):
    pool.wait_ge(norm_steps, it * 6 + 3 * (q + 1))
    done(pool, xn_ready, it, q - 1)
    nc.gpsimd.tensor_tensor(rstd[:, :], vare[:, :], sb["minus_half"][:, 0:1].to_broadcast([P, GT]), ALU.pow)\
        .then_inc(rstd_ready, 1)


def norm_apply(nc, dve, x_sb, it, q, mv, rstd, xn, rstd_ready, xn_ready, done, free):
    done(dve, rstd_ready, it, q)
    free()
    for j in range(GT):
        last = nc.vector.tensor_scalar(xn[:, j, :],
                                       x_sb[:, bass.ds((it * 2 + q) * GT + j, 1), :].rearrange("p a n -> p (a n)"),
                                       mv[:, j, 0:1], rstd[:, j:j + 1], ALU.subtract, ALU.mult)
    last.then_inc(xn_ready, 1)


class SlotFinder:

    def __init__(self, ph, nc, m):
        self.nc, self.m = nc, m
        self.onehot = ph.sbuf("onehot", [P, GT * m.K, m.E])
        self.picked = ph.sbuf("picked", [P, GT * m.K, m.E])
        self.shift = ph.sbuf("shift", [P, GT, m.K])
        self.steps = ph.sem("finder_steps")

    def rows(self, dve, it, q, slots, staged):
        nc, m = self.nc, self.m
        group = bass.ds((it * 2 + q) * GT, GT)
        base = it * 6 + 3 * q
        nc.vector.tensor_tensor(self.onehot[:, :, :].rearrange("p (j k) e -> p j k e", j=GT),
                                m.iota[:, :, :].rearrange("p (j k) e -> p j k e", j=GT),
                                m.chosen[:, group, :].unsqueeze(3).to_broadcast([P, GT, m.K, m.E]), ALU.is_equal)\
            .then_inc(self.steps, 1)
        dve.wait_ge(self.steps, base + 1)
        nc.vector.tensor_tensor(self.picked[:, :, :], self.onehot[:, :, :],
                                m.offset[:, :].unsqueeze(1).to_broadcast([P, GT * m.K, m.E]), ALU.mult)\
            .then_inc(self.steps, 1)
        dve.wait_ge(self.steps, base + 2)
        nc.vector.tensor_reduce(self.shift[:, :, :].rearrange("p j k -> p (j k)"), self.picked[:, :, :], AX.X, ALU.add)\
            .then_inc(self.steps, 1)
        dve.wait_ge(self.steps, base + 3)
        nc.vector.tensor_tensor(slots[:, q % 2, :].rearrange("p (j k) -> p j k", j=GT), self.shift[:, :, :],
                                m.slots[:, group, :], ALU.add).then_inc(staged, 1)


def combine0(nc, sb, m):
    K = m.K
    with ExitStack() as ctx:
        ph = Phase(ctx, nc, "combine0")
        slots = ph.sbuf("slots_now", [P, 2, GT * K], I32)
        weights = ph.sbuf("weights_now", [P, 2, GT * K])
        got = ph.sbuf("rows_got", [P, GT, K, H])
        acc = ph.sbuf("acc", [P, GT, 2, H])
        find = SlotFinder(ph, nc, m)
        opened, passed = ph.sem("opened"), ph.sem("passed")
        staged, steps, used = ph.sem("slots_staged"), ph.sem("sum_steps"), ph.sem("rows_used")
        gathered = [ph.sem(f"gathered{j}") for j in range(GT)]
        block = ctx.enter_context(nc.Block())

        @block.gpsimd
        def _(pool):
            with pool.Fori(0, NG // 2) as it:
                for q in range(2):
                    pool.wait_ge(staged, it * 2 + (q + 1))
                    for j in range(GT):
                        pool.wait_ge(used, it * (2 * GT) + (q * GT + j + 1))
                        pool.sem_inc(passed, 1)
                        for k in range(K):
                            n = j * K + k
                            pool.indirect_dma_start(got[:, j, k, :], None, m.rows_out,
                                                    bass.IndirectOffsetOnAxis(ap=slots[:, q, n:n + 1], axis=0))\
                                .then_inc(gathered[j], 16)

        @block.vector
        def _(dve):
            dve.sem_inc(used, GT)

            def stage(it, q):
                if not (isinstance(it, int) and it * 2 + q == 0):
                    dve.wait_ge(used, it * (2 * GT) + q * GT)
                nc.vector.tensor_copy(weights[:, q % 2, :].rearrange("p (j k) -> p j k", j=GT),
                                      m.weights[:, bass.ds((it * 2 + q) * GT, GT), :])
                find.rows(dve, it, q, slots, staged)

            def tile(it, q, j):
                x = sb["x"][:, bass.ds((it * 2 + q) * GT + j, 1), :].rearrange("p a n -> p (a n)")
                if j == 0:
                    dve.wait_ge(staged, it * 2 + (q + 1))
                dve.wait_ge(gathered[j], it * (32 * K) + 16 * K * (q + 1))
                dve.wait_ge(used, it * (2 * GT) + (q * GT + j + 1))
                base = it * (2 * GT * (K - 1)) + (q * GT + j) * (K - 1)
                for k in range(K):
                    into = x if k == K - 1 else acc[:, j, k % 2, :]
                    add = x if k == 0 else acc[:, j, (k - 1) % 2, :]
                    if k > 0:
                        dve.wait_ge(steps, base + k)
                    nc.vector.scalar_tensor_tensor(out=into, in0=got[:, j, k, :],
                                                   scalar=weights[:, q % 2, j * K + k:j * K + k + 1], in1=add,
                                                   op0=ALU.mult, op1=ALU.add).then_inc(used if k == K - 1 else steps, 1)
            stage(0, 0)
            with dve.Fori(0, NG // 2 - 1) as it:
                for q in range(2):
                    stage(it, q + 1)
                    for j in range(GT):
                        tile(it, q, j)
            for q in range(2):
                if q == 0:
                    stage(NG // 2 - 1, 1)
                for j in range(GT):
                    tile(NG // 2 - 1, q, j)
            dve.wait_ge(used, NT + GT)


C_HEADS = 16
C_DH = H // C_HEADS
C_HALF = C_HEADS // KT
VW = C_DH + 1


def attention1(nc, ins, sb, m, w, region, later, later_written):
    with ExitStack() as ctx:
        ph = Phase(ctx, nc, "attn1")
        x_sb, ident = sb["x"], sb["ident"]
        stats_a, mv_a = ph.sbuf("stats_a", [P, GT, 6]), ph.sbuf("mv_a", [P, GT, 2])
        vare_a, rstd_a = ph.sbuf("vare_a", [P, GT]), ph.sbuf("rstd_a", [P, GT])
        stats_f, mv_f = ph.sbuf("stats_f", [P, GT, 6]), ph.sbuf("mv_f", [P, GT, 2])
        vare_f, rstd_f = ph.sbuf("vare_f", [P, GT]), ph.sbuf("rstd_f", [P, GT])
        stats_d, mv_d = ph.sbuf("stats_d", [P, 2, 6]), ph.sbuf("mv_d", [P, 2, 2])
        vare_d, rstd_d = ph.sbuf("vare_d", [P, 2]), ph.sbuf("rstd_d", [P, 2])
        xa = region[:, 30:32, :, :].rearrange("p j a n -> p (j a) n")
        xf = ph.sbuf("xf", [P, 2, GT, H])
        xt = region[:, 26:28, :, :].rearrange("p k a n -> p k (a n)")
        xft = ph.sbuf("xft", [P, KT, GN])
        ct = region[:, 0:4, :, :].rearrange("p (i k) a n -> p i k (a n)", i=2)
        q_t = region[:, 4:8, :, :].rearrange("p (i k) a n -> p i k (a n)", i=2)
        k_t = region[:, 8:12, :, :].rearrange("p (i k) a n -> p i k (a n)", i=2)
        q_bd = region[:, 12:20, :, :].rearrange("p (i f b) a (c s) -> p i f b (a c) s", i=2, f=KT, s=S)
        v_bd = ph.sbuf("v_bd", [P, 4, C_HEADS, 2, VW])
        clipped = region[:, 20:22, :, :].rearrange("p f a n -> p f (a n)")
        probs = region[:, 22:26, :, :].rearrange("p (i f) a n -> p i f (a n)", i=2)
        rsum = ph.sbuf("rsum", [P, C_HALF, 2])
        heads = ph.sbuf("heads", [P, 2, C_HALF, C_DH])
        ctx_t = ph.sbuf("ctx_t", [P, KT, 2, S])
        delta = ph.sbuf("delta", [P, 2, H])
        scaled = ph.sbuf("scaled", [P, H])
        xb = ph.sbuf("xb", [P, 2, H])
        ps_x = ph.psum("ps_x", [P, KT, GN])
        ps_q = ph.psum("ps_q", [P, GN])
        ps_s = ph.psum("ps_s", [P, KT, 512])
        ps_pv = ph.psum("ps_pv", [P, 512])
        ps_c = ph.psum("ps_c", [P, 512])
        rt = Routing(ctx, nc, sb, m, w["gate"], w["gate_b"])
        opened, passed = ph.sem("opened"), ph.sem("passed")
        rt.passed = passed
        loaded = [ph.sem("ct_loaded0"), ph.sem("ct_loaded1")]
        steps_a, steps_f, steps_d = ph.sem("norm_steps_a"), ph.sem("norm_steps_f"), ph.sem("norm_steps_d")
        rstd_a_ready, xa_ready, xa_t_made, xt_ready = (ph.sem(n) for n in ("rstd_a", "xa_ready", "xa_t_made", "xt_ready"))
        rstd_f_ready, xf_ready, xf_t_made, xft_ready = (ph.sem(n) for n in ("rstd_f", "xf_ready", "xf_t_made", "xft_ready"))
        by_group = [rstd_a_ready, xa_ready, xa_t_made, xt_ready, rstd_f_ready, xf_ready, xf_t_made, xft_ready]
        names = ("qbd0_ready", "qbd1_ready", "s_made", "clip_ready", "exp_ready", "pv_made", "rsum_ready",
                 "heads_ready", "ct_made", "ct_copied", "y_made", "delta_ready", "rstd_d", "xb_ready", "scaled_ready",
                 "x_ready")
        by_tile = {n: ph.sem(n) for n in names}
        (qbd0_ready, qbd1_ready, s_made, clip_ready, exp_ready, pv_made, rsum_ready, heads_ready, ct_made,
         ct_copied, y_made, delta_ready, rstd_d_ready, xb_ready, scaled_ready, x_ready) = by_tile.values()
        bank_made, bank_free = ph.sem("bank_made"), ph.sem("bank_free")
        USES = 8
        prepared = ph.sem("prepared")
        masks_now = ph.sbuf("masks_now", [P, 4, 2])
        LG, LT = 4, 4
        BODY = 2 * GT
        block = ctx.enter_context(nc.Block())

        def gdone(eng, s, it, q):
            eng.wait_ge(s, it * 2 + (q + 1 + LG))

        def tdone(eng, s, it, r):
            eng.wait_ge(s, it * BODY + (r + 1 + LT))

        def use_done(eng, s, it, u):
            eng.wait_ge(s, it * (2 * USES) + (u + 1 + USES))

        def gexists(it, q):
            return not isinstance(it, int) or 0 <= it * 2 + q < NG

        def texists(it, r):
            return not isinstance(it, int) or 0 <= it * BODY + r < NT

        def value_use(r):
            return USES * (r // GT) + (0, 1, 4, 7)[r % GT]

        def queries_ready(eng, it, q):
            use_done(eng, bank_free, it, USES * (q - 1) + 3)

        def keys_ready(eng, it, q):
            use_done(eng, bank_free, it, USES * (q - 1) + 6)

        def run(eng, step):
            for r in range(BODY):
                step(0, r)
            with eng.Fori(1, NG // 2 - 1) as it:
                for r in range(BODY):
                    step(it, r)
            for r in range(BODY + 2 * GT + 2):
                step(NG // 2 - 1, r)

        @block.sync
        def _(sp):
            def load(it, q):
                sp.dma_start(ct[:, q % 2, :, :], ins["ctx_t"][:, :, bass.ds((it * 2 + q) * GN, GN)]).then_inc(loaded[q % 2], 16)
            load(0, 0)
            load(0, 1)
            with sp.Fori(0, NG // 2 - 1) as it:
                for q in range(2):
                    use_done(sp, bank_made, it, value_use(q * GT + 1))
                    sp.sem_inc(passed, 1)
                    load(it, q + 2)
            tdone(sp, pv_made, NG // 2 - 1, BODY - 1)
            for into, source in later:
                sp.dma_start(into, source).then_inc(later_written, 16)

        def block_diagonal(engine, it, r, f, ready):
            t0 = (r % GT) * P
            for b in range(2):
                source = q_t[:, (r // GT) % 2, f, t0 + b * S:t0 + (b + 1) * S]
                last = engine.tensor_tensor(q_bd[:, r % 2, f, b, :, :], source.unsqueeze(1).to_broadcast([P, C_HALF, S]),
                                            w["head_mask"][:, :].unsqueeze(2).to_broadcast([P, C_HALF, S]), ALU.mult)
            last.then_inc(ready, 1)

        @block.tensor
        def _(pe):
            pe.wait_ge(opened, 1)

            def ct_loaded(it, q):
                pe.wait_ge(loaded[q % 2], it * 16 + 16 * (q // 2 + 1))

            def values(it, r, u):
                ct_loaded(it, r // GT)
                use_done(pe, bank_free, it, u - 1)
                for kt in range(KT):
                    last = nc.tensor.matmul(ps_q[:, 0:H], ct[:, (r // GT) % 2, kt, (r % GT) * P:(r % GT + 1) * P],
                                            w["v"][:, kt, :], start=(kt == 0), stop=(kt == KT - 1))
                last.then_inc(bank_made, 1)

            def project(it, q, f, u, weights, source):
                use_done(pe, bank_free, it, u - 1)
                for kt in range(KT):
                    last = nc.tensor.matmul(ps_q[:, :], weights[:, kt, f * P:(f + 1) * P], source[:, kt, :],
                                            start=(kt == 0), stop=(kt == KT - 1))
                last.then_inc(bank_made, 1)

            def queries(it, q, f, u):
                gdone(pe, xt_ready, it, q)
                project(it, q, f, u, w["q"], xt)

            def keys(it, q, f, u):
                ct_loaded(it, q)
                project(it, q, f, u, w["k"], ct[:, q % 2, :, :])

            def scores(it, r):
                keys_ready(pe, it, r // GT)
                tdone(pe, qbd0_ready, it, r)
                tdone(pe, qbd1_ready, it, r)
                tdone(pe, clip_ready, it, r - 1)
                for f in range(KT):
                    for b in range(2):
                        t0 = (r % GT) * P + b * S
                        last = nc.tensor.matmul(ps_s[b * S:(b + 1) * S, f, :], k_t[:, (r // GT) % 2, f, t0:t0 + S],
                                                q_bd[:, r % 2, f, b, :, :].rearrange("p h s -> p (h s)"),
                                                start=True, stop=True)
                last.then_inc(s_made, 1)

            def transposes(it, q, source, ready, free, made):
                gdone(pe, ready, it, q)
                for s, d in free:
                    gdone(pe, s, it, q + d)
                for j in range(GT):
                    for kt in range(KT):
                        last = nc.tensor.transpose(ps_x[:, kt, j * P:(j + 1) * P], source[:, j, kt * P:(kt + 1) * P], ident[:, :])
                last.then_inc(made, 1)

            def context_transposes(it, r):
                tdone(pe, heads_ready, it, r)
                tdone(pe, delta_ready, it, r - 1)
                for b in range(2):
                    last = nc.tensor.transpose(ps_c[:, b * P:(b + 1) * P], heads[:, b, :, :].rearrange("p h d -> p (h d)"),
                                               ident[:, :])
                last.then_inc(ct_made, 1)

            def outputs(it, r):
                tdone(pe, exp_ready, it, r)
                use_done(pe, bank_free, it, value_use(r - 2))
                tdone(pe, heads_ready, it, r - 1)
                for h in range(C_HALF):
                    for f in range(KT):
                        hh = f * C_HALF + h
                        last = nc.tensor.matmul(ps_pv[f * S:(f + 1) * S, h * 2 * VW:(h + 1) * 2 * VW],
                                                probs[:, r % 2, f, h * S:(h + 1) * S],
                                                v_bd[:, r % 4, hh, :, :].rearrange("p b d -> p (b d)"), start=True, stop=True)
                last.then_inc(pv_made, 1)

            def projection(it, r):
                tdone(pe, ct_copied, it, r)
                for f in range(KT):
                    last = nc.tensor.matmul(ps_c[:, 256:512], ctx_t[:, f, :, :].rearrange("p b s -> p (b s)"), w["o"][:, f, :],
                                            start=(f == 0), stop=(f == KT - 1))
                last.then_inc(y_made, 1)

            def step(it, r):
                g, j = r // GT, r % GT
                u = value_use(r)
                if texists(it, r + 2):
                    values(it, r + 2, u)
                if texists(it, r + 1):
                    scores(it, r + 1)
                if j == 0 and gexists(it, g + 1):
                    transposes(it, g + 1, xa, xa_ready, ((xt_ready, -1), (xft_ready, -3)), xa_t_made)
                if j == 3 and gexists(it, g - 1):
                    transposes(it, g - 1, xf[:, (g - 1) % 2, :, :], xf_ready,
                               ((xft_ready, -1),) + (((xt_ready, 2),) if gexists(it, g + 1) else ()), xf_t_made)
                if texists(it, r - 1):
                    context_transposes(it, r - 1)
                for f in range(KT):
                    if j == 1 and gexists(it, g + 1):
                        queries(it, g + 1, f, u + 1 + f)
                    if j == 2 and gexists(it, g + 1):
                        keys(it, g + 1, f, u + 1 + f)
                    if f == 0 and texists(it, r):
                        outputs(it, r)
                if texists(it, r - 1):
                    projection(it, r - 1)
                if j == 3 and gexists(it, g - 1):
                    gdone(pe, xft_ready, it, g - 1)
                    rt.make_logits(pe, it, g - 1, xft, gdone)
                if j == 0 and gexists(it, g - 2):
                    rt.make_ranks(pe, it, g - 2, gdone)

            transposes(0, 0, xa, xa_ready, (), xa_t_made)
            for f in range(KT):
                queries(0, 0, f, f - 6)
            values(0, 0, -4)
            for f in range(KT):
                keys(0, 0, f, f - 3)
            values(0, 1, -1)
            scores(0, 0)
            run(pe, step)

        @block.scalar
        def _(act):
            act.wait_ge(opened, 1)

            def copy_projected(it, q, f, u, out, bias, scale):
                use_done(act, bank_made, it, u)
                if not (isinstance(it, int) and it * 2 + q < 2):
                    tdone(act, s_made, it, (q - 1) * GT - 1)
                    tdone(act, qbd0_ready, it, (q - 1) * GT - 1)
                    tdone(act, qbd1_ready, it, (q - 1) * GT - 1)
                nc.scalar.activation(out[:, q % 2, f, :], ps_q[:, :], ACT.Identity, bias=bias[:, f:f + 1],
                                     scale=scale).then_inc(bank_free, 1)

            def copy_values(it, r, u):
                use_done(act, bank_made, it, u)
                tdone(act, pv_made, it, r - 4)
                for b in range(2):
                    half = slice(b * S, (b + 1) * S)
                    last = nc.scalar.activation(v_bd[half, r % 4, :, b, 0:C_DH],
                                                ps_q[half, 0:H].rearrange("p (h d) -> p h d", h=C_HEADS), ACT.Copy)
                last.then_inc(bank_free, 1)

            def exponentials(it, r):
                tdone(act, clip_ready, it, r)
                tdone(act, pv_made, it, r - 2)
                nc.scalar.activation(probs[:, r % 2, :, :], clipped[:, :, :], ACT.Exp, bias=masks_now[:, r % 4, 1:2],
                                     scale=masks_now[:, r % 4, 0:1]).then_inc(exp_ready, 1)

            def copy_transposed(it, q, out, made, ready, reader):
                gdone(act, made, it, q)
                reader(it, q)
                last = nc.scalar.activation(out[:, :, :], ps_x[:, :, :], ACT.Copy)
                last.then_inc(ready, 1)

            def xt_reader(it, q):
                if not (isinstance(it, int) and it * 2 + q < 1):
                    use_done(act, bank_made, it, USES * (q - 2) + 3)

            def xft_reader(it, q):
                gdone(act, rt.logits_made, it, q - 1)

            def copy_context(it, r):
                tdone(act, ct_made, it, r)
                tdone(act, y_made, it, r - 1)
                nc.scalar.activation(ctx_t[:, :, :, :], ps_c[:, 0:256].rearrange("p (b f s) -> p f b s", b=2, f=KT), ACT.Copy)\
                    .then_inc(ct_copied, 1)

            def step(it, r):
                g, j = r // GT, r % GT
                u = value_use(r)
                if texists(it, r + 2):
                    copy_values(it, r + 2, u)
                if texists(it, r - 1):
                    copy_context(it, r - 1)
                if j == 0 and gexists(it, g + 1):
                    copy_transposed(it, g + 1, xt, xa_t_made, xt_ready, xt_reader)
                if j == 3 and gexists(it, g - 1):
                    copy_transposed(it, g - 1, xft, xf_t_made, xft_ready, xft_reader)
                for f in range(KT):
                    if j == 1 and gexists(it, g + 1):
                        copy_projected(it, g + 1, f, u + 1 + f, q_t, w["bq"], C_DH ** -0.5)
                    if j == 2 and gexists(it, g + 1):
                        copy_projected(it, g + 1, f, u + 1 + f, k_t, w["bk"], 1.0)
                    if f == 0 and texists(it, r + 1):
                        exponentials(it, r + 1)

            copy_transposed(0, 0, xt, xa_t_made, xt_ready, xt_reader)
            for f in range(KT):
                copy_projected(0, 0, f, f - 6, q_t, w["bq"], C_DH ** -0.5)
            act.wait_ge(prepared, 2)
            copy_values(0, 0, -4)
            for f in range(KT):
                copy_projected(0, 0, f, f - 3, k_t, w["bk"], 1.0)
            copy_values(0, 1, -1)
            exponentials(0, 0)
            run(act, step)

        @block.vector
        def _(dve):
            dve.wait_ge(opened, 1)

            def statistics(it, q, stats, mv, vare, steps):
                norm_statistics(nc, dve, x_sb, it, q, stats, mv, vare, steps, passed)

            def apply_a(it, q):
                norm_apply(nc, dve, x_sb, it, q, mv_a, rstd_a, xa, rstd_a_ready, xa_ready, gdone,
                           lambda: gdone(dve, xa_t_made, it, q - 1))

            def apply_f(it, q):
                def free():
                    gdone(dve, xf_t_made, it, q - 2)
                    gdone(dve, rt.rows_sent, it, q - 2)
                norm_apply(nc, dve, x_sb, it, q, mv_f, rstd_f, xf[:, q % 2, :, :], rstd_f_ready, xf_ready, gdone, free)

            def spread_queries(it, r):
                queries_ready(dve, it, r // GT)
                tdone(dve, s_made, it, r - 2)
                block_diagonal(nc.vector, it, r, 0, qbd0_ready)

            def clip(it, r):
                tdone(dve, s_made, it, r)
                tdone(dve, exp_ready, it, r - 1)
                nc.vector.tensor_copy(masks_now[:, r % 4, :], sb["masks"][:, bass.ds(it * BODY + r, 1), :]
                                      .rearrange("p a c -> p (a c)"))
                nc.vector.tensor_scalar(clipped[:, :, :], ps_s[:, :, :], 50.0, -50.0, ALU.min, ALU.max).then_inc(clip_ready, 1)

            def normalise(it, r):
                tdone(dve, pv_made, it, r)
                ps = ps_pv[:, 0:C_HALF * 2 * VW].rearrange("p (h b v) -> p h b v", h=C_HALF, b=2)
                tdone(dve, heads_ready, it, r - 1)
                nc.vector.reciprocal(rsum[:, :, :], ps[:, :, :, C_DH]).then_inc(rsum_ready, 1)
                tdone(dve, rsum_ready, it, r)
                tdone(dve, ct_made, it, r - 1)
                nc.vector.tensor_tensor(heads[:, :, :, :].rearrange("p b h d -> p h b d"), ps[:, :, :, 0:C_DH],
                                        rsum[:, :, :].unsqueeze(3).to_broadcast([P, C_HALF, 2, C_DH]), ALU.mult)\
                    .then_inc(heads_ready, 1)

            def delta_statistics(it, r):
                base = it * (3 * BODY) + 3 * r
                tdone(dve, y_made, it, r)
                tdone(dve, scaled_ready, it, r - 2)
                nc.vector.tensor_tensor(delta[:, r % 2, :], ps_c[:, 256:512], w["bo"][:, :], ALU.add).then_inc(delta_ready, 1)
                tdone(dve, delta_ready, it, r)
                dve.sem_inc(passed, 1)
                nc.vector.bn_stats(stats_d[:, r % 2, :], delta[:, r % 2, :]).then_inc(steps_d, 1)
                dve.wait_ge(steps_d, base + 1)
                dve.sem_inc(passed, 1)
                nc.vector.bn_aggr(mv_d[:, r % 2, :], stats_d[:, r % 2, :]).then_inc(steps_d, 1)
                dve.wait_ge(steps_d, base + 2)
                nc.vector.tensor_scalar(vare_d[:, r % 2:r % 2 + 1], mv_d[:, r % 2, 1:2], w["rs"][:, 1:2], EPS,
                                        ALU.mult, ALU.add).then_inc(steps_d, 1)

            def residual(it, r):
                tile = x_sb[:, bass.ds(it * BODY + r, 1), :].rearrange("p a n -> p (a n)")
                tdone(dve, rstd_d_ready, it, r)
                tdone(dve, xb_ready, it, r)
                tdone(dve, x_ready, it, r - 1)
                nc.vector.scalar_tensor_tensor(out=scaled[:, :], in0=delta[:, r % 2, :], scalar=mv_d[:, r % 2, 0:1],
                                               in1=w["gamma"][:, :], op0=ALU.subtract, op1=ALU.mult).then_inc(scaled_ready, 1)
                tdone(dve, scaled_ready, it, r)
                nc.vector.scalar_tensor_tensor(out=tile, in0=scaled[:, :], scalar=rstd_d[:, r % 2:r % 2 + 1],
                                               in1=xb[:, r % 2, :], op0=ALU.mult, op1=ALU.add).then_inc(x_ready, 1)

            def step(it, r):
                g, j = r // GT, r % GT
                if j == 0 and gexists(it, g - 2):
                    rt.choose(dve, it, g - 2, gdone)
                if texists(it, r + 2):
                    spread_queries(it, r + 2)
                if j == 3 and gexists(it, g + 2):
                    apply_a(it, g + 2)
                if texists(it, r + 1):
                    clip(it, r + 1)
                if j == 2 and gexists(it, g + 2):
                    statistics(it, g + 2, stats_a, mv_a, vare_a, steps_a)
                if j == 1 and gexists(it, g - 2):
                    rt.place_rows(dve, it, g - 2, gdone)
                if texists(it, r - 2):
                    residual(it, r - 2)
                if texists(it, r):
                    normalise(it, r)
                if j == 1 and gexists(it, g - 1):
                    tdone(dve, x_ready, it, g * GT - 1)
                    statistics(it, g - 1, stats_f, mv_f, vare_f, steps_f)
                if j == 2 and gexists(it, g - 1):
                    apply_f(it, g - 1)
                if texists(it, r - 1):
                    delta_statistics(it, r - 1)

            nc.vector.memset(v_bd[:, :, :, :, :], 0.0).then_inc(prepared, 1)
            dve.wait_ge(prepared, 1)
            for b in range(2):
                last = nc.vector.memset(v_bd[b * S:(b + 1) * S, :, :, b, C_DH:VW], 1.0)
            last.then_inc(prepared, 1)
            for q in range(2):
                statistics(0, q, stats_a, mv_a, vare_a, steps_a)
                apply_a(0, q)
            spread_queries(0, 0)
            spread_queries(0, 1)
            clip(0, 0)
            run(dve, step)

        @block.gpsimd
        def _(pool):
            for s in by_group:
                pool.sem_inc(s, LG)
            for s in by_tile.values():
                pool.sem_inc(s, LT)
            for s in (bank_made, bank_free):
                pool.sem_inc(s, 2)
            rt.start(pool, LG)
            pool.sem_inc(opened, 1)

            def deviation(it, q, vare, rstd, steps, xn_ready, rstd_ready):
                norm_deviation(nc, pool, sb, it, q, vare, rstd, steps, xn_ready, rstd_ready, gdone)

            def spread_queries(it, r):
                queries_ready(pool, it, r // GT)
                tdone(pool, s_made, it, r - 2)
                block_diagonal(nc.gpsimd, it, r, 1, qbd1_ready)

            def add_beta(it, r):
                tdone(pool, scaled_ready, it, r - 2)
                tdone(pool, x_ready, it, r - 2)
                nc.gpsimd.tensor_tensor(xb[:, r % 2, :], x_sb[:, bass.ds(it * BODY + r, 1), :].rearrange("p a n -> p (a n)"),
                                        w["beta"][:, :], ALU.add).then_inc(xb_ready, 1)

            def delta_deviation(it, r):
                pool.wait_ge(steps_d, it * (3 * BODY) + 3 * (r + 1))
                tdone(pool, x_ready, it, r - 2)
                nc.gpsimd.tensor_tensor(rstd_d[:, r % 2:r % 2 + 1], vare_d[:, r % 2:r % 2 + 1], sb["minus_half"][:, :],
                                        ALU.pow).then_inc(rstd_d_ready, 1)

            def step(it, r):
                g, j = r // GT, r % GT
                if texists(it, r + 2):
                    spread_queries(it, r + 2)
                if texists(it, r - 2):
                    delta_deviation(it, r - 2)
                if texists(it, r - 1):
                    add_beta(it, r - 1)
                q = g - 2 if j >= 2 else g - 3
                if gexists(it, q):
                    rt.scatter(pool, it, q, xf[:, q % 2, :, :], ((j + 2) % GT,), gdone)
                if j == 2 and gexists(it, g - 3):
                    rt.mark_sent(pool, it, g - 3)
                if j == 1 and gexists(it, g - 1):
                    deviation(it, g - 1, vare_f, rstd_f, steps_f, xf_ready, rstd_f_ready)
                if j == 2 and gexists(it, g + 2):
                    deviation(it, g + 2, vare_a, rstd_a, steps_a, xa_ready, rstd_a_ready)

            for q in range(2):
                deviation(0, q, vare_a, rstd_a, steps_a, xa_ready, rstd_a_ready)
            spread_queries(0, 0)
            spread_queries(0, 1)
            for it in range(NG // 2 - 1):
                for r in range(BODY):
                    step(it, r)
            for r in range(BODY + 2 * GT + 2):
                step(NG // 2 - 1, r)


def setup_attention1(ph, block, nc, ins, sb, w):
    mask_i = ph.sbuf("mask_i", [P, NT], I32)
    rs = ph.sbuf("rs_in", [P, 1])
    bv = ph.sbuf("bv_in", [P, KT])
    bv_wide = ph.sbuf("bv_wide", [P, KT, P])
    ps_b = ph.psum("ps_bias", [P, 512])
    bias_made = ph.sem("bias_made")
    loaded, steps, masked = ph.sem("weights_loaded"), ph.sem("scale_steps"), ph.sem("mask_steps")
    names = ("q", "k", "v", "o", "gate")

    @block.sync
    def _(sp):
        for n in names:
            sp.dma_start(w[n][:, :, :], ins["w_" + n]).then_inc(loaded, 16)
        for n in ("bq", "bk"):
            sp.dma_start(w[n][:, :], ins[n]).then_inc(loaded, 16)
        sp.dma_start(bv[:, :], ins["bv"]).then_inc(loaded, 16)
        for n in ("bo", "beta", "gamma", "gate_b"):
            sp.dma_start(w[n][:, :], ins[n].broadcast_to([P, w[n].shape[1]])).then_inc(loaded, 16)
        sp.dma_start(rs[:, :], ins["rs"].broadcast_to([P, 1])).then_inc(loaded, 16)
        sp.dma_start(mask_i[:, :], ins["mask"]).then_inc(loaded, 16)

    @block.vector
    def _(dve):
        dve.wait_ge(loaded, 16 * 14)
        nc.vector.tensor_copy(bv_wide[:, :, :], bv[:, :].unsqueeze(2).to_broadcast([P, KT, P])).then_inc(steps, 1)
        nc.vector.tensor_scalar(w["bq"][:, :], w["bq"][:, :], C_DH ** -0.5, None, ALU.mult).then_inc(steps, 1)
        nc.vector.tensor_scalar(w["rs"][:, 0:1], rs[:, :], 0.0, 0.3, ALU.max, ALU.min).then_inc(steps, 1)
        nc.vector.tensor_copy(sb["masks"][:, :, 0], mask_i[:, :]).then_inc(masked, 1)
        dve.wait_ge(masked, 1)
        nc.vector.tensor_scalar(sb["masks"][:, :, 0], sb["masks"][:, :, 0], 0.5, None, ALU.is_gt).then_inc(masked, 1)
        dve.wait_ge(steps, 3)
        nc.vector.tensor_tensor(w["rs"][:, 1:2], w["rs"][:, 0:1], w["rs"][:, 0:1], ALU.mult).then_inc(steps, 1)
        nc.vector.tensor_scalar(w["gamma"][:, :], w["gamma"][:, :], w["rs"][:, 0:1], None, ALU.mult).then_inc(steps, 1)
        dve.wait_ge(masked, 2)
        nc.vector.tensor_scalar(sb["masks"][:, :, 1], sb["masks"][:, :, 0], 50.0, -50.0, ALU.mult, ALU.add)\
            .then_inc(masked, 1)
        dve.wait_ge(steps, 5)
        dve.wait_ge(masked, 3)
        dve.wait_ge(bias_made, 1)
        nc.vector.tensor_tensor(w["bo"][:, :], ps_b[:, 0:H], w["bo"][:, :], ALU.add).then_inc(steps, 1)
        dve.wait_ge(steps, 6)

    @block.tensor
    def _(pe):
        pe.wait_ge(loaded, 16 * 14)
        pe.wait_ge(steps, 1)
        for kt in range(KT):
            last = nc.tensor.matmul(ps_b[:, 0:H], bv_wide[:, kt, :], w["o"][:, kt, :], start=(kt == 0), stop=(kt == KT - 1))
        last.then_inc(bias_made, 1)

    @block.gpsimd
    def _(pool):
        head_mask = w["head_mask"]
        made = ph.sem("head_mask_made")
        nc.gpsimd.memset(head_mask[:, :], 1.0).then_inc(made, 1)
        pool.wait_ge(made, 1)
        nc.gpsimd.affine_select(out=head_mask[:, :], in_=head_mask[:, :], compare_op=ALU.is_ge, fill=0.0,
                                base=0, pattern=[[-C_DH, C_HALF]], channel_multiplier=1).then_inc(made, 1)
        pool.wait_ge(made, 2)
        nc.gpsimd.affine_select(out=head_mask[:, :], in_=head_mask[:, :], compare_op=ALU.is_gt, fill=0.0,
                                base=C_DH, pattern=[[C_DH, C_HALF]], channel_multiplier=-1).then_inc(made, 1)
        pool.wait_ge(made, 3)


def combine1(nc, sb, m, out):
    K, E = m.K, m.E
    with ExitStack() as ctx:
        ph = Phase(ctx, nc, "combine1")
        slots = ph.sbuf("slots_now", [P, 2, GT * K], I32)
        weights = ph.sbuf("weights_now", [P, 2, GT * K])
        got = ph.sbuf("rows_got", [P, GT, K, H])
        acc = ph.sbuf("acc", [P, GT, 2, H])
        weighted = ph.sbuf("weighted", [P, GT * K, E])
        by_expert = ph.sbuf("by_expert", [P, GT, E])
        by_expert_t = ph.sbuf("by_expert_t", [P, 2, GT, P])
        ps_t = ph.psum("ps_t", [P, GT, P])
        ps_b = ph.psum("ps_b", [P, GT, 512])
        find = SlotFinder(ph, nc, m)
        opened, passed = ph.sem("opened"), ph.sem("passed")
        staged, steps, used = ph.sem("slots_staged"), ph.sem("sum_steps"), ph.sem("rows_used")
        weight_steps = ph.sem("weight_steps")
        we_t_made, we_t_ready, bias_made = ph.sem("we_t_made"), ph.sem("we_t_ready"), ph.sem("bias_made")
        gathered = [ph.sem(f"gathered{j}") for j in range(GT)]
        stored = ph.sem("tiles_stored")
        block = ctx.enter_context(nc.Block())

        @block.gpsimd
        def _(pool):
            with pool.Fori(0, NG // 2) as it:
                for q in range(2):
                    pool.wait_ge(staged, it * 2 + (q + 1))
                    for j in range(GT):
                        pool.wait_ge(used, it * (2 * GT) + (q * GT + j + 1))
                        pool.sem_inc(passed, 1)
                        for k in range(K):
                            n = j * K + k
                            pool.indirect_dma_start(got[:, j, k, :], None, m.rows_out,
                                                    bass.IndirectOffsetOnAxis(ap=slots[:, q, n:n + 1], axis=0))\
                                .then_inc(gathered[j], 16)

        @block.tensor
        def _(pe):
            pe.wait_ge(opened, 1)
            with pe.Fori(0, NG // 2) as it:
                for q in range(2):
                    pe.wait_ge(weight_steps, it * 4 + (2 * q + 2))
                    pe.wait_ge(we_t_ready, it * 2 + (q + 1))
                    for j in range(GT):
                        last = nc.tensor.transpose(ps_t[0:E, j, :], by_expert[:, j, :], sb["ident"][:, :])
                    last.then_inc(we_t_made, 1)
                    pe.wait_ge(we_t_ready, it * 2 + (q + 2))
                    pe.wait_ge(used, it * (2 * GT) + (q * GT + GT))
                    for j in range(GT):
                        last = nc.tensor.matmul(ps_b[:, j, 0:H], by_expert_t[:, q, j, :], sb["b_down"][:, :],
                                                start=True, stop=True)
                    last.then_inc(bias_made, 1)

        @block.scalar
        def _(act):
            act.wait_ge(opened, 1)
            with act.Fori(0, NG // 2) as it:
                for q in range(2):
                    act.wait_ge(we_t_made, it * 2 + (q + 1))
                    nc.scalar.activation(by_expert_t[0:E, q, :, :], ps_t[0:E, :, :], ACT.Copy).then_inc(we_t_ready, 1)

        @block.vector
        def _(dve):
            dve.sem_inc(used, GT)
            nc.vector.memset(by_expert_t[:, :, :, :], 0.0).then_inc(we_t_ready, 1)
            dve.wait_ge(we_t_ready, 1)
            dve.sem_inc(opened, 1)

            def stage(it, q):
                if not (isinstance(it, int) and it * 2 + q == 0):
                    dve.wait_ge(used, it * (2 * GT) + q * GT)
                nc.vector.tensor_copy(weights[:, q % 2, :].rearrange("p (j k) -> p j k", j=GT),
                                      m.weights[:, bass.ds((it * 2 + q) * GT, GT), :])
                find.rows(dve, it, q, slots, staged)
                nc.vector.tensor_tensor(weighted[:, :, :].rearrange("p (j k) e -> p j k e", j=GT),
                                        find.onehot[:, :, :].rearrange("p (j k) e -> p j k e", j=GT),
                                        m.weights[:, bass.ds((it * 2 + q) * GT, GT), :].unsqueeze(3)
                                        .to_broadcast([P, GT, K, E]), ALU.mult).then_inc(weight_steps, 1)
                dve.wait_ge(weight_steps, it * 4 + (2 * q + 1))
                if not (isinstance(it, int) and it * 2 + q == 0):
                    dve.wait_ge(we_t_made, it * 2 + q)
                nc.vector.tensor_reduce(by_expert[:, :, :], weighted[:, :, :].rearrange("p (j k) e -> p j e k", j=GT),
                                        AX.X, ALU.add).then_inc(weight_steps, 1)

            def tile(it, q, j):
                x = sb["x"][:, bass.ds((it * 2 + q) * GT + j, 1), :].rearrange("p a n -> p (a n)")
                if j == 0:
                    dve.wait_ge(staged, it * 2 + (q + 1))
                    dve.wait_ge(bias_made, it * 2 + (q + 1))
                dve.wait_ge(gathered[j], it * (32 * K) + 16 * K * (q + 1))
                dve.wait_ge(used, it * (2 * GT) + (q * GT + j + 1))
                base = it * (2 * GT * K) + (q * GT + j) * K
                nc.vector.tensor_tensor(acc[:, j, 1, :], x, ps_b[:, j, 0:H], ALU.add).then_inc(steps, 1)
                for k in range(K):
                    into = x if k == K - 1 else acc[:, j, k % 2, :]
                    dve.wait_ge(steps, base + (k + 1))
                    nc.vector.scalar_tensor_tensor(out=into, in0=got[:, j, k, :],
                                                   scalar=weights[:, q % 2, j * K + k:j * K + k + 1],
                                                   in1=acc[:, j, (k + 1) % 2, :], op0=ALU.mult, op1=ALU.add)\
                        .then_inc(used if k == K - 1 else steps, 1)
            stage(0, 0)
            with dve.Fori(0, NG // 2 - 1) as it:
                for q in range(2):
                    for j in range(GT):
                        tile(it, q, j)
                        if j == 0:
                            stage(it, q + 1)
            for q in range(2):
                for j in range(GT):
                    tile(NG // 2 - 1, q, j)
                    if j == 0 and q == 0:
                        stage(NG // 2 - 1, 1)
            dve.wait_ge(used, NT + GT)

        @block.sync
        def _(sp):
            with sp.Fori(0, NT) as t:
                sp.wait_ge(used, t + (GT + 1))
                sp.sem_inc(passed, 1)
                sp.dma_start(out[bass.ds(t * P, P), :], sb["x"][:, bass.ds(t, 1), :].rearrange("p a n -> p (a n)"))\
                  .then_inc(stored, 16)
            sp.wait_ge(stored, 16 * NT)


def build_program(nc, ins, out):
    with ExitStack() as ctx:
        def sbt(name, shape, dt=F32):
            return ctx.enter_context(nc.sbuf_tensor(name, shape, dt))
        m0 = Moe(nc, "l0", experts=16, top=2, inner=64)
        m1 = Moe(nc, "l1", experts=32, top=4, inner=128)
        sb = dict(x=sbt("x_sb", [P, NT, H]), ident=sbt("ident", [P, P]), minus_half=sbt("minus_half", [P, 1]),
                  onesf=sbt("onesf", [P, 1]), ones=sbt("ones", [P, P], BF16), before=sbt("before", [P, P], BF16),
                  upto=sbt("upto", [P, P]), zeros=sbt("zeros", [P, H]), block_iota=sbt("block_iota", [P, 256]),
                  masks=sbt("masks", [P, NT, 2]), term_ones=sbt("term_ones", [P, P], BF16),
                  bias1=sbt("bias1", [P, m1.E, 2 * m1.I], BF16), b_down=sbt("b_down_sb", [P, H]),
                  b_out=sbt("b_out", [P, 1]))
        m1.tables(ctx, nc)
        w1 = dict(gate=sbt("w1_gate", [P, KT, m1.E]), gate_b=sbt("w1_gate_b", [P, m1.E]),
                  q=sbt("w1_q", [P, KT, H]), k=sbt("w1_k", [P, KT, H]), v=sbt("w1_v", [P, KT, H]), o=sbt("w1_o", [P, KT, H]),
                  bq=sbt("w1_bq", [P, KT]), bk=sbt("w1_bk", [P, KT]), bo=sbt("w1_bo", [P, H]),
                  beta=sbt("w1_beta", [P, H]), gamma=sbt("w1_gamma", [P, H]), rs=sbt("w1_rs", [P, 2]),
                  head_mask=sbt("head_mask", [P, C_HALF]))
        w_down1 = sbt("w_down1", [P, m1.E, H])
        later_loaded = ctx.enter_context(nc.semaphore("later_loaded"))

        with ExitStack() as layer0:
            def sb0(name, shape, dt=F32):
                return layer0.enter_context(nc.sbuf_tensor(name, shape, dt))
            m0.tables(layer0, nc)
            w0 = dict(gate=sb0("w0_gate", [P, KT, m0.E + 1]), shared_in=sb0("w0_shared_in", [P, 2, KT, H]),
                      shared_out=sb0("w0_shared_out", [P, 2, H]))
            w_gu0 = sb0("w_gu0", [P, m0.E, KT, 2 * m0.I])
            w_down0 = sb0("w_down0", [P, m0.E, H])
            sb["w_down0"] = w_down0
            later = [(w0["gate"][:, :, :], ins["w0_gate"]), (w0["shared_in"][:, :, :, :], ins["shared_in"]),
                     (w0["shared_out"][:, :, :], ins["shared_out"]), (w_gu0[:, :, :, :], ins["w_gu0"]),
                     (w_down0[0:m0.I, :, :], ins["w_down0"]), (w_down1[:, :, :], ins["w_down1"])]
            with ExitStack() as attention:
                def sba(name, shape):
                    return attention.enter_context(nc.sbuf_tensor(name, shape, F32))
                sb.update(a_bd=sba("a_bd", [P, 2, A_HEADS // 2, P]), bv=sba("bv", [P, A_HEADS // 2, S]),
                          ctx_bd=sba("ctx_bd", [P, 2, 2, 2 * A_N]))
                with ExitStack() as setup:
                    phases = [Phase(setup, nc, name) for name in ("fold", "setup1", "constants")]
                    block = setup.enter_context(nc.Block())
                    zeroed = zero_operands(phases[0], block, nc, sb, m0)
                    setup_attention_weights(phases[0], block, nc, ins, sb)
                    setup_attention1(phases[1], block, nc, ins, sb, w1)
                    setup_constants(phases[2], block, nc, ins, sb, (m0, m1), zeroed)
                later += [(m.rows_in[m.E * m.CAP:m.E * m.CAP + m.spare * P, :].rearrange("(c p) h -> p c h", p=P),
                           sb["zeros"][:, :].unsqueeze(1).to_broadcast([P, m.spare, H])) for m in (m0, m1)]
                attention0(nc, ins, sb, later, later_loaded)
            wait_for(nc, later_loaded, 16 * len(later))
            shared_expert(nc, sb, m0, w0)
            block_tables(nc, sb, m0)
            experts(nc, sb, m0, w_gu0, w_down0, None, None, Swish)
            combine0(nc, sb, m0)
        with nc.sbuf_tensor("w_gu1", [P, m1.E, KT, 2 * m1.I], F32) as w_gu1:
            half = m1.E // 2
            attention1(nc, ins, sb, m1, w1, w_gu1,
                       [(w_gu1[:, c:c + half, :, :], ins["w_gu1"][:, c:c + half, :, :]) for c in (0, half)], later_loaded)
            block_tables(nc, sb, m1)
            wait_for(nc, later_loaded, 16 * (len(later) + 2))
            experts(nc, sb, m1, w_gu1, w_down1, sb["bias1"], sb["term_ones"], ClippedSwish)
        combine1(nc, sb, m1, out)


def wait_for(nc, semaphore, count):
    with nc.Block() as block:
        @block.sync
        def _(sp):
            sp.wait_ge(semaphore, count)


def _heads(w):
    return w.reshape(64, 8, 64).transpose(2, 1, 0)


def _rows(w):
    return w.T.reshape(KT, P, -1).transpose(1, 0, 2)


def _layouts(a):
    import numpy as np
    w_k, w_v = np.split(a["L0_xattn_W_kv"], 2, axis=1)
    e0, e1 = a["L0_ffn_w1"].shape[0], a["L1_ffn_w_gate"].shape[0]
    gu0 = np.concatenate([a["L0_ffn_w1"], a["L0_ffn_w3"]], axis=1).transpose(0, 2, 1)
    gu1 = np.concatenate([a["L1_ffn_w_gate"], a["L1_ffn_w_up"]], axis=2)
    return {
        "x": a["x"].reshape(T, H), "ctx": a["ctx_2048"],
        "ctx_keys": a["ctx_2048"].reshape(NT, 2, S, KT, P).transpose(0, 4, 1, 3, 2),
        "wq": _heads(a["L0_xattn_W_q"]), "wk": _heads(w_k), "wv": _heads(w_v),
        "wo": a["L0_xattn_W_out"].reshape(8, 64, 64).transpose(1, 0, 2), "b_out": a["L0_xattn_b_out"].reshape(64, 1),
        "w0_gate": _rows(np.concatenate([a["L0_ffn_gate_w"], a["L0_ffn_shared_gate_w"]])),
        "shared_in": np.stack([_rows(a["L0_ffn_ws_gate"]), _rows(a["L0_ffn_ws_up"])], axis=1),
        "shared_out": _rows(a["L0_ffn_ws_down"]),
        "w_gu0": gu0.reshape(e0, KT, P, -1).transpose(2, 0, 1, 3),
        "w_down0": a["L0_ffn_w2"].transpose(2, 0, 1),
        "ctx_t": a["ctx_2048"].reshape(T, H).T.reshape(KT, P, T).transpose(1, 0, 2),
        "mask": a["mask_BxS2_ik0"].reshape(NT, P).T,
        "w_q": _rows(a["L1_xattn_Wq"]), "w_k": _rows(a["L1_xattn_Wk"]), "w_v": _rows(a["L1_xattn_Wv"]),
        "w_o": _rows(a["L1_xattn_Wo"]), "w_gate": _rows(a["L1_ffn_gate_w"]),
        "bq": a["L1_xattn_bq"].reshape(KT, P).T, "bk": a["L1_xattn_bk"].reshape(KT, P).T,
        "bv": a["L1_xattn_bv"].reshape(KT, P).T, "bo": a["L1_xattn_bo"].reshape(1, H),
        "beta": a["L1_xattn_ln_beta"].reshape(1, H), "gamma": a["L1_xattn_ln_gamma"].reshape(1, H),
        "gate_b": a["L1_ffn_gate_b"].reshape(1, -1), "rs": a["L1_xattn_residual_scale"].reshape(1, 1),
        "w_gu1": gu1.reshape(e1, KT, P, -1).transpose(2, 0, 1, 3),
        "w_down1": a["L1_ffn_w_down"].transpose(1, 0, 2),
        "bias_gu1": np.concatenate([a["L1_ffn_b_gate"], a["L1_ffn_b_up"]], axis=1), "b_down1": a["L1_ffn_b_down"],
    }


def kernel(**inputs):
    import numpy as np
    import concourse.bacc as bacc
    from concourse.bass_utils import run_bass_kernel_spmd

    nc = bacc.Bacc("TRN2", target_bir_lowering=False, num_devices=1)
    arrays, ins = {}, {}
    for name, a in _layouts({n: np.asarray(a) for n, a in inputs.items()}).items():
        arrays["in_" + name] = np.ascontiguousarray(a)
        ins[name] = nc.dram_tensor("in_" + name, a.shape, mybir.dt.from_np(a.dtype), kind="ExternalInput").ap()
    out = nc.dram_tensor("out", (T, H), F32, kind="ExternalOutput").ap()
    build_program(nc, ins, out)
    result = run_bass_kernel_spmd(nc, [arrays], core_ids=[0])
    return result.results[0]["out"].reshape(B, S, H)
```
